# Optimizing a Trainium2 kernel written in Bass

```python
import numpy as np
import jax
import jax.numpy as jnp

def _softmax(x, axis=-1):
    return jax.nn.softmax(x, axis=axis)

def _gelu(x):
    return jax.nn.gelu(x, approximate=True)

def _silu(x):
    return jax.nn.silu(x)

def _sigmoid(x):
    return jax.nn.sigmoid(x)

def _layernorm(x, axis=-1, eps=1e-05):
    m = jnp.mean(x, axis=axis, keepdims=True)
    v = jnp.var(x, axis=axis, keepdims=True)
    return (x - m) / jnp.sqrt(v + eps)

def _scatter_add(tgt, idx, src, axis=0):
    return tgt.at[idx].add(src)

def _segment_sum(src, seg, n):
    return jax.ops.segment_sum(src, seg, n)
kernel_name = 'mk_gps_d1_gnn_r8_4f2f99'

def setup_inputs(seed: int=0):
    np.random.seed(seed)
    _w = jnp.asarray

    def _rec_inputs():
        import jax
        import jax.numpy as jnp
        _gk = jax.random.key(seed)
        x = -0.0002117 + 1 * jax.random.normal(jax.random.fold_in(_gk, 1), (12500, 256), jnp.float32)
        src = jax.random.randint(jax.random.fold_in(_gk, 2), (200000,), 0, 12500, jnp.int32)
        dst = jax.random.randint(jax.random.fold_in(_gk, 3), (200000,), 0, 12500, jnp.int32)
        _o = jnp.argsort(dst, stable=True)
        src = src[_o]
        dst = dst[_o]
        edge_weight = jax.random.uniform(jax.random.fold_in(_gk, 12), (200000,), jnp.float32, 0.0, 1)
        return (x, src, dst, edge_weight)
    x, src, dst, edge_weight = _rec_inputs()

    def _L0_gnn_setup():
        import jax, jax.numpy as jnp
        import numpy as np
        N_NODES = 12500
        N_EDGES = 400000
        IN_F = 256
        OUT_F = 256
        key = jax.random.key(seed)
        k1, k2, k3, k4, k5, k6 = jax.random.split(key, 6)
        H = jax.random.normal(k1, (N_NODES, IN_F), dtype=jnp.float32)
        row = jax.random.randint(k2, (N_EDGES,), 0, N_NODES)
        col = jax.random.randint(k3, (N_EDGES,), 0, N_NODES)
        edge_index = jnp.stack([row, col], axis=0)
        edge_vals = jax.random.uniform(k4, (N_EDGES,), dtype=jnp.float32)
        stdv = 1.0 / np.sqrt(OUT_F)
        W = jax.random.uniform(k5, (IN_F, OUT_F), dtype=jnp.float32, minval=-stdv, maxval=stdv)
        b = jax.random.uniform(k6, (OUT_F,), dtype=jnp.float32, minval=-stdv, maxval=stdv)
        return {'H': H, 'edge_index': edge_index, 'edge_vals': edge_vals, 'W': W, 'b': b}
    _L0_gnn_all = _L0_gnn_setup()
    _L0_gnn_in = {k: v for k, v in _L0_gnn_all.items() if k in ('W', 'b')}
    del _L0_gnn_all

    def _L0_mix_setup():
        import jax, jax.numpy as jnp
        import numpy as np
        NUM_HEADS = 8
        key = jax.random.key(seed)
        ks = jax.random.split(key, 5)
        B, N, C = (8, 2048, 256)
        x = jax.random.normal(ks[0], (B, N, C), dtype=jnp.float32)
        Wq = jax.random.normal(ks[1], (C, C), dtype=jnp.float32) * 0.02
        Wkv = jax.random.normal(ks[2], (2 * C, C), dtype=jnp.float32) * 0.02
        Wproj = jax.random.normal(ks[3], (C, C), dtype=jnp.float32) * 0.02
        bproj = jnp.zeros((C,), dtype=jnp.float32)
        return {'x': x, 'Wq': Wq, 'Wkv': Wkv, 'Wproj': Wproj, 'bproj': bproj}
    _L0_mix_all = _L0_mix_setup()
    _L0_mix_in = {k: v for k, v in _L0_mix_all.items() if k in ('Wq', 'Wkv', 'Wproj', 'bproj')}
    del _L0_mix_all

    def _L0_ffn_setup():
        import jax, jax.numpy as jnp
        import numpy as np
        D_MODEL = 256
        EXPERT_DIM = 512
        NUM_EXPERTS = 8
        TOP_K = 2
        SEQ_LEN = 256
        BATCH = 2
        key = jax.random.key(seed)
        ks = jax.random.split(key, 8)
        s = 0.02
        x = jax.random.normal(ks[0], (SEQ_LEN, BATCH, D_MODEL), dtype=jnp.float32)
        Wg = jax.random.normal(ks[1], (D_MODEL, NUM_EXPERTS), dtype=jnp.float32) * s
        bg = jax.random.normal(ks[2], (NUM_EXPERTS,), dtype=jnp.float32) * s
        bias = jnp.zeros((NUM_EXPERTS,), dtype=jnp.float32)
        W1 = jax.random.normal(ks[3], (NUM_EXPERTS, D_MODEL, EXPERT_DIM), dtype=jnp.float32) * s
        b1 = jax.random.normal(ks[4], (NUM_EXPERTS, EXPERT_DIM), dtype=jnp.float32) * s
        W2 = jax.random.normal(ks[5], (NUM_EXPERTS, EXPERT_DIM, D_MODEL), dtype=jnp.float32) * s
        b2 = jax.random.normal(ks[6], (NUM_EXPERTS, D_MODEL), dtype=jnp.float32) * s
        return {'x': x, 'Wg': Wg, 'bg': bg, 'bias': bias, 'W1': W1, 'b1': b1, 'W2': W2, 'b2': b2}
    _L0_ffn_all = _L0_ffn_setup()
    _L0_ffn_in = {k: v for k, v in _L0_ffn_all.items() if k in ('Wg', 'bg', 'bias', 'W1', 'b1', 'W2', 'b2')}
    del _L0_ffn_all
    return {'x': x, 'src': src, 'dst': dst, 'edge_weight': edge_weight, 'L0_gnn_W': _L0_gnn_in['W'], 'L0_gnn_b': _L0_gnn_in['b'], 'L0_mix_Wq': _L0_mix_in['Wq'], 'L0_mix_Wkv': _L0_mix_in['Wkv'], 'L0_mix_Wproj': _L0_mix_in['Wproj'], 'L0_mix_bproj': _L0_mix_in['bproj'], 'L0_ffn_Wg': _L0_ffn_in['Wg'], 'L0_ffn_bg': _L0_ffn_in['bg'], 'L0_ffn_bias': _L0_ffn_in['bias'], 'L0_ffn_W1': _L0_ffn_in['W1'], 'L0_ffn_b1': _L0_ffn_in['b1'], 'L0_ffn_W2': _L0_ffn_in['W2'], 'L0_ffn_b2': _L0_ffn_in['b2']}

def reference(x, src, dst, edge_weight, L0_gnn_W, L0_gnn_b, L0_mix_Wq, L0_mix_Wkv, L0_mix_Wproj, L0_mix_bproj, L0_ffn_Wg, L0_ffn_bg, L0_ffn_bias, L0_ffn_W1, L0_ffn_b1, L0_ffn_W2, L0_ffn_b2):
    import jax
    import jax.numpy as jnp

    def _L0_gnn_ref(H, edge_index, edge_vals, W, b):
        import jax, jax.numpy as jnp
        import numpy as np
        N_NODES = 12500
        N_EDGES = 400000
        IN_F = 256
        OUT_F = 256
        HW = H @ W
        row, col = (edge_index[0], edge_index[1])
        msgs = edge_vals[:, None] * HW[col]
        AHW = jax.ops.segment_sum(msgs, row, num_segments=N_NODES)
        return AHW + b

    def _L0_mix_ref(x, Wq, Wkv, Wproj, bproj):
        import jax, jax.numpy as jnp
        import numpy as np
        NUM_HEADS = 8
        B, N, C = x.shape
        h = NUM_HEADS
        d = C // h
        q = jnp.einsum('bnc,oc->bno', x, Wq).reshape(B, N, h, d).transpose(0, 2, 1, 3)
        kv = jnp.einsum('bnc,oc->bno', x, Wkv).reshape(B, N, 2, h, d)
        k = kv[:, :, 0].transpose(0, 2, 1, 3)
        v = kv[:, :, 1].transpose(0, 2, 1, 3)
        q = jax.nn.elu(q) + 1.0
        k = jax.nn.elu(k) + 1.0
        k_sum = k.sum(axis=2)
        D_inv = 1.0 / jnp.maximum(jnp.einsum('bhnd,bhd->bhn', q, k_sum), 1e-06)
        context = jnp.einsum('bhnd,bhne->bhde', k, v)
        attn = jnp.einsum('bhnd,bhde->bhne', q, context) * D_inv[..., None]
        out = attn.transpose(0, 2, 1, 3).reshape(B, N, C)
        out = jnp.einsum('bnc,oc->bno', out, Wproj) + bproj
        return out

    def _L0_ffn_ref(x, Wg, bg, bias, W1, b1, W2, b2):
        import jax, jax.numpy as jnp
        import numpy as np
        D_MODEL = 256
        EXPERT_DIM = 512
        NUM_EXPERTS = 8
        TOP_K = 2
        SEQ_LEN = 256
        BATCH = 2
        x_flat = x.reshape(-1, D_MODEL)
        gate_logits = x_flat @ Wg + bg + bias
        topk_vals, topk_idx = jax.lax.top_k(gate_logits, TOP_K)
        topk_w = jax.nn.softmax(topk_vals, axis=-1)
        combine = (jax.nn.one_hot(topk_idx, NUM_EXPERTS, dtype=x.dtype) * topk_w[..., None]).sum(axis=1)
        h = jax.nn.relu(jnp.einsum('td,edh->teh', x_flat, W1) + b1)
        y = jnp.einsum('teh,ehd->ted', h, W2) + b2
        out = jnp.einsum('ted,te->td', y, combine)
        return out.reshape(x.shape)
    edge_index = jnp.stack([src, dst])
    xn = _layernorm(x, axis=-1)
    x = x + _L0_gnn_ref(xn, edge_index, edge_weight, L0_gnn_W, L0_gnn_b) + _L0_mix_ref(xn[None], L0_mix_Wq, L0_mix_Wkv, L0_mix_Wproj, L0_mix_bproj)[0]
    x = x + _L0_ffn_ref(_layernorm(x, axis=-1)[None], L0_ffn_Wg, L0_ffn_bg, L0_ffn_bias, L0_ffn_W1, L0_ffn_b1, L0_ffn_W2, L0_ffn_b2)[0]
    return x

_drawn_inputs = setup_inputs


def setup_inputs(seed=0):
    import zlib

    import numpy as np

    out = dict(_drawn_inputs(seed))
    spreads = {'L0_mix_bproj': (0.0, 0.1), 'L0_ffn_bias': (0.0, 0.288)}
    factors = {'L0_mix_Wq': 8.0,
     'L0_mix_Wkv': 8.0,
     'L0_mix_Wproj': 8.0,
     'L0_ffn_bg': 7.191,
     'L0_ffn_b1': 22.746,
     'L0_ffn_b2': 6.529}
    for name, (base, spread) in spreads.items():
        noise = np.random.default_rng([zlib.crc32(name.encode()), seed]).standard_normal(out[name].shape)
        drawn = base * np.exp(spread * noise) if base else spread * noise
        out[name] = jnp.asarray(drawn.astype(out[name].dtype))
    for name, factor in factors.items():
        out[name] = (out[name] * factor).astype(out[name].dtype)
    return out
```

```python
from contextlib import ExitStack

from concourse.bass import DynSlice


class Steps:

    def __init__(self, eng, sem):
        self.eng, self.sem, self.base, self.count = eng, sem, 0, 0

    def done(self, instruction):
        instruction.then_inc(self.sem, 1)
        self.count += 1

    def settle(self):
        self.eng.wait_ge(self.sem, self.base + self.count)

    def enter(self, turn, per_turn):
        self.before, self.per_turn = self.count, per_turn
        self.base, self.count = turn * per_turn + self.before, 0

    def leave(self, turns):
        assert self.count == self.per_turn, (self.count, self.per_turn)
        self.base, self.count = 0, self.before + turns * self.per_turn


def load_offsets(eng, name, row, first, count, top):
    registers = [eng.alloc_register(f"{name}{i}") for i in range(count)]
    eng.load(registers, row[0:1, first:first + count] if isinstance(first, int) else row[0:1, DynSlice(first, count)])
    return [eng.snap(r, min_val=0, max_val=top) for r in registers]


def gps_layer(nc, x, src, dst, edge_weight, gnn_W, gnn_b, mix_Wq, mix_Wkv, mix_Wproj, mix_bproj,
              ffn_Wg, ffn_bg, ffn_bias, ffn_W1, ffn_b1, ffn_W2, ffn_b2, out):
    import concourse.bass as bass
    from concourse import mybir

    F32, BF16, I32 = mybir.dt.float32, mybir.dt.bfloat16, mybir.dt.int32
    ALU, ACT, AX = mybir.AluOpType, mybir.ActivationFunctionType, mybir.AxisListType.X
    ds = bass.ds
    Offset = bass.IndirectOffsetOnAxis

    P = 128
    N, C = x.shape
    E = src.shape[0]
    KC = C // P
    NB = -(-N // P)
    LAST = N - (NB - 1) * P
    PAIRS = NB // 2
    HEADS, HD = 8, 32
    EXPERTS, _, HID = ffn_W1.shape
    KH = HID // P
    EPS = 1e-5
    CH = 8
    HB = NB // 2
    ET = -(-E // (P * 2 * CH)) * 2 * CH
    CHUNKS = ET // CH
    SET, RING = 4, 4
    TT = -(-((ET * P + NB * (P - 1)) // P) // (SET * RING)) * SET * RING
    TSETS = TT // SET
    TPP = -(-TT // P)
    TX = -(-((2 * NB * P + EXPERTS * (P - 1)) // P) // 4) * 4
    XPP = max(2, -(-TX // P))
    assert KC * HID == KH * C and NB % 4 == 2 and HB * CH <= 512 and KC == 2 and 4 * C == 1024 and HID == 512

    h_table = nc.dram_tensor("h_table", (NB * P, C), F32, kind="Internal").ap()
    q_dram = nc.dram_tensor("q_dram", (PAIRS, P, 2 * C), F32, kind="Internal").ap()
    edge_list = nc.dram_tensor("edge_list", (P * TT, 3), I32, kind="Internal").ap()
    tile_dram = nc.dram_tensor("tile_dram", (P * TPP,), I32, kind="Internal").ap()
    xtile_dram = nc.dram_tensor("xtile_dram", (2, P * XPP), I32, kind="Internal").ap()
    x_sorted = nc.dram_tensor("x_sorted", (TX * P, C), F32, kind="Internal").ap()
    y_sorted = nc.dram_tensor("y_sorted", (TX * P, C), F32, kind="Internal").ap()

    with ExitStack() as whole:
        def sem(name):
            return whole.enter_context(nc.semaphore(name))

        def sb(name, shape, dtype, scope=whole):
            return scope.enter_context(nc.sbuf_tensor(name, shape, dtype))

        acc = sb("acc", [P, NB, C], F32)
        ident = sb("ident", [P, P], F32)
        iota_n = sb("iota_n", [P, P], F32)
        tri = sb("tri", [P, P], BF16)
        tri_rest = sb("tri_rest", [P, P], BF16)
        ones_bf = sb("ones_bf", [P, P], BF16)
        row_mean = sb("row_mean", [P, NB, 2], F32)
        rstd = sb("rstd", [P, NB], F32)
        newton = sb("newton", [P, NB], F32)
        stats = sb("stats", [P, 2, 6], F32)
        pair_stats = sb("pair_stats", [P, 2, 2], F32)
        turn_mark = sb("turn_mark", [P, 1], F32)
        eps_col = sb("eps_col", [P, 1], F32)

        early = ExitStack()
        record = sb("record", [P, ET, 4], I32, early)
        block_bf = sb("block_bf", [P, ET], BF16, early)
        onehot = sb("onehot", [P, 2, NB, CH], BF16, early)
        totals = sb("totals", [P, NB, CH], F32, early)
        picked = totals
        base = sb("base", [P, NB, CH], F32, early)
        scan_a = sb("scan_a", [P, NB], F32, early)
        scan_b = sb("scan_b", [P, NB], F32, early)
        scan_i = sb("scan_i", [P, NB], I32, early)
        pos_f = sb("pos_f", [P, CH], F32, early)
        pos_i = sb("pos_i", [P, 3, CH], I32, early)
        iota_b = sb("iota_b", [P, NB, CH], BF16, early)
        iota_t = sb("iota_t", [P, TPP], F32, early)
        tile_f = sb("tile_f", [P, TPP], F32, early)
        tile_i = sb("tile_i", [P, TPP], I32, early)
        tile_row = sb("tile_row", [1, P * TPP], I32, early)
        scatter_stage = sb("scatter_stage", [P, 2, CH, 4], I32, early)
        zeros = sb("zeros", [P, 4 * C], F32, early)
        w_cat = sb("w_cat", [P, KC, 4 * C], F32, early)
        wp_t = sb("wp_t", [P, KC, C], F32, early)
        head_mask = sb("head_mask", [P, P], F32, early)
        row_ok = sb("row_ok", [P, 2, P], F32, early)
        bias_row = sb("bias_row", [P, C], F32, early)
        ctx_t = sb("ctx_t", [P, KC, P], F32, early)
        ksum = sb("ksum", [P, C], F32, early)
        mix_w = sb("mix_w", [P, KC, C], F32, early)
        xn = sb("xn", [P, 2, C], F32, early)
        inputs = ExitStack()
        src_i = sb("src_i", [P, ET], I32, inputs)
        dst_i = sb("dst_i", [P, ET], I32, inputs)
        w_in = sb("w_in", [P, ET], I32, inputs)
        tile_cmp = sb("tile_cmp", [P, TPP, NB], F32, inputs)
        w_nat = sb("w_nat", [P, 8, C], F32, inputs)
        bias_in = sb("bias_in", [P, 2, C], F32, inputs)
        inputs.close()
        attention = ExitStack()
        h_out = sb("h_out", [P, 2, 2, C], F32, attention)
        q_out = sb("q_out", [P, 2, 2, C], F32, attention)
        k_act = sb("k_act", [P, 2, 2, C], F32, attention)
        v_sb = sb("v_sb", [P, 2, 2, C], F32, attention)
        exp_kq = sb("exp_kq", [P, 2, 2, C], F32, attention)
        relu_kq = sb("relu_kq", [P, 2, 2, C], F32, attention)
        xn_t = sb("xn_t", [P, 2, KC, 2 * P], F32, attention)
        den = sb("den", [P, 4, 2 * HEADS], F32, attention)
        attention.close()
        gather_stage = sb("gather_stage", [P, RING, SET, 3], I32, early)
        message = sb("message", [P, RING, SET, C], F32, early)
        select = sb("select", [P, 2, SET, P], F32, early)
        early.close()

        w1 = sb("w1", [P, EXPERTS, KC, HID], F32)
        fx = sb("fx", [P, 2, C], F32)
        fx_t = sb("fx_t", [P, 2, KC, P], F32)
        hid = sb("hid", [P, 2, HID], F32)
        hid_t = sb("hid_t", [P, 2, KH, P], F32)
        fy = sb("fy", [P, 2, C], F32)
        wg = sb("wg", [P, KC, EXPERTS], F32)
        gate_b = sb("gate_b", [P, 2, EXPERTS], F32)
        top_w = sb("top_w", [P, 2, NB], F32)
        token_pos = sb("token_pos", [P, NB, 2], I32)
        pos_stage = sb("pos_stage", [P, 2, 2, 2], I32)
        xtile_row = sb("xtile_row", [1, 2, P * XPP], I32)
        route = ExitStack()
        logits = sb("logits", [P, NB, EXPERTS], F32, route)
        pick = sb("pick", [P, 2, NB, EXPERTS], F32, route)
        both_bf = sb("both_bf", [P, NB, EXPERTS], BF16, route)
        work = sb("work", [P, NB, EXPERTS], F32, route)
        rank = sb("rank", [P, NB, EXPERTS], F32, route)
        carry_a = sb("carry_a", [P, NB, EXPERTS], F32, route)
        carry_b = sb("carry_b", [P, NB, EXPERTS], F32, route)
        small = sb("small", [P, 6, NB], F32, route)
        iota_e = sb("iota_e", [P, 2, EXPERTS], F32, route)
        ends = sb("ends", [P, 4, EXPERTS], F32, route)
        ends_i = sb("ends_i", [P, EXPERTS], I32, route)
        iota_x = sb("iota_x", [P, XPP], F32, route)
        xcmp = sb("xcmp", [P, XPP, EXPERTS], F32, route)
        xtile_f = sb("xtile_f", [P, XPP], F32, route)
        xtile_i = sb("xtile_i", [P, 2, XPP], I32, route)
        fxn = sb("fxn", [P, 2, 2, C], F32, route)
        fxn_t = sb("fxn_t", [P, 2, KC, 2 * P], F32, route)
        route.close()
        w2 = sb("w2", [P, EXPERTS, KH, C], F32)
        b12 = sb("b12", [P, EXPERTS, HID + C], F32)

        bank = [whole.enter_context(nc.psum_tensor(f"bank{i}", [P, 512], F32)) for i in range(8)]

        s_const = sem("s_const")
        s_passed = sem("s_passed")
        s_pool = sem("s_pool")
        s_dve = sem("s_dve")
        s_act = sem("s_act")
        s_edges = sem("s_edges")
        s_x = sem("s_x")
        s_wload = sem("s_wload")
        s_zeroed = sem("s_zeroed")
        s_record = sem("s_record")
        s_hot = sem("s_hot")
        s_hot_read = sem("s_hot_read")
        s_base = sem("s_base")
        s_rank = sem("s_rank")
        s_rank_read = sem("s_rank_read")
        s_rank_next = sem("s_rank_next")
        s_pos = sem("s_pos")
        s_staged = [sem(f"s_staged{i}") for i in range(2)]
        s_scattered = [sem(f"s_scattered{i}") for i in range(2)]
        s_tile_out = sem("s_tile_out")
        s_tile_dram = sem("s_tile_dram")
        s_tile_row = sem("s_tile_row")
        s_wt_psum = sem("s_wt_psum")
        s_wt = sem("s_wt")
        s_var = sem("s_var")
        s_std = sem("s_std")
        s_xn = sem("s_xn")
        s_xt_psum = sem("s_xt_psum")
        s_xt = sem("s_xt")
        s_proj = sem("s_proj")
        s_proj_read = sem("s_proj_read")
        s_kq = sem("s_kq")
        s_hq_out = [sem(f"s_hq_out{i}") for i in range(2)]
        s_ctx = sem("s_ctx")
        s_ctx_sb = sem("s_ctx_sb")
        s_mixw_psum = sem("s_mixw_psum")
        s_mixw = sem("s_mixw")
        s_q_in = [sem(f"s_q_in{i}") for i in range(2)]
        s_qn = sem("s_qn")
        s_qt_psum = sem("s_qt_psum")
        s_qt = sem("s_qt")
        s_mix = sem("s_mix")
        s_mix_added = sem("s_mix_added")
        s_list = [sem(f"s_list{i}") for i in range(RING)]
        s_message = [sem(f"s_message{i}") for i in range(RING)]
        s_select = sem("s_select")
        s_agg = sem("s_agg")
        s_added = sem("s_added")
        s_w1 = sem("s_w1")
        s_w2 = sem("s_w2")
        s_fin = sem("s_fin")
        s_gate = sem("s_gate")
        s_gate_read = sem("s_gate_read")
        s_route = sem("s_route")
        s_route_psum = sem("s_route_psum")
        s_route_done = sem("s_route_done")
        s_xtile_dram = sem("s_xtile_dram")
        s_xtile_row = sem("s_xtile_row")
        s_pos_in = [sem(f"s_pos_in{i}") for i in range(2)]
        s_fxn = sem("s_fxn")
        s_sent = [sem(f"s_sent{i}") for i in range(2)]
        s_fx = [sem(f"s_fx{i}") for i in range(2)]
        s_fxt_psum = sem("s_fxt_psum")
        s_fxt = sem("s_fxt")
        s_hid_psum = sem("s_hid_psum")
        s_hid = sem("s_hid")
        s_hidt_psum = sem("s_hidt_psum")
        s_hidt = sem("s_hidt")
        s_fy_psum = sem("s_fy_psum")
        s_fy = sem("s_fy")
        s_fy_out = [sem(f"s_fy_out{i}") for i in range(2)]
        s_back_idx = [sem(f"s_back_idx{i}") for i in range(2)]
        s_back = [sem(f"s_back{i}") for i in range(2)]
        s_sum = sem("s_sum")
        s_out = [sem(f"s_out{i}") for i in range(2)]

        back_1 = w1[:, 0:2, :, :].rearrange("p s u n -> p s (u n)")[:, :, 0:2 * C].rearrange("p s (u c) -> p s u c", u=2)
        back_2 = w1[:, 2:4, :, :].rearrange("p s u n -> p s (u n)")[:, :, 0:2 * C].rearrange("p s (u c) -> p s u c", u=2)
        result = w1[:, 4:6, :, :].rearrange("p s u n -> p s (u n)")[:, :, 0:2 * C].rearrange("p s (u c) -> p s u c", u=2)

        block = whole.enter_context(nc.Block())
        full = E // ET
        wide = full // 16 * 16
        edge_parts = [(0, wide), (wide, full)] if full > wide else [(0, wide)]
        edge_parts = [(a, b) for a, b in edge_parts if b > a]
        rest = E - full * ET
        x_full = x[0:(NB - 1) * P, :].rearrange("(b p) c -> p b c", p=P)

        XCUT = [0, NB // 4, NB // 2, NB - 1]
        N_EDGE_LOADS = 3 * (len(edge_parts) + (1 if rest else 0))

        @block.sync
        def _(sp):
            sp.wait_ge(s_const, 1)
            for a, b in edge_parts:
                for tile, arr in ((src_i, src), (dst_i, dst), (w_in, edge_weight.bitcast(I32))):
                    sp.dma_start(tile[a:b, :], arr[a * ET:b * ET].rearrange("(p t) -> p t", t=ET)).then_inc(s_edges, 16)
            if rest:
                for tile, arr in ((src_i, src), (dst_i, dst), (w_in, edge_weight.bitcast(I32))):
                    sp.dma_start(tile[full:full + 1, 0:rest], arr[full * ET:E].rearrange("(a n) -> a n", a=1)).then_inc(s_edges, 16)
            sp.wait_ge(s_const, 2)
            for a, b in zip(XCUT[:-1], XCUT[1:]):
                sp.dma_start(acc[:, a:b, :], x_full[:, a:b, :]).then_inc(s_x, 16)
            sp.dma_start(acc[0:LAST, NB - 1, :], x[(NB - 1) * P:N, :]).then_inc(s_x, 16)
            sp.dma_start(w_nat[:, 0:2, :], mix_Wq.rearrange("(a p) c -> p a c", p=P)).then_inc(s_wload, 16)
            sp.dma_start(w_nat[:, 2:6, :], mix_Wkv.rearrange("(a p) c -> p a c", p=P)).then_inc(s_wload, 16)
            sp.dma_start(w_nat[:, 6:8, :], mix_Wproj.rearrange("(a p) c -> p a c", p=P)).then_inc(s_wload, 16)
            sp.dma_start(w_cat[:, :, 0:C], gnn_W.rearrange("(k p) n -> p k n", p=P)).then_inc(s_wload, 16)
            sp.dma_start(bias_in[:, 0, :], gnn_b.partition_broadcast(P)).then_inc(s_wload, 16)
            sp.dma_start(bias_in[:, 1, :], mix_bproj.partition_broadcast(P)).then_inc(s_wload, 16)
            lrow = edge_list.rearrange("(p t) c -> p (t c)", p=P)
            zcols = 4 * C
            nz = 0
            for a in range(0, 3 * TT, zcols):
                b = min(a + zcols, 3 * TT)
                sp.dma_start(lrow[:, a:b], zeros[:, 0:b - a].bitcast(I32)).then_inc(s_zeroed, 16)
                nz += 1
            sp.dma_start(x_sorted.rearrange("(p t) c -> p t c", p=P),
                         zeros[:, 0:C].unsqueeze(1).to_broadcast([P, TX, C])).then_inc(s_zeroed, 16)
            sp.wait_ge(s_tile_out, 1)
            sp.dma_start(tile_dram.rearrange("(p t) -> p t", p=P), tile_i[:, :]).then_inc(s_tile_dram, 16)
            sp.wait_ge(s_tile_dram, 16)
            sp.dma_start(tile_row[:, :], tile_dram.rearrange("(a n) -> a n", a=1)).then_inc(s_tile_row, 16)
            sp.wait_ge(s_record, 4)

            def stage(first_tile, slot):
                sp.dma_start(scatter_stage[:, slot, :, :], record[:, ds(first_tile, CH), :]).then_inc(s_staged[slot], 16)
            for slot in range(2):
                sp.wait_ge(s_pos, slot + 1)
                stage(slot * CH, slot)
            with sp.Fori(1, CHUNKS // 2) as m:
                for slot in range(2):
                    first_tile = sp.snap(m * (2 * CH) + slot * CH)
                    sp.wait_ge(s_pos, m * 2 + (slot + 1))
                    sp.sem_inc(s_passed, 1)
                    sp.wait_ge(s_scattered[slot], m * (16 * CH))
                    stage(first_tile, slot)

            for slot in range(2):
                sp.wait_ge(s_scattered[slot], 16 * CH * (CHUNKS // 2))
            sp.wait_ge(s_mix_added, PAIRS)
            lset = edge_list.rearrange("(p t) c -> p t c", p=P)

            def stage_list(first_tile, slot):
                sp.dma_start(gather_stage[:, slot, :, :], lset[:, ds(first_tile, SET), :]).then_inc(s_list[slot], 16)
            for slot in range(RING):
                stage_list(slot * SET, slot)
            with sp.Fori(1, TSETS // RING) as m:
                for slot in range(RING):
                    first_tile = sp.snap((m * RING + slot) * SET)
                    sp.wait_ge(s_agg, m * RING + (slot - RING + 1))
                    stage_list(first_tile, slot)

            sp.wait_ge(s_added, TSETS)
            sp.dma_start(w1[:, :, :, :], ffn_W1.rearrange("e (k p) n -> p e k n", p=P)).then_inc(s_w1, 16)
            sp.dma_start(wg[:, :, :], ffn_Wg.rearrange("(k p) n -> p k n", p=P)).then_inc(s_fin, 16)
            sp.dma_start(gate_b[:, 0, :], ffn_bg.partition_broadcast(P)).then_inc(s_fin, 16)
            sp.dma_start(gate_b[:, 1, :], ffn_bias.partition_broadcast(P)).then_inc(s_fin, 16)
            sp.wait_ge(s_route_done, 1)
            sp.dma_start(xtile_dram.rearrange("a (p t) -> p a t", p=P), xtile_i[:, :, :]).then_inc(s_xtile_dram, 16)
            sp.wait_ge(s_xtile_dram, 16)
            sp.dma_start(xtile_row[:, :, :], xtile_dram.unsqueeze(0)).then_inc(s_xtile_row, 16)

            def stage_pos(b, slot, signal):
                sp.dma_start(pos_stage[:, slot, :, :], token_pos[:, ds(b, 2), :]).then_inc(signal[slot], 16)
            for g in range(2):
                stage_pos(2 * g, g, s_pos_in)
            with sp.Fori(1, PAIRS // 2) as m:
                for slot in range(2):
                    first_block = sp.snap(m * 4 + 2 * slot)
                    sp.wait_ge(s_sent[slot], m * 64)
                    stage_pos(first_block, slot, s_pos_in)
            sp.wait_ge(s_sent[0], PAIRS // 2 * 64)
            stage_pos(NB - 2, 0, s_pos_in)

            sp.wait_ge(s_sent[0], (PAIRS // 2 + 1) * 64)
            sp.wait_ge(s_sent[1], PAIRS // 2 * 64)
            sp.wait_ge(s_xtile_row, 16)
            sp.dma_start(w2[:, :, :, :], ffn_W2.rearrange("e (k p) n -> p e k n", p=P)).then_inc(s_w2, 16)
            sp.dma_start(b12[:, :, 0:HID], ffn_b1.partition_broadcast(P)).then_inc(s_w2, 16)
            sp.dma_start(b12[:, :, HID:HID + C], ffn_b2.partition_broadcast(P)).then_inc(s_w2, 16)

            x_tiles = x_sorted.rearrange("(t p) c -> t p c", p=P)

            def load_x(t, slot):
                sp.dma_start(fx[:, slot, :], x_tiles[ds(t, 1), :, :].rearrange("a p c -> p (a c)")).then_inc(s_fx[slot], 16)
            for slot in range(2):
                load_x(slot, slot)
            with sp.Fori(1, TX // 2) as m:
                for slot in range(2):
                    tile = sp.snap(m * 2 + slot)
                    sp.wait_ge(s_fxt_psum, m * 2 + (slot - 1))
                    load_x(tile, slot)

            for s in range(2):
                sp.wait_ge(s_fy_out[s], 16 * (TX // 2))
            for g in range(2):
                stage_pos(2 * g, g, s_back_idx)
            with sp.Fori(1, PAIRS // 2) as m:
                for slot in range(2):
                    first_block = sp.snap(m * 4 + 2 * slot)
                    sp.wait_ge(s_back[slot], m * 64)
                    stage_pos(first_block, slot, s_back_idx)
            sp.wait_ge(s_back[0], PAIRS // 2 * 64)
            stage_pos(NB - 2, 0, s_back_idx)

        @block.gpsimd
        def _(pool):
            steps = Steps(pool, s_pool)
            pool.memset(src_i[:, :], NB * P - 1)
            pool.memset(dst_i[:, :], 0)
            pool.memset(w_in[:, :], 0).then_inc(s_const, 1)
            pool.memset(acc[:, NB - 1, :], 0.0)
            pool.memset(zeros[:, :], 0.0).then_inc(s_const, 1)
            pool.iota(iota_b[:, :, :], [[1, NB], [0, CH]], base=0, channel_multiplier=0, allow_small_or_imprecise_dtypes=True)
            pool.iota(iota_t[:, :], [[1, TPP]], base=0, channel_multiplier=TPP, allow_small_or_imprecise_dtypes=True)
            pool.iota(iota_n[:, :], [[1, P]], base=0, channel_multiplier=0, allow_small_or_imprecise_dtypes=True)
            pool.memset(eps_col[:, :], EPS)
            steps.done(pool.memset(ones_bf[:, :], 1.0))
            steps.done(pool.memset(ident[:, :], 0.0))
            steps.done(pool.memset(head_mask[:, :], 1.0))
            steps.done(pool.memset(row_ok[:, :, :], 1.0))
            steps.settle()
            pool.affine_select(out=tri[:, :], in_=ones_bf[:, :], pattern=[[1, P]], compare_op=ALU.is_gt,
                               fill=0.0, base=0, channel_multiplier=-1)
            pool.affine_select(out=tri_rest[:, :], in_=ones_bf[:, :], pattern=[[-1, P]], compare_op=ALU.is_ge,
                               fill=0.0, base=0, channel_multiplier=1)
            pool.affine_select(out=row_ok[:, 1, :], in_=row_ok[:, 1, :], pattern=[[0, P]], compare_op=ALU.is_ge,
                               fill=0.0, base=LAST - 1, channel_multiplier=-1)
            heads = head_mask[:, :].rearrange("p (h d) -> p h d", d=HD)
            steps.done(pool.affine_select(out=heads, in_=heads, pattern=[[-HD, P // HD], [0, HD]],
                                          compare_op=ALU.is_ge, fill=0.0, base=0, channel_multiplier=1))
            steps.settle()
            pool.affine_select(out=heads, in_=heads, pattern=[[HD, P // HD], [0, HD]],
                               compare_op=ALU.is_ge, fill=0.0, base=HD - 1, channel_multiplier=-1)
            pool.affine_select(out=ident[:, :], in_=ident[:, :], pattern=[[-1, P]], compare_op=ALU.not_equal,
                               fill=1.0, base=0, channel_multiplier=1).then_inc(s_const, 1)
            pool.wait_ge(s_edges, 16 * N_EDGE_LOADS)
            pool.tensor_copy(record[:, :, 1], dst_i[:, :]).then_inc(s_record, 1)
            pool.tensor_copy(record[:, :, 3], w_in[:, :]).then_inc(s_record, 1)

            n_zero = -(-3 * TT // (4 * C)) + 1
            def pass_gate():
                pool.sem_inc(s_passed, 1)
            pool.wait_ge(s_zeroed, 16 * n_zero)
            with pool.Fori(0, CHUNKS // 2) as m:
                for slot in range(2):
                    pool.wait_ge(s_staged[slot], m * 16 + 16)
                    pass_gate()
                    for j in range(CH):
                        pool.indirect_dma_start(
                            out=edge_list, out_offset=Offset(ap=scatter_stage[:, slot, j, 0:1], axis=0),
                            in_=scatter_stage[:, slot, j, 1:4], in_offset=None).then_inc(s_scattered[slot], 16)

            pool.wait_ge(s_hq_out[0], 32 * (PAIRS // 2 + 1))
            pool.wait_ge(s_hq_out[1], 32 * (PAIRS // 2))

            def gather_set(slot):
                pass_gate()
                for j in range(SET):
                    pool.indirect_dma_start(
                        out=message[:, slot, j, :], out_offset=None, in_=h_table,
                        in_offset=Offset(ap=gather_stage[:, slot, j, 0:1], axis=0)).then_inc(s_message[slot], 16)
            for slot in range(RING):
                pool.wait_ge(s_list[slot], 16)
                gather_set(slot)
            with pool.Fori(1, TSETS // RING) as m:
                for slot in range(RING):
                    pool.wait_ge(s_list[slot], m * 16 + 16)
                    gather_set(slot)

            pool.wait_ge(s_added, TSETS)
            pool.iota(iota_e[:, 0, :], [[1, EXPERTS]], base=0, channel_multiplier=0, allow_small_or_imprecise_dtypes=True)
            pool.iota(iota_e[:, 1, :], [[1, EXPERTS]], base=-EXPERTS, channel_multiplier=0, allow_small_or_imprecise_dtypes=True)
            pool.iota(iota_x[:, :], [[1, XPP]], base=0, channel_multiplier=XPP,
                      allow_small_or_imprecise_dtypes=True).then_inc(s_const, 1)

            def send(g, slot):
                pool.wait_ge(s_pos_in[slot], g * 8 + (16 - 8 * slot))
                pool.wait_ge(s_fxn, PAIRS + 1 + g)
                pass_gate()
                for u in range(2):
                    for k in range(2):
                        pool.indirect_dma_start(
                            out=x_sorted, out_offset=Offset(ap=pos_stage[:, slot, u, k:k + 1], axis=0),
                            in_=fxn[:, slot, u, :], in_offset=None).then_inc(s_sent[slot], 16)
            with pool.Fori(0, PAIRS // 2) as m:
                for slot in range(2):
                    send(m * 2 + slot, slot)
            send(PAIRS - 1, 0)

            def fetch(g, slot, first=False):
                pool.wait_ge(s_back_idx[slot], g * 8 + (16 - 8 * slot))
                if not first:
                    pool.wait_ge(s_sum, g - 1)
                pass_gate()
                for u in range(2):
                    for k, into in ((0, back_1), (1, back_2)):
                        pool.indirect_dma_start(
                            out=into[:, slot, u, :], out_offset=None, in_=y_sorted,
                            in_offset=Offset(ap=pos_stage[:, slot, u, k:k + 1], axis=0)).then_inc(s_back[slot], 16)
            for s in range(2):
                fetch(s, s, first=True)
            with pool.Fori(1, PAIRS // 2) as m:
                for slot in range(2):
                    fetch(m * 2 + slot, slot)
            fetch(PAIRS - 1, 0)

        @block.scalar
        def _(act):
            steps = Steps(act, s_act)
            for i in range(4):
                act.wait_ge(s_wt_psum, i + 1)
                ps = bank[2 + i][:, :].rearrange("p (k a n) -> p k a n", k=KC, a=2)
                into = [w_cat[:, :, 3 * C:4 * C], w_cat[:, :, C:2 * C], w_cat[:, :, 2 * C:3 * C], wp_t[:, :, :]][i]
                act.activation(into.rearrange("p k (a n) -> p k a n", a=2), ps, ACT.Copy).then_inc(s_wt, 1)

            act.wait_ge(s_var, 1)
            act.activation(rstd[:, :], row_mean[:, :, 1], ACT.Sqrt, bias=eps_col[:, :]).then_inc(s_std, 1)

            def project(g, slot, first=False):
                act.wait_ge(s_xt_psum, g + 1)
                act.activation(xn_t[:, slot, :, :].rearrange("p k n -> p (k n)"), bank[2][:, :], ACT.Copy).then_inc(s_xt, 1)
                if not first:
                    for_slot = (g - slot) * 16
                    act.wait_ge(s_hq_out[slot], for_slot)
                    act.wait_ge(s_ctx, g - 1)
                for u in range(2):
                    act.wait_ge(s_proj, g * 2 + (u + 1))
                    hk, vq = bank[3 + 2 * u], bank[4 + 2 * u]
                    act.activation(h_out[:, slot, u, :], hk[:, 0:C], ACT.Copy)
                    act.activation(v_sb[:, slot, u, :], vq[:, 0:C], ACT.Copy)
                    if u == 0 and not first:
                        act.wait_ge(s_kq, g * 2)
                    elif u == 0 and slot == 1:
                        act.wait_ge(s_kq, 2)
                    act.activation(exp_kq[:, 0, u, :], hk[:, C:2 * C], ACT.Exp)
                    act.activation(exp_kq[:, 1, u, :], vq[:, C:2 * C], ACT.Exp)
                    act.activation(relu_kq[:, 0, u, :], hk[:, C:2 * C], ACT.Relu)
                    act.activation(relu_kq[:, 1, u, :], vq[:, C:2 * C], ACT.Relu).then_inc(s_proj_read, 1)

            h_pairs = h_table.rearrange("(g u p) c -> g p u c", u=2, p=P)

            def store(g, slot):
                act.wait_ge(s_proj_read, g * 2 + 2)
                act.dma_start(h_pairs[ds(g, 1), :, :, :].rearrange("a p u c -> p (a u) c"),
                              h_out[:, slot, :, :]).then_inc(s_hq_out[slot], 16)
                act.wait_ge(s_kq, g * 2 + 2)
                act.dma_start(q_dram[ds(g, 1), :, :].rearrange("a p n -> p (a n)"),
                              q_out[:, slot, :, :].rearrange("p u c -> p (u c)")).then_inc(s_hq_out[slot], 16)
            for g in range(2):
                project(g, g, first=True)
                store(g, g)
            with act.Fori(1, PAIRS // 2) as m:
                for slot in range(2):
                    project(m * 2 + slot, slot)
                    store(m * 2 + slot, slot)
            project(PAIRS - 1, 0)
            store(PAIRS - 1, 0)

            def bring_q(g, slot):
                act.dma_start(q_out[:, slot, :, :].rearrange("p u c -> p (u c)"),
                              q_dram[ds(g, 1), :, :].rearrange("a p n -> p (a n)")).then_inc(s_q_in[slot], 16)

            def copy_qt(g, slot, first=False):
                act.wait_ge(s_qt_psum, g + 1)
                if not first:
                    act.wait_ge(s_mix, g - 1)
                act.activation(xn_t[:, slot, :, :].rearrange("p k n -> p (k n)"), bank[2][:, :], ACT.Copy).then_inc(s_qt, 1)
            for s in range(2):
                act.wait_ge(s_hq_out[s], 32 * (PAIRS // 2 + (PAIRS % 2 if s == 0 else 0)))
            for g in range(2):
                bring_q(g, g)

            def q_turn(g, slot, first=False):
                copy_qt(g - 2, slot, first)
                act.wait_ge(s_qn, g - 1)
                bring_q(g, slot)
            for slot in range(2):
                q_turn(2 + slot, slot, first=True)
            with act.Fori(2, PAIRS // 2) as m:
                for slot in range(2):
                    q_turn(m * 2 + slot, slot)
            copy_qt(PAIRS - 3, 0)
            act.wait_ge(s_qn, PAIRS - 2)
            bring_q(PAIRS - 1, 0)
            copy_qt(PAIRS - 2, 1)
            copy_qt(PAIRS - 1, 0)

            act.wait_ge(s_var, 2)
            act.activation(rstd[:, :], row_mean[:, :, 1], ACT.Sqrt, bias=eps_col[:, :]).then_inc(s_std, 1)

            def gate_copy(g, slot, first=False):
                act.wait_ge(s_xt_psum, PAIRS + 1 + g)
                if not first:
                    act.wait_ge(s_gate, g - 1)
                act.activation(fxn_t[:, slot, :, :].rearrange("p k n -> p (k n)"), bank[slot][:, :], ACT.Copy).then_inc(s_xt, 1)
            for slot in range(2):
                gate_copy(slot, slot, first=True)
            with act.Fori(1, PAIRS // 2) as m:
                for slot in range(2):
                    gate_copy(m * 2 + slot, slot)
            gate_copy(PAIRS - 1, 0)
            act.wait_ge(s_route, 1)
            act.activation(top_w[:, 1, :], small[:, 4, :], ACT.Exp).then_inc(s_route, 1)

            y_tiles = y_sorted.rearrange("(t p) c -> t p c", p=P)

            def copy_x(t, slot, first=False):
                act.wait_ge(s_fxt_psum, t + 1)
                if not first:
                    act.wait_ge(s_hid_psum, t - 1)
                act.activation(fx_t[:, slot, :, :].rearrange("p k n -> p (k n)"), bank[slot][:, 0:C], ACT.Copy).then_inc(s_fxt, 1)

            def hidden(t, slot, first=False):
                act.wait_ge(s_hidt_psum, t + 1)
                if not first:
                    act.wait_ge(s_fy_psum, t - 1)
                act.activation(hid_t[:, slot, :, :].rearrange("p k n -> p (k n)"), bank[4 + slot][:, :], ACT.Relu).then_inc(s_hidt, 1)

            def store_y(t, slot):
                act.wait_ge(s_fy, t + 1)
                act.dma_start(y_tiles[ds(t, 1), :, :].rearrange("a p c -> p (a c)"), fy[:, slot, :]).then_inc(s_fy_out[slot], 16)

            def expert_pair(t, first=False, last=False):
                hidden(t, 0, first)
                if not last:
                    copy_x(t + 2, 0)
                    copy_x(t + 3, 1)
                hidden(t + 1, 1, first)
                store_y(t, 0)
                store_y(t + 1, 1)
            copy_x(0, 0, first=True)
            copy_x(1, 1, first=True)
            expert_pair(0, first=True)
            with act.Fori(1, TX // 2 - 1) as m:
                expert_pair(m * 2)
            expert_pair(TX - 2, last=True)

            out_full = out[0:(PAIRS - 1) * 2 * P, :].rearrange("(g u p) c -> g p u c", u=2, p=P)

            def store_out(g, slot):
                act.wait_ge(s_sum, g + 1)
                act.dma_start(out_full[ds(g, 1), :, :, :].rearrange("a p u c -> p (a u) c"),
                              result[:, slot, :, :]).then_inc(s_out[slot], 16)
            with act.Fori(0, PAIRS // 2) as m:
                for slot in range(2):
                    store_out(m * 2 + slot, slot)
            act.wait_ge(s_sum, PAIRS)
            act.dma_start(out[(NB - 2) * P:(NB - 1) * P, :], result[:, 0, 0, :]).then_inc(s_out[0], 16)
            act.dma_start(out[(NB - 1) * P:N, :], result[0:LAST, 0, 1, :]).then_inc(s_out[0], 16)
            act.wait_ge(s_out[0], 16 * (PAIRS // 2 + 2))
            act.wait_ge(s_out[1], 16 * (PAIRS // 2))

        @block.tensor
        def _(pe):
            pe.wait_ge(s_const, 3)
            def counts(i):
                return bank[i][:, 0:HB * CH]

            def hot(slot, half):
                return onehot[:, slot, half * HB:(half + 1) * HB, :].rearrange("p b t -> p (b t)")

            def count(chunk, slot, first=False):
                pe.wait_ge(s_hot, chunk + 1)
                for half in range(2):
                    last = nc.tensor.matmul(counts(half), ones_bf[:, :], hot(slot, half), start=first, stop=True,
                                            skip_group_check=True)
                last.then_inc(s_hot_read, 1)
            count(0, 0, first=True)
            count(1, 1)
            with pe.Fori(1, CHUNKS // 2) as m:
                for slot in range(2):
                    count(m * 2 + slot, slot)
            pe.wait_ge(s_base, 1)
            for half in range(2):
                nc.tensor.matmul(counts(half), ident[:, :],
                                 base[:, half * HB:(half + 1) * HB, :].rearrange("p b t -> p (b t)"),
                                 start=True, stop=True, skip_group_check=True)

            def ranks(chunk, slot):
                pe.wait_ge(s_hot, chunk + (CHUNKS + 1))
                for half in range(2):
                    nc.tensor.matmul(counts(half), tri[:, :], hot(slot, half), start=False, stop=True,
                                     skip_group_check=True).then_inc(s_rank, 1)
                for half in range(2):
                    pe.wait_ge(s_rank_read, chunk * 2 + (half + 1))
                    last = nc.tensor.matmul(counts(half), tri_rest[:, :], hot(slot, half), start=False, stop=True,
                                            skip_group_check=True)
                last.then_inc(s_rank_next, 1)
            with pe.Fori(0, CHUNKS // 2) as m:
                for slot in range(2):
                    ranks(m * 2 + slot, slot)

            pe.wait_ge(s_wload, 16 * 6)
            for i in range(4):
                for k in range(KC):
                    for a in range(2):
                        last = nc.tensor.transpose(bank[2 + i][:, (k * 2 + a) * P:(k * 2 + a + 1) * P],
                                                   w_nat[:, 2 * i + a, k * P:(k + 1) * P], ident[:, :])
                last.then_inc(s_wt_psum, 1)
            pe.wait_ge(s_wt, 4)

            def transpose_pair(source, ps, signal):
                for k in range(KC):
                    for u in range(2):
                        last = nc.tensor.transpose(ps[:, (k * 2 + u) * P:(k * 2 + u + 1) * P],
                                                   source[:, u, k * P:(k + 1) * P], ident[:, :])
                last.then_inc(signal, 1)

            def normed(g, first=False):
                pe.wait_ge(s_xn, g + 1)
                if not first:
                    pe.wait_ge(s_xt, g)
                transpose_pair(xn, bank[2], s_xt_psum)

            def project(g, slot, first=False):
                pe.wait_ge(s_xt, g + 1)
                for u in range(2):
                    if not first:
                        pe.wait_ge(s_proj_read, g * 2 + (u - 1))
                    for cols, ps in ((0, bank[3 + 2 * u]), (2 * C, bank[4 + 2 * u])):
                        for k in range(KC):
                            last = nc.tensor.matmul(ps[:, :], xn_t[:, slot, k, u * P:(u + 1) * P],
                                                    w_cat[:, k, cols:cols + 2 * C], start=(k == 0), stop=(k == KC - 1))
                    last.then_inc(s_proj, 1)

            def context(g, slot, first=False, final=False):
                pe.wait_ge(s_kq, g * 2 + 1)
                for u in range(2):
                    ok = row_ok[:, 1 if final and u == 1 else 0, :]
                    for h in range(KC):
                        nc.tensor.matmul(bank[7][:, h * P:(h + 1) * P], v_sb[:, slot, u, h * P:(h + 1) * P],
                                         k_act[:, slot, u, h * P:(h + 1) * P],
                                         start=(first and u == 0 and h == 0), stop=True, skip_group_check=True)
                    last = nc.tensor.matmul(bank[7][:, C:2 * C], ok, k_act[:, slot, u, :], start=False, stop=True,
                                            skip_group_check=True)
                last.then_inc(s_ctx, 1)
            normed(0, first=True)
            normed(1)
            project(0, 0, first=True)
            normed(2)
            project(1, 1)
            context(0, 0, first=True)
            with pe.Fori(1, PAIRS // 2) as m:
                for slot in range(2):
                    g = m * 2 + slot
                    normed(g + 1)
                    project(g, slot)
                    context(g - 1, 1 - slot)
            project(PAIRS - 1, 0)
            context(PAIRS - 2, 1)
            context(PAIRS - 1, 0, final=True)

            pe.wait_ge(s_ctx_sb, 1)
            for h in range(KC):
                last = nc.tensor.matmul(bank[5][:, h * C:(h + 1) * C], ctx_t[:, h, :], wp_t[:, h, :],
                                        start=True, stop=True)
            last.then_inc(s_mixw_psum, 1)

            def q_transpose(g, first=False):
                pe.wait_ge(s_qn, g + 1)
                if not first:
                    pe.wait_ge(s_qt, g)
                transpose_pair(xn, bank[2], s_qt_psum)

            def mix(g, slot, first=False):
                pe.wait_ge(s_qt, g + 1)
                if not first:
                    pe.wait_ge(s_mix_added, g - 1)
                for u in range(2):
                    ps = bank[3 + slot][:, u * C:(u + 1) * C]
                    for k in range(KC):
                        last = nc.tensor.matmul(ps, xn_t[:, slot, k, u * P:(u + 1) * P], mix_w[:, k, :],
                                                start=(k == 0), stop=(k == KC - 1))
                last.then_inc(s_mix, 1)
            pe.wait_ge(s_mixw, 1)
            q_transpose(0, first=True)
            q_transpose(1)
            mix(0, 0, first=True)
            q_transpose(2)
            mix(1, 1, first=True)
            with pe.Fori(1, PAIRS // 2) as m:
                for slot in range(2):
                    g = m * 2 + slot
                    q_transpose(g + 1)
                    mix(g, slot)
            mix(PAIRS - 1, 0)

            def aggregate(k, slot, first=False):
                pe.wait_ge(s_select, k + 1)
                if first:
                    pe.wait_ge(s_message[slot], 64)
                else:
                    pe.wait_ge(s_message[slot], (k - slot) * 16 + 64)
                if not (first and slot < 2):
                    pe.wait_ge(s_added, k - 1)
                for j in range(SET):
                    ps = bank[(slot % 2) * 2 + j // 2][:, (j % 2) * C:(j % 2 + 1) * C]
                    last = nc.tensor.matmul(ps, select[:, slot % 2, j, :], message[:, slot, j, :], start=True, stop=True)
                last.then_inc(s_agg, 1)
            for slot in range(RING):
                aggregate(slot, slot, first=True)
            with pe.Fori(1, TSETS // RING) as m:
                for slot in range(RING):
                    aggregate(m * RING + slot, slot)

            pe.wait_ge(s_fin, 48)

            def f_transpose(g, slot, first=False):
                pe.wait_ge(s_fxn, g + 1)
                if not first:
                    pe.wait_ge(s_xt, g + (PAIRS - 1))
                transpose_pair(fxn[:, slot, :, :], bank[slot], s_xt_psum)

            def gate(g, slot, first=False):
                pe.wait_ge(s_xt, PAIRS + 1 + g)
                if not first:
                    pe.wait_ge(s_gate_read, g - 1)
                for u in range(2):
                    for k in range(KC):
                        last = nc.tensor.matmul(bank[2 + slot][:, u * EXPERTS:(u + 1) * EXPERTS],
                                                fxn_t[:, slot, k, u * P:(u + 1) * P], wg[:, k, :],
                                                start=(k == 0), stop=(k == KC - 1))
                last.then_inc(s_gate, 1)
            f_transpose(0, 0, first=True)
            f_transpose(1, 1, first=True)
            gate(0, 0, first=True)
            f_transpose(2, 0)
            gate(1, 1, first=True)
            with pe.Fori(1, PAIRS // 2) as m:
                f_transpose(m * 2 + 1, 1)
                gate(m * 2, 0)
                f_transpose(m * 2 + 2, 0)
                gate(m * 2 + 1, 1)
            gate(PAIRS - 1, 0)
            pe.wait_ge(s_route, 1)
            for i, matrix in ((0, tri), (2, ones_bf)):
                for half in range(2):
                    last = nc.tensor.matmul(bank[4 + i + half][:, 0:HB * EXPERTS], matrix[:, :],
                                            both_bf[:, half * HB:(half + 1) * HB, :].rearrange("p b e -> p (b e)"),
                                            start=True, stop=True)
            last.then_inc(s_route_psum, 1)

            pe.wait_ge(s_w1, 16)
            pe.wait_ge(s_w2, 48)
            pe.wait_ge(s_xtile_row, 16)

            w1_flat = w1[:, :, :, :].rearrange("p e k n -> p (e k n)")
            w2_flat = w2[:, :, :, :].rearrange("p e k n -> p (e k n)")

            def x_transpose(t, slot, first=False):
                pe.wait_ge(s_fx[slot], t * 8 + (16 - 8 * slot))
                if not first:
                    pe.wait_ge(s_fxt, t - 1)
                for k in range(KC):
                    last = nc.tensor.transpose(bank[slot][:, k * P:(k + 1) * P], fx[:, slot, k * P:(k + 1) * P], ident[:, :])
                last.then_inc(s_fxt_psum, 1)

            def up(t, slot, expert, first=False):
                pe.wait_ge(s_fxt, t + 1)
                if not first:
                    pe.wait_ge(s_hid, t - 1)
                for k in range(KC):
                    last = nc.tensor.matmul(bank[2 + slot][:, :], fx_t[:, slot, k, :],
                                            w1_flat[:, ds(expert + k * HID, HID)],
                                            start=(k == 0), stop=(k == KC - 1))
                last.then_inc(s_hid_psum, 1)

            def hid_transpose(t, slot, first=False):
                pe.wait_ge(s_hid, t + 1)
                if not first:
                    pe.wait_ge(s_hidt, t - 1)
                for k in range(KH):
                    last = nc.tensor.transpose(bank[4 + slot][:, k * P:(k + 1) * P], hid[:, slot, k * P:(k + 1) * P], ident[:, :])
                last.then_inc(s_hidt_psum, 1)

            def down(t, slot, expert, first=False):
                pe.wait_ge(s_hidt, t + 1)
                if not first:
                    pe.wait_ge(s_fy, t - 1)
                for k in range(KH):
                    last = nc.tensor.matmul(bank[6 + slot][:, 0:C], hid_t[:, slot, k, :],
                                            w2_flat[:, ds(expert + k * C, C)],
                                            start=(k == 0), stop=(k == KH - 1))
                last.then_inc(s_fy_psum, 1)

            def expert_pair(t, experts, first=False, last=False):
                up(t, 0, experts[0], first)
                up(t + 1, 1, experts[1], first)
                hid_transpose(t, 0, first)
                if not last:
                    x_transpose(t + 2, 0)
                    x_transpose(t + 3, 1)
                hid_transpose(t + 1, 1, first)
                down(t, 0, experts[0], first)
                down(t + 1, 1, experts[1], first)

            def experts_of(name, t):
                return load_offsets(pe, name, xtile_row[:, 0, :], t, 4, (EXPERTS - 1) * KC * HID)
            x_transpose(0, 0, first=True)
            x_transpose(1, 1, first=True)
            e = experts_of("expert_first_", 0)
            expert_pair(0, e[0:2], first=True)
            expert_pair(2, e[2:4])
            with pe.Fori(1, TX // 4 - 1) as m:
                e = experts_of("expert_", m * 4)
                expert_pair(m * 4, e[0:2])
                expert_pair(m * 4 + 2, e[2:4])
            e = experts_of("expert_last_", TX - 4)
            expert_pair(TX - 4, e[0:2])
            expert_pair(TX - 2, e[2:4], last=True)

        @block.vector
        def _(dve):
            steps = Steps(dve, s_dve)
            V = nc.vector
            dve.wait_ge(s_edges, 16 * N_EDGE_LOADS)
            V.tensor_single_scalar(record[:, :, 0], src_i[:, :], 7, ALU.logical_shift_right).then_inc(s_record, 1)
            steps.done(V.tensor_single_scalar(src_i[:, :], src_i[:, :], P - 1, ALU.bitwise_and))
            steps.settle()
            V.tensor_copy(record[:, :, 2].bitcast(F32), src_i[:, :]).then_inc(s_record, 1)
            dve.wait_ge(s_record, 4)
            steps.done(V.tensor_copy(block_bf[:, :], record[:, :, 0]))
            steps.settle()
            dve.wait_ge(s_const, 3)

            def one_hot(chunk, slot):
                V.tensor_tensor(onehot[:, slot, :, :],
                                block_bf[:, ds(chunk * CH, CH)].unsqueeze(1).to_broadcast([P, NB, CH]),
                                iota_b[:, :, :], ALU.is_equal).then_inc(s_hot, 1)
            for slot in range(2):
                one_hot(slot, slot)
            with dve.Fori(1, CHUNKS // 2) as m:
                for slot in range(2):
                    dve.wait_ge(s_hot_read, m * 2 + (slot - 1))
                    one_hot(m * 2 + slot, slot)
            dve.wait_ge(s_hot_read, CHUNKS)
            for half in range(2):
                steps.done(V.tensor_copy(totals[:, half * HB:(half + 1) * HB, :].rearrange("p b t -> p (b t)"),
                                         bank[half][:, 0:HB * CH]))
            steps.settle()
            steps.done(V.tensor_reduce(scan_a[:, :], totals[:, :, :], AX, ALU.add))
            steps.settle()
            steps.done(V.tensor_scalar(scan_i[:, :], scan_a[:, :], float(P - 1), None, ALU.add))
            steps.settle()
            steps.done(V.tensor_single_scalar(scan_i[:, :], scan_i[:, :], 7, ALU.logical_shift_right))
            steps.settle()
            steps.done(V.tensor_copy(scan_a[:, :], scan_i[:, :]))
            steps.settle()
            here, there, step = scan_a, scan_b, 1
            while step < NB:
                steps.done(V.tensor_copy(there[:, 0:step], here[:, 0:step]))
                steps.done(V.tensor_tensor(there[:, step:NB], here[:, step:NB], here[:, 0:NB - step], ALU.add))
                steps.settle()
                here, there, step = there, here, 2 * step
            steps.done(V.tensor_tensor(tile_cmp[:, :, :], iota_t[:, :].unsqueeze(2).to_broadcast([P, TPP, NB]),
                                       here[:, :].unsqueeze(1).to_broadcast([P, TPP, NB]), ALU.is_ge))
            steps.done(V.memset(base[:, 0:1, 0], 0.0))
            steps.done(V.tensor_scalar(base[:, 1:NB, 0], here[:, 0:NB - 1], float(P), None, ALU.mult))
            steps.settle()
            steps.done(V.tensor_reduce(tile_f[:, :], tile_cmp[:, :, :], AX, ALU.add))
            for j in range(1, CH):
                steps.done(V.tensor_tensor(base[:, :, j], base[:, :, j - 1], totals[:, :, j - 1], ALU.add))
                steps.settle()
            V.tensor_scalar(tile_i[:, :], tile_f[:, :], float(NB - 1), float(C), ALU.min, ALU.mult).then_inc(s_tile_out, 1)
            V.engine_nop().then_inc(s_base, 1)

            def position(chunk, slot, first=False):
                if not first:
                    dve.wait_ge(s_rank_next, chunk - 1)
                one_hot(chunk, slot)

            def extract(chunk, slot):
                for half in range(2):
                    dve.wait_ge(s_rank, chunk * 2 + (half + 1))
                    part = slice(half * HB, (half + 1) * HB)
                    V.tensor_tensor(picked[:, part, :].rearrange("p b t -> p (b t)"),
                                    onehot[:, slot, part, :].rearrange("p b t -> p (b t)"),
                                    bank[half][:, 0:HB * CH], ALU.mult).then_inc(s_rank_read, 1)
                dve.wait_ge(s_rank_read, chunk * 2 + 2)
                steps.done(V.tensor_reduce(pos_f[:, :], picked[:, :, :].rearrange("p b t -> p t b"), AX, ALU.add))
                steps.settle()
                steps.done(V.tensor_copy(pos_i[:, 0, :], pos_f[:, :]))
                steps.settle()
                steps.done(V.tensor_single_scalar(pos_i[:, 1, :], pos_i[:, 0, :], 7, ALU.logical_shift_right))
                steps.done(V.tensor_single_scalar(pos_i[:, 2, :], pos_i[:, 0, :], P - 1, ALU.bitwise_and))
                steps.settle()
                V.scalar_tensor_tensor(record[:, ds(chunk * CH, CH), 0], pos_i[:, 2, :], float(TT), pos_i[:, 1, :],
                                       ALU.mult, ALU.add).then_inc(s_pos, 1)
            position(0, 0, first=True)
            position(1, 1, first=True)
            extract(0, 0)
            with dve.Fori(1, CHUNKS // 2) as m:
                steps.enter(m - 1, 8)
                position(m * 2, 0)
                extract(m * 2 - 1, 1)
                position(m * 2 + 1, 1)
                extract(m * 2, 0)
                steps.leave(CHUNKS // 2 - 1)
            extract(CHUNKS - 1, 1)

            def all_row_stats():
                with dve.Fori(0, PAIRS) as g:
                    steps.enter(g, 6)
                    for u in range(2):
                        steps.done(V.bn_stats(stats[:, u, :], acc[:, ds(g * 2 + u, 1), :].rearrange("p a c -> p (a c)")))
                    steps.settle()
                    steps.done(V.memset(turn_mark[:, :], 0.0))
                    for u in range(2):
                        steps.done(V.bn_aggr(pair_stats[:, u, :], stats[:, u, :]))
                    steps.settle()
                    steps.done(V.tensor_copy(row_mean[:, ds(g * 2, 2), :], pair_stats[:, :, :]))
                    steps.leave(PAIRS)
                steps.settle()
                V.engine_nop().then_inc(s_var, 1)

            def invert_std(nth):
                dve.wait_ge(s_std, nth)
                steps.done(V.reciprocal(rstd[:, :], rstd[:, :]))
                steps.settle()
                steps.done(V.tensor_tensor(newton[:, :], rstd[:, :], rstd[:, :], ALU.mult))
                steps.settle()
                steps.done(V.scalar_tensor_tensor(newton[:, :], row_mean[:, :, 1], EPS, newton[:, :], ALU.add, ALU.mult))
                steps.settle()
                steps.done(V.tensor_scalar(newton[:, :], newton[:, :], -0.5, 1.5, ALU.mult, ALU.add))
                steps.settle()
                steps.done(V.tensor_tensor(rstd[:, :], rstd[:, :], newton[:, :], ALU.mult))
                steps.settle()

            def normalise(g, into, signal):
                for u in range(2):
                    b = g * 2 + u
                    last = V.tensor_scalar(into[:, u, :], acc[:, ds(b, 1), :].rearrange("p a c -> p (a c)"),
                                           row_mean[:, ds(b, 1), 0], rstd[:, ds(b, 1)], ALU.subtract, ALU.mult)
                last.then_inc(signal, 1)
            dve.wait_ge(s_x, 16 * len(XCUT))
            all_row_stats()
            dve.wait_ge(s_wload, 16 * 6)
            steps.done(V.tensor_tensor(bias_row[:, :], bias_in[:, 0, :], bias_in[:, 1, :], ALU.add))
            invert_std(1)

            def activate(g, slot):
                dve.wait_ge(s_proj_read, g * 2 + 2)
                for i, into in ((0, k_act), (1, q_out)):
                    V.scalar_tensor_tensor(into[:, slot, :, :].rearrange("p u c -> p (u c)"),
                                           exp_kq[:, i, :, :].rearrange("p u c -> p (u c)"), 1.0,
                                           relu_kq[:, i, :, :].rearrange("p u c -> p (u c)"),
                                           ALU.min, ALU.add).then_inc(s_kq, 1)
            normalise(0, xn, s_xn)
            dve.wait_ge(s_xt_psum, 1)
            normalise(1, xn, s_xn)
            activate(0, 0)
            dve.wait_ge(s_xt_psum, 2)
            normalise(2, xn, s_xn)
            activate(1, 1)
            with dve.Fori(1, PAIRS // 2) as m:
                for slot in range(2):
                    g = m * 2 + slot
                    dve.wait_ge(s_xt_psum, g + 1)
                    normalise(g + 1, xn, s_xn)
                    dve.wait_ge(s_ctx, g - 1)
                    dve.wait_ge(s_hq_out[slot], (g - slot) * 16)
                    activate(g, slot)
            dve.wait_ge(s_ctx, PAIRS - 2)
            dve.wait_ge(s_hq_out[0], (PAIRS - 1) * 16)
            activate(PAIRS - 1, 0)

            dve.wait_ge(s_ctx, PAIRS)
            for h in range(KC):
                steps.done(V.tensor_tensor(ctx_t[:, h, :], head_mask[:, :], bank[7][:, h * P:(h + 1) * P], ALU.mult))
            steps.done(V.tensor_copy(ksum[:, :], bank[7][:, C:2 * C]))
            steps.settle()
            V.engine_nop().then_inc(s_ctx_sb, 1)
            dve.wait_ge(s_mixw_psum, 1)
            V.tensor_copy(mix_w[:, :, :].rearrange("p k c -> p (k c)"), bank[5][:, :]).then_inc(s_mixw, 1)

            def scale_q(g, slot, first=False):
                if first:
                    dve.wait_ge(s_q_in[slot], 16)
                else:
                    dve.wait_ge(s_q_in[slot], g * 8 + (16 - 8 * slot))
                steps.done(V.tensor_tensor(k_act[:, 0, :, :], q_out[:, slot, :, :],
                                           ksum[:, :].unsqueeze(1).to_broadcast([P, 2, C]), ALU.mult))
                steps.settle()
                steps.done(V.tensor_reduce(den[:, 0, :], k_act[:, 0, :, :].rearrange("p u (h d) -> p (u h) d", d=HD), AX, ALU.add))
                steps.settle()
                steps.done(V.tensor_scalar(den[:, 1, :], den[:, 0, :], 1e-6, None, ALU.max))
                steps.settle()
                steps.done(V.reciprocal(den[:, 2, :], den[:, 1, :]))
                steps.settle()
                if not first or slot:
                    dve.wait_ge(s_qt_psum, g)
                V.tensor_tensor(xn[:, :, :].rearrange("p u (h d) -> p (u h) d", d=HD),
                                q_out[:, slot, :, :].rearrange("p u (h d) -> p (u h) d", d=HD),
                                den[:, 2, :].unsqueeze(2).to_broadcast([P, 2 * HEADS, HD]), ALU.mult).then_inc(s_qn, 1)

            def add_mix(g, slot):
                pair = acc[:, ds(g * 2, 2), :]
                steps.done(V.tensor_tensor(pair, pair, bias_row[:, :].unsqueeze(1).to_broadcast([P, 2, C]), ALU.add))
                steps.settle()
                dve.wait_ge(s_mix, g + 1)
                pair = pair.rearrange("p u c -> p (u c)")
                V.tensor_tensor(pair, pair, bank[3 + slot][:, :], ALU.add).then_inc(s_mix_added, 1)
            scale_q(0, 0, first=True)
            scale_q(1, 1, first=True)
            scale_q(2, 0)
            add_mix(0, 0)
            with dve.Fori(1, PAIRS // 2) as m:
                steps.enter(m - 1, 10)
                scale_q(m * 2 + 1, 1)
                add_mix(m * 2 - 1, 1)
                scale_q(m * 2 + 2, 0)
                add_mix(m * 2, 0)
                steps.leave(PAIRS // 2 - 1)
            add_mix(PAIRS - 2, 1)
            add_mix(PAIRS - 1, 0)

            dve.wait_ge(s_tile_row, 16)
            dve.wait_ge(s_mix_added, PAIRS)

            def select_tile(slot, j):
                return V.tensor_scalar(select[:, slot % 2, j, :], iota_n[:, :], gather_stage[:, slot, j, 1:2].bitcast(F32),
                                       gather_stage[:, slot, j, 2:3].bitcast(F32), ALU.is_equal, ALU.mult)

            acc_flat = acc[:, :, :].rearrange("p b c -> p (b c)")

            def add_set(slot, blocks):
                for j in range(SET):
                    to = acc_flat[:, ds(blocks[j], C)]
                    ps = bank[(slot % 2) * 2 + j // 2][:, (j % 2) * C:(j % 2 + 1) * C]
                    added = V.tensor_tensor(to, to, ps, ALU.add)
                    if j < SET - 1:
                        steps.done(added)
                        steps.settle()
                added.then_inc(s_added, 1)

            def set_turn(k, slot, k_list=None, add_slot=None, first=False):
                dve.wait_ge(s_list[slot], k_list)
                for j in range(SET):
                    made = select_tile(slot, j)
                made.then_inc(s_select, 1)
                if not first:
                    blocks = load_offsets(dve, f"block_{slot}_{int(isinstance(k, int))}_", tile_row, k * SET - SET, SET, (NB - 1) * C)
                    if slot != 1 or not isinstance(k, int):
                        dve.wait_ge(s_added, k - 1)
                    dve.wait_ge(s_agg, k)
                    add_set(add_slot, blocks)
            set_turn(0, 0, 16, first=True)
            for slot in range(1, RING):
                set_turn(slot, slot, 16, slot - 1)
            with dve.Fori(1, TSETS // RING) as m:
                steps.enter(m - 1, (SET - 1) * RING)
                for slot in range(RING):
                    set_turn(m * RING + slot, slot, m * 16 + 16, (slot - 1) % RING)
                steps.leave(TSETS // RING - 1)
            dve.wait_ge(s_added, TSETS - 1)
            dve.wait_ge(s_agg, TSETS)
            add_set(RING - 1, load_offsets(dve, "block_end_", tile_row, TT - SET, SET, (NB - 1) * C))

            dve.wait_ge(s_added, TSETS)
            all_row_stats()
            invert_std(2)

            def read_logits(g, slot):
                dve.wait_ge(s_gate, g + 1)
                V.tensor_copy(logits[:, ds(g * 2, 2), :].rearrange("p b e -> p (b e)"),
                              bank[2 + slot][:, 0:2 * EXPERTS]).then_inc(s_gate_read, 1)

            def norm_next(g, slot):
                dve.wait_ge(s_xt_psum, g + (PAIRS - 1))
                normalise(g, fxn[:, slot, :, :], s_fxn)
            normalise(0, fxn[:, 0, :, :], s_fxn)
            normalise(1, fxn[:, 1, :, :], s_fxn)
            with dve.Fori(1, PAIRS // 2) as m:
                for slot in range(2):
                    norm_next(m * 2 + slot, slot)
                    read_logits(m * 2 + (slot - 2), slot)
            norm_next(PAIRS - 1, 0)
            read_logits(PAIRS - 3, 0)
            read_logits(PAIRS - 2, 1)
            read_logits(PAIRS - 1, 0)
            dve.wait_ge(s_gate_read, PAIRS)
            dve.wait_ge(s_fin, 48)
            dve.wait_ge(s_const, 4)
            for i in range(2):
                steps.done(V.tensor_tensor(logits[:, :, :], logits[:, :, :],
                                           gate_b[:, i, :].unsqueeze(1).to_broadcast([P, NB, EXPERTS]), ALU.add))
                steps.settle()

            def over_experts(col):
                return small[:, col, :].unsqueeze(2).to_broadcast([P, NB, EXPERTS])

            def over_blocks(row):
                return row.unsqueeze(1).to_broadcast([P, NB, EXPERTS])

            def best(i):
                steps.done(V.tensor_reduce(small[:, i, :], logits[:, :, :], AX, ALU.max))
                steps.settle()
                steps.done(V.tensor_tensor(work[:, :, :], logits[:, :, :], over_experts(i), ALU.is_equal))
                steps.settle()
                steps.done(V.tensor_tensor(work[:, :, :], work[:, :, :], over_blocks(iota_e[:, 1, :]), ALU.mult))
                steps.settle()
                steps.done(V.tensor_reduce(small[:, 2 + i, :], work[:, :, :], AX, ALU.min))
                steps.settle()
                steps.done(V.tensor_tensor(pick[:, i, :, :], over_blocks(iota_e[:, 1, :]), over_experts(2 + i), ALU.is_equal))
                steps.settle()
            best(0)
            steps.done(V.tensor_scalar(work[:, :, :], pick[:, 0, :, :], 1.0, -1.0, ALU.subtract, ALU.mult))
            steps.settle()
            steps.done(V.tensor_tensor(logits[:, :, :], logits[:, :, :], work[:, :, :], ALU.mult))
            steps.settle()
            steps.done(V.scalar_tensor_tensor(logits[:, :, :], pick[:, 0, :, :], -3.0e38, logits[:, :, :], ALU.mult, ALU.add))
            steps.settle()
            best(1)
            steps.done(V.tensor_tensor(small[:, 4, :], small[:, 1, :], small[:, 0, :], ALU.subtract))
            steps.done(V.tensor_tensor(both_bf[:, :, :], pick[:, 0, :, :], pick[:, 1, :, :], ALU.add))
            steps.settle()
            V.engine_nop().then_inc(s_route, 1)
            dve.wait_ge(s_route, 2)
            steps.done(V.tensor_scalar(small[:, 5, :], top_w[:, 1, :], 1.0, None, ALU.add))
            steps.settle()
            steps.done(V.reciprocal(top_w[:, 0, :], small[:, 5, :]))
            steps.settle()
            steps.done(V.tensor_tensor(top_w[:, 1, :], top_w[:, 1, :], top_w[:, 0, :], ALU.mult))
            dve.wait_ge(s_route_psum, 1)
            for half in range(2):
                steps.done(V.tensor_copy(carry_a[:, half * HB:(half + 1) * HB, :].rearrange("p b e -> p (b e)"),
                                         bank[6 + half][:, 0:HB * EXPERTS]))
            steps.settle()
            here, there, step = carry_a, carry_b, 1
            while step < NB:
                steps.done(V.tensor_copy(there[:, 0:step, :], here[:, 0:step, :]))
                steps.done(V.tensor_tensor(there[:, step:NB, :], here[:, step:NB, :], here[:, 0:NB - step, :], ALU.add))
                steps.settle()
                here, there, step = there, here, 2 * step
            steps.done(V.tensor_scalar(ends_i[:, :], here[:, NB - 1, :], float(P - 1), None, ALU.add))
            steps.settle()
            steps.done(V.tensor_single_scalar(ends_i[:, :], ends_i[:, :], 7, ALU.logical_shift_right))
            steps.settle()
            steps.done(V.tensor_copy(ends[:, 0, :], ends_i[:, :]))
            steps.settle()
            for e in range(1, EXPERTS):
                steps.done(V.tensor_tensor(ends[:, 0, e:e + 1], ends[:, 0, e:e + 1], ends[:, 0, e - 1:e], ALU.add))
                steps.settle()
            steps.done(V.tensor_tensor(xcmp[:, :, :], iota_x[:, :].unsqueeze(2).to_broadcast([P, XPP, EXPERTS]),
                                       ends[:, 0, :].unsqueeze(1).to_broadcast([P, XPP, EXPERTS]), ALU.is_ge))
            steps.done(V.memset(ends[:, 1, 0:1], 0.0))
            steps.done(V.tensor_scalar(ends[:, 1, 1:EXPERTS], ends[:, 0, 0:EXPERTS - 1], float(P), None, ALU.mult))
            steps.settle()
            steps.done(V.tensor_reduce(xtile_f[:, :], xcmp[:, :, :], AX, ALU.add))
            steps.settle()
            for i, stride in ((0, KC * HID), (1, HID + C)):
                steps.done(V.tensor_scalar(xtile_i[:, i, :], xtile_f[:, :], float(EXPERTS - 1), float(stride), ALU.min, ALU.mult))
            for half in range(2):
                steps.done(V.tensor_copy(rank[:, half * HB:(half + 1) * HB, :].rearrange("p b e -> p (b e)"),
                                         bank[4 + half][:, 0:HB * EXPERTS]))
            steps.settle()
            steps.done(V.tensor_tensor(rank[:, 1:NB, :], rank[:, 1:NB, :], here[:, 0:NB - 1, :], ALU.add))
            steps.settle()
            steps.done(V.tensor_tensor(rank[:, :, :], rank[:, :, :], over_blocks(ends[:, 1, :]), ALU.add))
            steps.settle()
            for i in range(2):
                steps.done(V.tensor_tensor(work[:, :, :], rank[:, :, :], pick[:, i, :, :], ALU.mult))
                steps.settle()
                steps.done(V.tensor_reduce(small[:, i, :], work[:, :, :], AX, ALU.add))
                steps.settle()
                steps.done(V.tensor_copy(token_pos[:, :, i], small[:, i, :]))
            steps.settle()
            V.engine_nop().then_inc(s_route_done, 1)

            dve.wait_ge(s_xt_psum, 2 * PAIRS)
            normalise(0, fxn[:, 0, :, :], s_fxn)
            normalise(1, fxn[:, 1, :, :], s_fxn)
            with dve.Fori(1, PAIRS // 2) as m:
                for slot in range(2):
                    dve.wait_ge(s_sent[slot], m * 64)
                    normalise(m * 2 + slot, fxn[:, slot, :, :], s_fxn)
            dve.wait_ge(s_sent[0], PAIRS // 2 * 64)
            normalise(PAIRS - 1, fxn[:, 0, :, :], s_fxn)

            dve.wait_ge(s_w2, 48)
            dve.wait_ge(s_xtile_row, 16)

            b12_flat = b12[:, :, :].rearrange("p e n -> p (e n)")

            def add_b1(t, slot, expert, first=False):
                dve.wait_ge(s_hid_psum, t + 1)
                if not first:
                    dve.wait_ge(s_hidt_psum, t - 1)
                V.tensor_tensor(hid[:, slot, :], bank[2 + slot][:, :],
                                b12_flat[:, ds(expert, HID)], ALU.add).then_inc(s_hid, 1)

            def add_b2(t, slot, expert, first=False):
                dve.wait_ge(s_fy_psum, t + 1)
                if not first:
                    dve.wait_ge(s_fy_out[slot], (t - slot) * 8)
                V.tensor_tensor(fy[:, slot, :], bank[6 + slot][:, 0:C],
                                b12_flat[:, ds(expert + HID, C)], ALU.add).then_inc(s_fy, 1)

            def expert_pair(t, experts, first=False):
                add_b1(t, 0, experts[0], first)
                add_b1(t + 1, 1, experts[1], first)
                add_b2(t, 0, experts[0], first)
                add_b2(t + 1, 1, experts[1], first)

            def experts_of(name, t):
                return load_offsets(dve, name, xtile_row[:, 1, :], t, 4, (EXPERTS - 1) * (HID + C))
            e = experts_of("expert_first_", 0)
            expert_pair(0, e[0:2], first=True)
            expert_pair(2, e[2:4])
            with dve.Fori(1, TX // 4) as m:
                e = experts_of("expert_", m * 4)
                expert_pair(m * 4, e[0:2])
                expert_pair(m * 4 + 2, e[2:4])

            def combine(g, slot, first=False):
                dve.wait_ge(s_back[slot], 64 if first else (g - slot) * 32 + 64)
                if not first:
                    dve.wait_ge(s_out[slot], (g - slot) * 8)
                for u in range(2):
                    b = g * 2 + u
                    steps.done(V.scalar_tensor_tensor(result[:, slot, u, :], back_1[:, slot, u, :], top_w[:, 0, ds(b, 1)],
                                                      acc[:, ds(b, 1), :].rearrange("p a c -> p (a c)"), ALU.mult, ALU.add))
                steps.settle()
                for u in range(2):
                    b = g * 2 + u
                    last = V.scalar_tensor_tensor(result[:, slot, u, :], back_2[:, slot, u, :], top_w[:, 1, ds(b, 1)],
                                                  result[:, slot, u, :], ALU.mult, ALU.add)
                last.then_inc(s_sum, 1)
            combine(0, 0, first=True)
            combine(1, 1, first=True)
            with dve.Fori(1, PAIRS // 2) as m:
                steps.enter(m - 1, 4)
                for slot in range(2):
                    combine(m * 2 + slot, slot)
                steps.leave(PAIRS // 2 - 1)
            combine(PAIRS - 1, 0)


_INS = ["x", "src", "dst", "edge_weight", "L0_gnn_W", "L0_gnn_b", "L0_mix_Wq", "L0_mix_Wkv", "L0_mix_Wproj",
        "L0_mix_bproj", "L0_ffn_Wg", "L0_ffn_bg", "L0_ffn_bias", "L0_ffn_W1", "L0_ffn_b1", "L0_ffn_W2", "L0_ffn_b2"]


def kernel(**inputs):
    import numpy as np
    import concourse.bacc as bacc
    from concourse import mybir
    from concourse.bass_utils import run_bass_kernel_spmd

    nc = bacc.Bacc("TRN2", target_bir_lowering=False, num_devices=1)
    arrays, args = {}, []
    for name in _INS:
        a = np.ascontiguousarray(inputs[name])
        arrays[f"in_{name}"] = a
        args.append(nc.dram_tensor(f"in_{name}", a.shape, mybir.dt.from_np(a.dtype), kind="ExternalInput").ap())
    out = nc.dram_tensor("out", inputs["x"].shape, mybir.dt.float32, kind="ExternalOutput").ap()
    gps_layer(nc, *args, out)
    return run_bass_kernel_spmd(nc, [arrays], core_ids=[0]).results[0]["out"]
```

```python
from contextlib import ExitStack

from concourse.bass import DynSlice


class Steps:

    def __init__(self, eng, sem):
        self.eng, self.sem, self.base, self.count = eng, sem, 0, 0

    def done(self, instruction):
        instruction.then_inc(self.sem, 1)
        self.count += 1

    def settle(self):
        self.eng.wait_ge(self.sem, self.base + self.count)

    def enter(self, turn, per_turn):
        self.before, self.per_turn = self.count, per_turn
        self.base, self.count = turn * per_turn + self.before, 0

    def leave(self, turns):
        assert self.count == self.per_turn, (self.count, self.per_turn)
        self.base, self.count = 0, self.before + turns * self.per_turn


def load_offsets(eng, name, row, first, count, top):
    registers = [eng.alloc_register(f"{name}{i}") for i in range(count)]
    eng.load(registers, row[0:1, first:first + count] if isinstance(first, int) else row[0:1, DynSlice(first, count)])
    return [eng.snap(r, min_val=0, max_val=top) for r in registers]


def gps_layer(nc, x, src, dst, edge_weight, gnn_W, gnn_b, mix_Wq, mix_Wkv, mix_Wproj, mix_bproj,
              ffn_Wg, ffn_bg, ffn_bias, ffn_W1, ffn_b1, ffn_W2, ffn_b2, out):
    import concourse.bass as bass
    from concourse import mybir

    F32, BF16, I32 = mybir.dt.float32, mybir.dt.bfloat16, mybir.dt.int32
    ALU, ACT, AX = mybir.AluOpType, mybir.ActivationFunctionType, mybir.AxisListType.X
    ds = bass.ds
    Offset = bass.IndirectOffsetOnAxis

    P = 128
    N, C = x.shape
    E = src.shape[0]
    KC = C // P
    NB = -(-N // P)
    LAST = N - (NB - 1) * P
    PAIRS = NB // 2
    HEADS, HD = 8, 32
    EXPERTS, _, HID = ffn_W1.shape
    KH = HID // P
    EPS = 1e-5
    CH = 8
    HB = NB // 2
    ET = -(-E // (P * 2 * CH)) * 2 * CH
    CHUNKS = ET // CH
    SET, RING = 4, 4
    TT = -(-((ET * P + NB * (P - 1)) // P) // (SET * RING)) * SET * RING
    TSETS = TT // SET
    TPP = -(-TT // P)
    TURN = 7
    TB = 2 * TURN
    TURNS = PAIRS // TURN
    TURNS_1 = TURNS * 3 // 7
    HALF_PAIRS = [TURNS_1 * TURN, (TURNS - TURNS_1) * TURN]
    HALF_BEGIN = [0, HALF_PAIRS[0]]
    NBX = 2 * max(HALF_PAIRS)
    TX = [-(-((4 * n * P + EXPERTS * (P - 1)) // P) // 4) * 4 for n in HALF_PAIRS]
    TXS = sum(TX)
    XPP = 2
    G1, GROUPS = TX[0] // 4, TXS // 4
    SPARE = 2
    BACK = HALF_PAIRS[0] - SPARE
    assert PAIRS % TURN == 0 and max(TX) <= P * XPP and G1 + 2 + BACK < GROUPS and HALF_PAIRS[1] % 2 == 0
    assert KC * HID == KH * C and NB % 4 == 2 and HB * CH <= 512 and KC == 2 and 4 * C == 1024 and HID == 512

    h_table = nc.dram_tensor("h_table", (NB * P, C), F32, kind="Internal").ap()
    q_dram = nc.dram_tensor("q_dram", (PAIRS, P, 2 * C), F32, kind="Internal").ap()
    edge_list = nc.dram_tensor("edge_list", (P * TT, 3), I32, kind="Internal").ap()
    tile_dram = nc.dram_tensor("tile_dram", (P * TPP,), I32, kind="Internal").ap()
    xtile_dram = nc.dram_tensor("xtile_dram", (2, 2, P * XPP), I32, kind="Internal").ap()
    x_sorted = [nc.dram_tensor(f"x_sorted{i}", (TX[i] * P, C), F32, kind="Internal").ap() for i in range(2)]
    y_sorted = [nc.dram_tensor(f"y_sorted{i}", (TX[i] * P, C), F32, kind="Internal").ap() for i in range(2)]
    acc_dram = nc.dram_tensor("acc_dram", (P, 2 * SPARE * C), F32, kind="Internal").ap()

    with ExitStack() as whole:
        def sem(name):
            return whole.enter_context(nc.semaphore(name))

        def sb(name, shape, dtype, scope=whole):
            return scope.enter_context(nc.sbuf_tensor(name, shape, dtype))

        acc = sb("acc", [P, NB, C], F32)
        ident = sb("ident", [P, P], F32)
        tri = sb("tri", [P, P], BF16)
        ones_bf = sb("ones_bf", [P, P], BF16)
        row_mean = sb("row_mean", [P, NB, 2], F32)
        rstd = sb("rstd", [P, NB], F32)
        newton = sb("newton", [P, NB], F32)
        stats = sb("stats", [P, TB, 6], F32)
        turn_stats = sb("turn_stats", [P, TB, 2], F32)
        turn_mark = sb("turn_mark", [P, 1], F32)
        eps_col = sb("eps_col", [P, 1], F32)

        early = ExitStack()
        iota_n = sb("iota_n", [P, P], F32, early)
        tri_rest = sb("tri_rest", [P, P], BF16, early)
        record = sb("record", [P, ET, 4], I32, early)
        block_bf = sb("block_bf", [P, ET], BF16, early)
        onehot = sb("onehot", [P, 2, NB, CH], BF16, early)
        totals = sb("totals", [P, NB, CH], F32, early)
        picked = totals
        base = sb("base", [P, NB, CH], F32, early)
        scan_a = sb("scan_a", [P, NB], F32, early)
        scan_b = sb("scan_b", [P, NB], F32, early)
        scan_i = sb("scan_i", [P, NB], I32, early)
        pos_f = sb("pos_f", [P, CH], F32, early)
        pos_i = sb("pos_i", [P, 3, CH], I32, early)
        iota_b = sb("iota_b", [P, NB, CH], BF16, early)
        iota_t = sb("iota_t", [P, TPP], F32, early)
        tile_f = sb("tile_f", [P, TPP], F32, early)
        tile_i = sb("tile_i", [P, TPP], I32, early)
        tile_row = sb("tile_row", [1, P * TPP], I32, early)
        scatter_stage = sb("scatter_stage", [P, 2, CH, 4], I32, early)
        zeros = sb("zeros", [P, 4 * C], F32, early)
        w_cat = sb("w_cat", [P, KC, 4 * C], F32, early)
        wp_t = sb("wp_t", [P, KC, C], F32, early)
        head_mask = sb("head_mask", [P, P], F32, early)
        row_ok = sb("row_ok", [P, 2, P], F32, early)
        bias_row = sb("bias_row", [P, C], F32, early)
        ctx_t = sb("ctx_t", [P, KC, P], F32, early)
        ksum = sb("ksum", [P, C], F32, early)
        mix_w = sb("mix_w", [P, KC, C], F32, early)
        xn = sb("xn", [P, 2, C], F32, early)
        inputs = ExitStack()
        src_i = sb("src_i", [P, ET], I32, inputs)
        dst_i = sb("dst_i", [P, ET], I32, inputs)
        w_in = sb("w_in", [P, ET], I32, inputs)
        tile_cmp = sb("tile_cmp", [P, TPP, NB], F32, inputs)
        w_nat = sb("w_nat", [P, 8, C], F32, inputs)
        bias_in = sb("bias_in", [P, 2, C], F32, inputs)
        inputs.close()
        attention = ExitStack()
        h_out = sb("h_out", [P, 2, 2, C], F32, attention)
        q_out = sb("q_out", [P, 2, 2, C], F32, attention)
        k_act = sb("k_act", [P, 2, 2, C], F32, attention)
        v_sb = sb("v_sb", [P, 2, 2, C], F32, attention)
        exp_kq = sb("exp_kq", [P, 2, 2, C], F32, attention)
        relu_kq = sb("relu_kq", [P, 2, 2, C], F32, attention)
        xn_t = sb("xn_t", [P, 2, KC, 2 * P], F32, attention)
        den = sb("den", [P, 4, 2 * HEADS], F32, attention)
        attention.close()
        gather_stage = sb("gather_stage", [P, RING, SET, 3], I32, early)
        message = sb("message", [P, RING, SET, C], F32, early)
        select = sb("select", [P, 2, SET, P], F32, early)
        early.close()

        w1 = sb("w1", [P, EXPERTS, KC, HID], F32)
        fx = sb("fx", [P, 2, C], F32)
        fx_t = sb("fx_t", [P, 2, KC, P], F32)
        hid = sb("hid", [P, 2, HID], F32)
        hid_t = sb("hid_t", [P, 2, KH, P], F32)
        fy = sb("fy", [P, 2, C], F32)
        wg = sb("wg", [P, KC, EXPERTS], F32)
        gate_b = sb("gate_b", [P, 2, EXPERTS], F32)
        top_w = sb("top_w", [P, 2, NB], F32)
        token_pos = sb("token_pos", [P, NB, 2], I32)
        pos_stage = sb("pos_stage", [P, 2, 2, 2], I32)
        xtile_row = sb("xtile_row", [1, 2, TXS], I32)
        w2 = sb("w2", [P, EXPERTS, KH, C], F32)
        route = ExitStack()
        logits = sb("logits", [P, NBX, EXPERTS], F32, route)
        pick = sb("pick", [P, 2, NBX, EXPERTS], F32, route)
        both_bf = sb("both_bf", [P, NBX, EXPERTS], BF16, route)
        work = sb("work", [P, NBX, EXPERTS], F32, route)
        rank = sb("rank", [P, NBX, EXPERTS], F32, route)
        carry_a = sb("carry_a", [P, NBX, EXPERTS], F32, route)
        carry_b = sb("carry_b", [P, NBX, EXPERTS], F32, route)
        small = sb("small", [P, 6, NBX], F32, route)
        iota_e = sb("iota_e", [P, 2, EXPERTS], F32, route)
        ends = sb("ends", [P, 4, EXPERTS], F32, route)
        ends_i = sb("ends_i", [P, EXPERTS], I32, route)
        iota_x = sb("iota_x", [P, XPP], F32, route)
        xcmp = sb("xcmp", [P, XPP, EXPERTS], F32, route)
        xtile_f = sb("xtile_f", [P, XPP], F32, route)
        xtile_i = sb("xtile_i", [P, 2, XPP], I32, route)
        fxn = sb("fxn", [P, 2, 2, C], F32, route)
        fxn_t = sb("fxn_t", [P, 2, KC, 2 * P], F32, route)
        route.close()
        b12 = sb("b12", [P, EXPERTS, HID + C], F32)

        bank = [whole.enter_context(nc.psum_tensor(f"bank{i}", [P, 512], F32)) for i in range(8)]

        s_const = sem("s_const")
        s_passed = sem("s_passed")
        s_pool = sem("s_pool")
        s_dve = sem("s_dve")
        s_act = sem("s_act")
        s_edges = sem("s_edges")
        s_x = sem("s_x")
        s_wload = sem("s_wload")
        s_zeroed = sem("s_zeroed")
        s_record = sem("s_record")
        s_hot = sem("s_hot")
        s_hot_read = sem("s_hot_read")
        s_base = sem("s_base")
        s_rank = sem("s_rank")
        s_rank_read = sem("s_rank_read")
        s_rank_next = sem("s_rank_next")
        s_pos = sem("s_pos")
        s_staged = [sem(f"s_staged{i}") for i in range(2)]
        s_scattered = [sem(f"s_scattered{i}") for i in range(2)]
        s_tile_out = sem("s_tile_out")
        s_tile_dram = sem("s_tile_dram")
        s_tile_row = sem("s_tile_row")
        s_wt_psum = sem("s_wt_psum")
        s_wt = sem("s_wt")
        s_var = sem("s_var")
        s_std = sem("s_std")
        s_xn = sem("s_xn")
        s_xt_psum = sem("s_xt_psum")
        s_xt = sem("s_xt")
        s_proj = sem("s_proj")
        s_proj_read = sem("s_proj_read")
        s_kq = sem("s_kq")
        s_hq_out = [sem(f"s_hq_out{i}") for i in range(2)]
        s_ctx = sem("s_ctx")
        s_ctx_sb = sem("s_ctx_sb")
        s_mixw_psum = sem("s_mixw_psum")
        s_mixw = sem("s_mixw")
        s_q_in = [sem(f"s_q_in{i}") for i in range(2)]
        s_qn = sem("s_qn")
        s_qt_psum = sem("s_qt_psum")
        s_qt = sem("s_qt")
        s_mix = sem("s_mix")
        s_mix_added = sem("s_mix_added")
        s_list = [sem(f"s_list{i}") for i in range(RING)]
        s_message = [sem(f"s_message{i}") for i in range(RING)]
        s_select = sem("s_select")
        s_agg = sem("s_agg")
        s_added = sem("s_added")
        s_w1 = sem("s_w1")
        s_w2 = sem("s_w2")
        s_b12 = sem("s_b12")
        s_fin = sem("s_fin")
        s_gate = sem("s_gate")
        s_gate_read = sem("s_gate_read")
        s_route = sem("s_route")
        s_route_psum = sem("s_route_psum")
        s_route_done = sem("s_route_done")
        s_xtile_dram = sem("s_xtile_dram")
        s_xtile_row = [sem(f"s_xtile_row{i}") for i in range(2)]
        s_fxn = sem("s_fxn")
        s_spill = sem("s_spill")
        s_reload = sem("s_reload")
        s_sent = [[sem(f"s_sent{h}_{i}") for i in range(2)] for h in range(2)]
        s_fx = [sem(f"s_fx{i}") for i in range(2)]
        s_fxt_psum = sem("s_fxt_psum")
        s_fxt = sem("s_fxt")
        s_hid_psum = sem("s_hid_psum")
        s_hid = sem("s_hid")
        s_hidt_psum = sem("s_hidt_psum")
        s_hidt = sem("s_hidt")
        s_fy_psum = sem("s_fy_psum")
        s_fy = sem("s_fy")
        s_fy_out = [sem(f"s_fy_out{i}") for i in range(2)]
        s_back_1 = sem("s_back_1")
        s_sum_1 = sem("s_sum_1")
        s_out_1 = sem("s_out_1")
        s_back = [sem(f"s_back{i}") for i in range(2)]
        s_sum = sem("s_sum")
        s_out = [sem(f"s_out{i}") for i in range(2)]

        spare = acc[:, 0:2 * SPARE, :]
        moving = [hid[:, :, :].rearrange("p s (u c) -> p s u c", c=C), spare.rearrange("p (s u) c -> p s u c", u=2)]
        back_1 = w1[:, 0:2, :, :].rearrange("p s u n -> p s (u n)")[:, :, 0:2 * C].rearrange("p s (u c) -> p s u c", u=2)
        back_2 = w1[:, 2:4, :, :].rearrange("p s u n -> p s (u n)")[:, :, 0:2 * C].rearrange("p s (u c) -> p s u c", u=2)
        result = w1[:, 4:6, :, :].rearrange("p s u n -> p s (u n)")[:, :, 0:2 * C].rearrange("p s (u c) -> p s u c", u=2)

        block = whole.enter_context(nc.Block())
        full = E // ET
        wide = full // 16 * 16
        edge_parts = [(0, wide), (wide, full)] if full > wide else [(0, wide)]
        edge_parts = [(a, b) for a, b in edge_parts if b > a]
        rest = E - full * ET
        x_full = x[0:(NB - 1) * P, :].rearrange("(b p) c -> p b c", p=P)

        XCUT = [0, NB // 4, NB // 2, NB - 1]
        N_EDGE_LOADS = 3 * (len(edge_parts) + (1 if rest else 0))

        @block.sync
        def _(sp):
            sp.wait_ge(s_const, 1)
            for a, b in edge_parts:
                for tile, arr in ((src_i, src), (dst_i, dst), (w_in, edge_weight.bitcast(I32))):
                    sp.dma_start(tile[a:b, :], arr[a * ET:b * ET].rearrange("(p t) -> p t", t=ET)).then_inc(s_edges, 16)
            if rest:
                for tile, arr in ((src_i, src), (dst_i, dst), (w_in, edge_weight.bitcast(I32))):
                    sp.dma_start(tile[full:full + 1, 0:rest], arr[full * ET:E].rearrange("(a n) -> a n", a=1)).then_inc(s_edges, 16)
            sp.wait_ge(s_const, 2)
            for a, b in zip(XCUT[:-1], XCUT[1:]):
                sp.dma_start(acc[:, a:b, :], x_full[:, a:b, :]).then_inc(s_x, 16)
            sp.dma_start(acc[0:LAST, NB - 1, :], x[(NB - 1) * P:N, :]).then_inc(s_x, 16)
            sp.dma_start(w_nat[:, 0:2, :], mix_Wq.rearrange("(a p) c -> p a c", p=P)).then_inc(s_wload, 16)
            sp.dma_start(w_nat[:, 2:6, :], mix_Wkv.rearrange("(a p) c -> p a c", p=P)).then_inc(s_wload, 16)
            sp.dma_start(w_nat[:, 6:8, :], mix_Wproj.rearrange("(a p) c -> p a c", p=P)).then_inc(s_wload, 16)
            sp.dma_start(w_cat[:, :, 0:C], gnn_W.rearrange("(k p) n -> p k n", p=P)).then_inc(s_wload, 16)
            sp.dma_start(bias_in[:, 0, :], gnn_b.partition_broadcast(P)).then_inc(s_wload, 16)
            sp.dma_start(bias_in[:, 1, :], mix_bproj.partition_broadcast(P)).then_inc(s_wload, 16)
            lrow = edge_list.rearrange("(p t) c -> p (t c)", p=P)
            zcols = 4 * C
            nz = 0
            for a in range(0, 3 * TT, zcols):
                b = min(a + zcols, 3 * TT)
                sp.dma_start(lrow[:, a:b], zeros[:, 0:b - a].bitcast(I32)).then_inc(s_zeroed, 16)
                nz += 1
            for half in range(2):
                sp.dma_start(x_sorted[half].rearrange("(p t) c -> p t c", p=P),
                             zeros[:, 0:C].unsqueeze(1).to_broadcast([P, TX[half], C])).then_inc(s_zeroed, 16)
            sp.wait_ge(s_tile_out, 1)
            sp.dma_start(tile_dram.rearrange("(p t) -> p t", p=P), tile_i[:, :]).then_inc(s_tile_dram, 16)
            sp.wait_ge(s_tile_dram, 16)
            sp.dma_start(tile_row[:, :], tile_dram.rearrange("(a n) -> a n", a=1)).then_inc(s_tile_row, 16)
            sp.wait_ge(s_record, 4)

            def stage(first_tile, slot):
                sp.dma_start(scatter_stage[:, slot, :, :], record[:, ds(first_tile, CH), :]).then_inc(s_staged[slot], 16)
            for slot in range(2):
                sp.wait_ge(s_pos, slot + 1)
                stage(slot * CH, slot)
            with sp.Fori(1, CHUNKS // 2) as m:
                for slot in range(2):
                    first_tile = sp.snap(m * (2 * CH) + slot * CH)
                    sp.wait_ge(s_pos, m * 2 + (slot + 1))
                    sp.sem_inc(s_passed, 1)
                    sp.wait_ge(s_scattered[slot], m * (16 * CH))
                    stage(first_tile, slot)

            for slot in range(2):
                sp.wait_ge(s_scattered[slot], 16 * CH * (CHUNKS // 2))
            sp.wait_ge(s_mix_added, PAIRS)
            lset = edge_list.rearrange("(p t) c -> p t c", p=P)

            def stage_list(first_tile, slot):
                sp.dma_start(gather_stage[:, slot, :, :], lset[:, ds(first_tile, SET), :]).then_inc(s_list[slot], 16)
            for slot in range(RING):
                stage_list(slot * SET, slot)
            with sp.Fori(1, TSETS // RING) as m:
                for slot in range(RING):
                    first_tile = sp.snap((m * RING + slot) * SET)
                    sp.wait_ge(s_agg, m * RING + (slot - RING + 1))
                    stage_list(first_tile, slot)

            sp.wait_ge(s_added, TSETS)
            sp.dma_start(wg[:, :, :], ffn_Wg.rearrange("(k p) n -> p k n", p=P)).then_inc(s_fin, 16)
            sp.dma_start(gate_b[:, 0, :], ffn_bg.partition_broadcast(P)).then_inc(s_fin, 16)
            sp.dma_start(gate_b[:, 1, :], ffn_bias.partition_broadcast(P)).then_inc(s_fin, 16)
            sp.dma_start(acc_dram, spare.rearrange("p b c -> p (b c)")).then_inc(s_spill, 16)
            sp.dma_start(w1[:, :, :, :], ffn_W1.rearrange("e (k p) n -> p e k n", p=P)).then_inc(s_w1, 16)
            sp.dma_start(w2[:, :, :, :], ffn_W2.rearrange("e (k p) n -> p e k n", p=P)).then_inc(s_w2, 16)
            for half in range(2):
                sp.wait_ge(s_route_done, half + 1)
                sp.dma_start(xtile_dram[half].rearrange("a (p t) -> p a t", p=P), xtile_i[:, :, :]).then_inc(s_xtile_dram, 16)
                sp.wait_ge(s_xtile_dram, half * 16 + 16)
                sp.dma_start(xtile_row[:, :, half * TX[0]:half * TX[0] + TX[half]],
                             xtile_dram[half, :, 0:TX[half]].unsqueeze(0)).then_inc(s_xtile_row[half], 16)
            sp.dma_start(b12[:, :, 0:HID], ffn_b1.partition_broadcast(P)).then_inc(s_b12, 16)
            sp.dma_start(b12[:, :, HID:HID + C], ffn_b2.partition_broadcast(P)).then_inc(s_b12, 16)

            x_tiles = [x_sorted[half].rearrange("(t p) c -> t p c", p=P) for half in range(2)]

            def load_x(half, t, slot):
                sp.dma_start(fx[:, slot, :], x_tiles[half][ds(t, 1), :, :].rearrange("a p c -> p (a c)")).then_inc(s_fx[slot], 16)

            def all_sent(half):
                for slot in range(2):
                    sp.wait_ge(s_sent[half][slot], (HALF_PAIRS[half] + 1 - slot) // 2 * 64)
            all_sent(0)
            for slot in range(2):
                load_x(0, slot, slot)
            with sp.Fori(1, TX[0] // 2) as m:
                for slot in range(2):
                    tile = sp.snap(m * 2 + slot)
                    sp.wait_ge(s_fxt_psum, m * 2 + (slot - 1))
                    load_x(0, tile, slot)
            all_sent(1)
            with sp.Fori(TX[0] // 2, TXS // 2) as m:
                for slot in range(2):
                    tile = sp.snap(m * 2 + (slot - TX[0]))
                    sp.wait_ge(s_fxt_psum, m * 2 + (slot - 1))
                    load_x(1, tile, slot)
            sp.wait_ge(s_out_1, 16 * BACK)
            sp.dma_start(spare.rearrange("p b c -> p (b c)"), acc_dram).then_inc(s_reload, 16)

        @block.gpsimd
        def _(pool):
            steps = Steps(pool, s_pool)
            pool.memset(src_i[:, :], NB * P - 1)
            pool.memset(dst_i[:, :], 0)
            pool.memset(w_in[:, :], 0).then_inc(s_const, 1)
            pool.memset(acc[:, NB - 1, :], 0.0)
            pool.memset(zeros[:, :], 0.0).then_inc(s_const, 1)
            pool.iota(iota_b[:, :, :], [[1, NB], [0, CH]], base=0, channel_multiplier=0, allow_small_or_imprecise_dtypes=True)
            pool.iota(iota_t[:, :], [[1, TPP]], base=0, channel_multiplier=TPP, allow_small_or_imprecise_dtypes=True)
            pool.iota(iota_n[:, :], [[1, P]], base=0, channel_multiplier=0, allow_small_or_imprecise_dtypes=True)
            pool.memset(eps_col[:, :], EPS)
            steps.done(pool.memset(ones_bf[:, :], 1.0))
            steps.done(pool.memset(ident[:, :], 0.0))
            steps.done(pool.memset(head_mask[:, :], 1.0))
            steps.done(pool.memset(row_ok[:, :, :], 1.0))
            steps.settle()
            pool.affine_select(out=tri[:, :], in_=ones_bf[:, :], pattern=[[1, P]], compare_op=ALU.is_gt,
                               fill=0.0, base=0, channel_multiplier=-1)
            pool.affine_select(out=tri_rest[:, :], in_=ones_bf[:, :], pattern=[[-1, P]], compare_op=ALU.is_ge,
                               fill=0.0, base=0, channel_multiplier=1)
            pool.affine_select(out=row_ok[:, 1, :], in_=row_ok[:, 1, :], pattern=[[0, P]], compare_op=ALU.is_ge,
                               fill=0.0, base=LAST - 1, channel_multiplier=-1)
            heads = head_mask[:, :].rearrange("p (h d) -> p h d", d=HD)
            steps.done(pool.affine_select(out=heads, in_=heads, pattern=[[-HD, P // HD], [0, HD]],
                                          compare_op=ALU.is_ge, fill=0.0, base=0, channel_multiplier=1))
            steps.settle()
            pool.affine_select(out=heads, in_=heads, pattern=[[HD, P // HD], [0, HD]],
                               compare_op=ALU.is_ge, fill=0.0, base=HD - 1, channel_multiplier=-1)
            pool.affine_select(out=ident[:, :], in_=ident[:, :], pattern=[[-1, P]], compare_op=ALU.not_equal,
                               fill=1.0, base=0, channel_multiplier=1).then_inc(s_const, 1)
            pool.wait_ge(s_edges, 16 * N_EDGE_LOADS)
            pool.tensor_copy(record[:, :, 1], dst_i[:, :]).then_inc(s_record, 1)
            pool.tensor_copy(record[:, :, 3], w_in[:, :]).then_inc(s_record, 1)

            n_zero = -(-3 * TT // (4 * C)) + 2
            def pass_gate():
                pool.sem_inc(s_passed, 1)
            pool.wait_ge(s_zeroed, 16 * n_zero)
            with pool.Fori(0, CHUNKS // 2) as m:
                for slot in range(2):
                    pool.wait_ge(s_staged[slot], m * 16 + 16)
                    pass_gate()
                    for j in range(CH):
                        pool.indirect_dma_start(
                            out=edge_list, out_offset=Offset(ap=scatter_stage[:, slot, j, 0:1], axis=0),
                            in_=scatter_stage[:, slot, j, 1:4], in_offset=None).then_inc(s_scattered[slot], 16)

            pool.wait_ge(s_hq_out[0], 32 * (PAIRS // 2 + 1))
            pool.wait_ge(s_hq_out[1], 32 * (PAIRS // 2))

            def gather_set(slot):
                pass_gate()
                for j in range(SET):
                    pool.indirect_dma_start(
                        out=message[:, slot, j, :], out_offset=None, in_=h_table,
                        in_offset=Offset(ap=gather_stage[:, slot, j, 0:1], axis=0)).then_inc(s_message[slot], 16)
            for slot in range(RING):
                pool.wait_ge(s_list[slot], 16)
                gather_set(slot)
            with pool.Fori(1, TSETS // RING) as m:
                for slot in range(RING):
                    pool.wait_ge(s_list[slot], m * 16 + 16)
                    gather_set(slot)

            pool.wait_ge(s_added, TSETS)
            pool.iota(iota_e[:, 0, :], [[1, EXPERTS]], base=0, channel_multiplier=0, allow_small_or_imprecise_dtypes=True)
            pool.iota(iota_e[:, 1, :], [[1, EXPERTS]], base=-EXPERTS, channel_multiplier=0, allow_small_or_imprecise_dtypes=True)
            pool.iota(iota_x[:, :], [[1, XPP]], base=0, channel_multiplier=XPP,
                      allow_small_or_imprecise_dtypes=True).then_inc(s_const, 1)

            def stage_pos(pair, slot):
                steps.done(pool.tensor_copy(pos_stage[:, slot, :, :], token_pos[:, ds(pair * 2, 2), :]))

            def send(half, i, turn, slot, first=False):
                if not first:
                    pool.wait_ge(s_sent[half][slot], turn * 64)
                pair = i + HALF_BEGIN[half]
                stage_pos(pair, slot)
                rows = moving[half][:, slot, :, :]
                steps.done(pool.tensor_tensor(rows, acc[:, ds(pair * 2, 2), :],
                                              row_mean[:, ds(pair * 2, 2), 0:1].to_broadcast([P, 2, C]), ALU.subtract))
                steps.settle()
                steps.done(pool.tensor_tensor(rows, rows, rstd[:, ds(pair * 2, 2)].unsqueeze(2).to_broadcast([P, 2, C]), ALU.mult))
                steps.settle()
                pass_gate()
                for u in range(2):
                    for k in range(2):
                        pool.indirect_dma_start(
                            out=x_sorted[half], out_offset=Offset(ap=pos_stage[:, slot, u, k:k + 1], axis=0),
                            in_=moving[half][:, slot, u, :], in_offset=None).then_inc(s_sent[half][slot], 16)

            def send_half(half):
                n = HALF_PAIRS[half]
                pool.wait_ge(s_route_done, half + 1)
                for slot in range(2):
                    send(half, slot, 0, slot, first=True)
                with pool.Fori(1, n // 2) as m:
                    steps.enter(m - 1, 6)
                    for slot in range(2):
                        send(half, m * 2 + slot, m, slot)
                    steps.leave(n // 2 - 1)
                if n % 2:
                    send(half, n - 1, n // 2, 0)
            send_half(0)
            for slot in range(2):
                pool.wait_ge(s_sent[0][slot], (HALF_PAIRS[0] + 1 - slot) // 2 * 64)
            pool.wait_ge(s_spill, 16)
            send_half(1)

            out_full = out[0:(PAIRS - 1) * 2 * P, :].rearrange("(g u p) c -> g p u c", u=2, p=P)
            for slot in range(2):
                pool.wait_ge(s_sent[1][slot], HALF_PAIRS[1] // 2 * 64)
                pool.wait_ge(s_fy_out[slot], TX[0] // 2 * 16)
            with pool.Fori(0, BACK) as i:
                steps.enter(i, 1)
                stage_pos(i + SPARE, 0)
                steps.settle()
                pass_gate()
                for k in range(2):
                    for u in range(2):
                        pool.indirect_dma_start(
                            out=spare[:, k * 2 + u, :], out_offset=None, in_=y_sorted[0],
                            in_offset=Offset(ap=pos_stage[:, 0, u, k:k + 1], axis=0)).then_inc(s_back_1, 16)
                at = pool.snap(i + SPARE)
                pool.wait_ge(s_sum_1, i + 1)
                pass_gate()
                pool.dma_start(out_full[ds(at, 1), :, :, :].rearrange("a p u c -> p (a u) c"),
                               spare[:, 0:2, :]).then_inc(s_out_1, 16)
                pool.wait_ge(s_out_1, i * 16 + 16)
                pass_gate()
                steps.leave(BACK)

            for slot in range(2):
                pool.wait_ge(s_fy_out[slot], TXS // 2 * 16)

            def fetch(pair, half, slot, summed=None):
                if summed is not None:
                    pool.wait_ge(s_sum, summed)
                stage_pos(pair, slot)
                steps.settle()
                pass_gate()
                for u in range(2):
                    for k, into in ((0, back_1), (1, back_2)):
                        pool.indirect_dma_start(
                            out=into[:, slot, u, :], out_offset=None, in_=y_sorted[half],
                            in_offset=Offset(ap=pos_stage[:, slot, u, k:k + 1], axis=0)).then_inc(s_back[slot], 16)
            for slot in range(2):
                fetch(HALF_BEGIN[1] + slot, 1, slot)
            with pool.Fori(1, HALF_PAIRS[1] // 2) as m:
                steps.enter(m - 1, 2)
                for slot in range(2):
                    fetch(m * 2 + (slot + HALF_BEGIN[1]), 1, slot, m * 2 + (slot - 1))
                steps.leave(HALF_PAIRS[1] // 2 - 1)
            for pair in range(SPARE):
                fetch(pair, 0, pair, HALF_PAIRS[1] + pair - 1)

        @block.scalar
        def _(act):
            steps = Steps(act, s_act)
            for i in range(4):
                act.wait_ge(s_wt_psum, i + 1)
                ps = bank[2 + i][:, :].rearrange("p (k a n) -> p k a n", k=KC, a=2)
                into = [w_cat[:, :, 3 * C:4 * C], w_cat[:, :, C:2 * C], w_cat[:, :, 2 * C:3 * C], wp_t[:, :, :]][i]
                act.activation(into.rearrange("p k (a n) -> p k a n", a=2), ps, ACT.Copy).then_inc(s_wt, 1)

            act.wait_ge(s_var, TURNS)
            act.activation(rstd[:, :], row_mean[:, :, 1], ACT.Sqrt, bias=eps_col[:, :]).then_inc(s_std, 1)

            def project(g, slot, first=False):
                act.wait_ge(s_xt_psum, g + 1)
                act.activation(xn_t[:, slot, :, :].rearrange("p k n -> p (k n)"), bank[2][:, :], ACT.Copy).then_inc(s_xt, 1)
                if not first:
                    for_slot = (g - slot) * 16
                    act.wait_ge(s_hq_out[slot], for_slot)
                    act.wait_ge(s_ctx, g - 1)
                for u in range(2):
                    act.wait_ge(s_proj, g * 2 + (u + 1))
                    hk, vq = bank[3 + 2 * u], bank[4 + 2 * u]
                    act.activation(h_out[:, slot, u, :], hk[:, 0:C], ACT.Copy)
                    act.activation(v_sb[:, slot, u, :], vq[:, 0:C], ACT.Copy)
                    if u == 0 and not first:
                        act.wait_ge(s_kq, g * 2)
                    elif u == 0 and slot == 1:
                        act.wait_ge(s_kq, 2)
                    act.activation(exp_kq[:, 0, u, :], hk[:, C:2 * C], ACT.Exp)
                    act.activation(exp_kq[:, 1, u, :], vq[:, C:2 * C], ACT.Exp)
                    act.activation(relu_kq[:, 0, u, :], hk[:, C:2 * C], ACT.Relu)
                    act.activation(relu_kq[:, 1, u, :], vq[:, C:2 * C], ACT.Relu).then_inc(s_proj_read, 1)

            h_pairs = h_table.rearrange("(g u p) c -> g p u c", u=2, p=P)

            def store(g, slot):
                act.wait_ge(s_proj_read, g * 2 + 2)
                act.dma_start(h_pairs[ds(g, 1), :, :, :].rearrange("a p u c -> p (a u) c"),
                              h_out[:, slot, :, :]).then_inc(s_hq_out[slot], 16)
                act.wait_ge(s_kq, g * 2 + 2)
                act.dma_start(q_dram[ds(g, 1), :, :].rearrange("a p n -> p (a n)"),
                              q_out[:, slot, :, :].rearrange("p u c -> p (u c)")).then_inc(s_hq_out[slot], 16)
            for g in range(2):
                project(g, g, first=True)
                store(g, g)
            with act.Fori(1, PAIRS // 2) as m:
                for slot in range(2):
                    project(m * 2 + slot, slot)
                    store(m * 2 + slot, slot)
            project(PAIRS - 1, 0)
            store(PAIRS - 1, 0)

            def bring_q(g, slot):
                act.dma_start(q_out[:, slot, :, :].rearrange("p u c -> p (u c)"),
                              q_dram[ds(g, 1), :, :].rearrange("a p n -> p (a n)")).then_inc(s_q_in[slot], 16)

            def copy_qt(g, slot, first=False):
                act.wait_ge(s_qt_psum, g + 1)
                if not first:
                    act.wait_ge(s_mix, g - 1)
                act.activation(xn_t[:, slot, :, :].rearrange("p k n -> p (k n)"), bank[2][:, :], ACT.Copy).then_inc(s_qt, 1)
            for s in range(2):
                act.wait_ge(s_hq_out[s], 32 * (PAIRS // 2 + (PAIRS % 2 if s == 0 else 0)))
            for g in range(2):
                bring_q(g, g)

            def q_turn(g, slot, first=False):
                copy_qt(g - 2, slot, first)
                act.wait_ge(s_qn, g - 1)
                bring_q(g, slot)
            for slot in range(2):
                q_turn(2 + slot, slot, first=True)
            with act.Fori(2, PAIRS // 2) as m:
                for slot in range(2):
                    q_turn(m * 2 + slot, slot)
            copy_qt(PAIRS - 3, 0)
            act.wait_ge(s_qn, PAIRS - 2)
            bring_q(PAIRS - 1, 0)
            copy_qt(PAIRS - 2, 1)
            copy_qt(PAIRS - 1, 0)

            def root(turn):
                act.wait_ge(s_var, turn + (TURNS + 1))
                act.activation(rstd[:, ds(turn * TB, TB)], row_mean[:, ds(turn * TB, TB), 1], ACT.Sqrt,
                               bias=eps_col[:, :]).then_inc(s_std, 1)

            def gate_copies(turn, first=False):
                for j in range(TURN):
                    g = turn * TURN + j
                    act.wait_ge(s_xt_psum, g + (PAIRS + 1))
                    if not first or j > 1:
                        act.wait_ge(s_gate, g if j == 0 else g - 1)
                    act.activation(fxn_t[:, j % 2, :, :].rearrange("p k n -> p (k n)"), bank[j % 2][:, :], ACT.Copy).then_inc(s_xt, 1)

            def softmax_exp(half):
                act.wait_ge(s_route, half * 2 + 1)
                blocks = slice(HALF_BEGIN[half] * 2, (HALF_BEGIN[half] + HALF_PAIRS[half]) * 2)
                act.activation(top_w[:, 1, blocks], small[:, 4, 0:2 * HALF_PAIRS[half]], ACT.Exp).then_inc(s_route, 1)
            root(0)
            gate_copies(0, first=True)
            root(1)
            with act.Fori(1, TURNS_1) as m:
                gate_copies(m)
                root(m + 1)
            softmax_exp(0)
            with act.Fori(TURNS_1, TURNS - 1) as m:
                gate_copies(m)
                root(m + 1)
            gate_copies(TURNS - 1)
            softmax_exp(1)

            y_tiles = [y_sorted[half].rearrange("(t p) c -> t p c", p=P) for half in range(2)]

            def copy_x(t, slot, first=False):
                act.wait_ge(s_fxt_psum, t + 1)
                if not first:
                    act.wait_ge(s_hid_psum, t - 1)
                act.activation(fx_t[:, slot, :, :].rearrange("p k n -> p (k n)"), bank[slot][:, 0:C], ACT.Copy).then_inc(s_fxt, 1)

            def hidden(t, slot, first=False):
                act.wait_ge(s_hidt_psum, t + 1)
                if not first:
                    act.wait_ge(s_fy_psum, t - 1)
                act.activation(hid_t[:, slot, :, :].rearrange("p k n -> p (k n)"), bank[4 + slot][:, :], ACT.Relu).then_inc(s_hidt, 1)

            def store_y(half, t, slot):
                act.wait_ge(s_fy, t + 1)
                act.dma_start(y_tiles[half][ds(t - half * TX[0], 1), :, :].rearrange("a p c -> p (a c)"),
                              fy[:, slot, :]).then_inc(s_fy_out[slot], 16)

            def expert_pair(half, t, first=False, last=False):
                hidden(t, 0, first)
                if not last:
                    copy_x(t + 2, 0)
                    copy_x(t + 3, 1)
                hidden(t + 1, 1, first)
                store_y(half, t, 0)
                store_y(half, t + 1, 1)
            copy_x(0, 0, first=True)
            copy_x(1, 1, first=True)
            expert_pair(0, 0, first=True)
            with act.Fori(1, TX[0] // 2) as m:
                expert_pair(0, m * 2)
            with act.Fori(TX[0] // 2, TXS // 2 - 1) as m:
                expert_pair(1, m * 2)
            expert_pair(1, TXS - 2, last=True)

            out_full = out[0:(PAIRS - 1) * 2 * P, :].rearrange("(g u p) c -> g p u c", u=2, p=P)

            def store_out(pair, i, slot):
                act.wait_ge(s_sum, i + 1)
                act.dma_start(out_full[ds(pair, 1), :, :, :].rearrange("a p u c -> p (a u) c"),
                              result[:, slot, :, :]).then_inc(s_out[slot], 16)
            with act.Fori(0, HALF_PAIRS[1] // 2 - 1) as m:
                for slot in range(2):
                    store_out(m * 2 + (slot + HALF_BEGIN[1]), m * 2 + slot, slot)
            store_out(PAIRS - 2, HALF_PAIRS[1] - 2, 0)
            act.wait_ge(s_sum, HALF_PAIRS[1])
            act.dma_start(out[(NB - 2) * P:(NB - 1) * P, :], result[:, 1, 0, :]).then_inc(s_out[1], 16)
            act.dma_start(out[(NB - 1) * P:N, :], result[0:LAST, 1, 1, :]).then_inc(s_out[1], 16)
            for pair in range(SPARE):
                store_out(pair, HALF_PAIRS[1] + pair, pair)
            act.wait_ge(s_out[0], 16 * (HALF_PAIRS[1] // 2 + 1))
            act.wait_ge(s_out[1], 16 * (HALF_PAIRS[1] // 2 + 2))

        @block.tensor
        def _(pe):
            pe.wait_ge(s_const, 3)
            def counts(i):
                return bank[i][:, 0:HB * CH]

            def hot(slot, half):
                return onehot[:, slot, half * HB:(half + 1) * HB, :].rearrange("p b t -> p (b t)")

            def count(chunk, slot, first=False):
                pe.wait_ge(s_hot, chunk + 1)
                for half in range(2):
                    last = nc.tensor.matmul(counts(half), ones_bf[:, :], hot(slot, half), start=first, stop=True,
                                            skip_group_check=True)
                last.then_inc(s_hot_read, 1)
            count(0, 0, first=True)
            count(1, 1)
            with pe.Fori(1, CHUNKS // 2) as m:
                for slot in range(2):
                    count(m * 2 + slot, slot)
            pe.wait_ge(s_base, 1)
            for half in range(2):
                nc.tensor.matmul(counts(half), ident[:, :],
                                 base[:, half * HB:(half + 1) * HB, :].rearrange("p b t -> p (b t)"),
                                 start=True, stop=True, skip_group_check=True)

            def ranks(chunk, slot):
                pe.wait_ge(s_hot, chunk + (CHUNKS + 1))
                for half in range(2):
                    nc.tensor.matmul(counts(half), tri[:, :], hot(slot, half), start=False, stop=True,
                                     skip_group_check=True).then_inc(s_rank, 1)
                for half in range(2):
                    pe.wait_ge(s_rank_read, chunk * 2 + (half + 1))
                    last = nc.tensor.matmul(counts(half), tri_rest[:, :], hot(slot, half), start=False, stop=True,
                                            skip_group_check=True)
                last.then_inc(s_rank_next, 1)
            with pe.Fori(0, CHUNKS // 2) as m:
                for slot in range(2):
                    ranks(m * 2 + slot, slot)

            pe.wait_ge(s_wload, 16 * 6)
            for i in range(4):
                for k in range(KC):
                    for a in range(2):
                        last = nc.tensor.transpose(bank[2 + i][:, (k * 2 + a) * P:(k * 2 + a + 1) * P],
                                                   w_nat[:, 2 * i + a, k * P:(k + 1) * P], ident[:, :])
                last.then_inc(s_wt_psum, 1)
            pe.wait_ge(s_wt, 4)

            def transpose_pair(source, ps, signal):
                for k in range(KC):
                    for u in range(2):
                        last = nc.tensor.transpose(ps[:, (k * 2 + u) * P:(k * 2 + u + 1) * P],
                                                   source[:, u, k * P:(k + 1) * P], ident[:, :])
                last.then_inc(signal, 1)

            def normed(g, first=False):
                pe.wait_ge(s_xn, g + 1)
                if not first:
                    pe.wait_ge(s_xt, g)
                transpose_pair(xn, bank[2], s_xt_psum)

            def project(g, slot, first=False):
                pe.wait_ge(s_xt, g + 1)
                for u in range(2):
                    if not first:
                        pe.wait_ge(s_proj_read, g * 2 + (u - 1))
                    for cols, ps in ((0, bank[3 + 2 * u]), (2 * C, bank[4 + 2 * u])):
                        for k in range(KC):
                            last = nc.tensor.matmul(ps[:, :], xn_t[:, slot, k, u * P:(u + 1) * P],
                                                    w_cat[:, k, cols:cols + 2 * C], start=(k == 0), stop=(k == KC - 1))
                    last.then_inc(s_proj, 1)

            def context(g, slot, first=False, final=False):
                pe.wait_ge(s_kq, g * 2 + 1)
                for u in range(2):
                    ok = row_ok[:, 1 if final and u == 1 else 0, :]
                    for h in range(KC):
                        nc.tensor.matmul(bank[7][:, h * P:(h + 1) * P], v_sb[:, slot, u, h * P:(h + 1) * P],
                                         k_act[:, slot, u, h * P:(h + 1) * P],
                                         start=(first and u == 0 and h == 0), stop=True, skip_group_check=True)
                    last = nc.tensor.matmul(bank[7][:, C:2 * C], ok, k_act[:, slot, u, :], start=False, stop=True,
                                            skip_group_check=True)
                last.then_inc(s_ctx, 1)
            normed(0, first=True)
            normed(1)
            project(0, 0, first=True)
            normed(2)
            project(1, 1)
            context(0, 0, first=True)
            with pe.Fori(1, PAIRS // 2) as m:
                for slot in range(2):
                    g = m * 2 + slot
                    normed(g + 1)
                    project(g, slot)
                    context(g - 1, 1 - slot)
            project(PAIRS - 1, 0)
            context(PAIRS - 2, 1)
            context(PAIRS - 1, 0, final=True)

            pe.wait_ge(s_ctx_sb, 1)
            for h in range(KC):
                last = nc.tensor.matmul(bank[5][:, h * C:(h + 1) * C], ctx_t[:, h, :], wp_t[:, h, :],
                                        start=True, stop=True)
            last.then_inc(s_mixw_psum, 1)

            def q_transpose(g, first=False):
                pe.wait_ge(s_qn, g + 1)
                if not first:
                    pe.wait_ge(s_qt, g)
                transpose_pair(xn, bank[2], s_qt_psum)

            def mix(g, slot, first=False):
                pe.wait_ge(s_qt, g + 1)
                if not first:
                    pe.wait_ge(s_mix_added, g - 1)
                for u in range(2):
                    ps = bank[3 + slot][:, u * C:(u + 1) * C]
                    for k in range(KC):
                        last = nc.tensor.matmul(ps, xn_t[:, slot, k, u * P:(u + 1) * P], mix_w[:, k, :],
                                                start=(k == 0), stop=(k == KC - 1))
                last.then_inc(s_mix, 1)
            pe.wait_ge(s_mixw, 1)
            q_transpose(0, first=True)
            q_transpose(1)
            mix(0, 0, first=True)
            q_transpose(2)
            mix(1, 1, first=True)
            with pe.Fori(1, PAIRS // 2) as m:
                for slot in range(2):
                    g = m * 2 + slot
                    q_transpose(g + 1)
                    mix(g, slot)
            mix(PAIRS - 1, 0)

            def aggregate(k, slot, first=False):
                pe.wait_ge(s_select, k + 1)
                if first:
                    pe.wait_ge(s_message[slot], 64)
                else:
                    pe.wait_ge(s_message[slot], (k - slot) * 16 + 64)
                if not (first and slot < 2):
                    pe.wait_ge(s_added, k - 1)
                for j in range(SET):
                    ps = bank[(slot % 2) * 2 + j // 2][:, (j % 2) * C:(j % 2 + 1) * C]
                    last = nc.tensor.matmul(ps, select[:, slot % 2, j, :], message[:, slot, j, :], start=True, stop=True)
                last.then_inc(s_agg, 1)
            for slot in range(RING):
                aggregate(slot, slot, first=True)
            with pe.Fori(1, TSETS // RING) as m:
                for slot in range(RING):
                    aggregate(m * RING + slot, slot)

            pe.wait_ge(s_fin, 48)

            def f_transpose(g, j, first=False):
                pe.wait_ge(s_fxn, g + 1)
                if not first:
                    pe.wait_ge(s_xt, g + (PAIRS if j == 0 else PAIRS - 1))
                transpose_pair(fxn[:, j % 2, :, :], bank[j % 2], s_xt_psum)

            def gate(g, j):
                pe.wait_ge(s_xt, g + (PAIRS + 1))
                for u in range(2):
                    for k in range(KC):
                        last = nc.tensor.matmul(bank[2][:, (j * 2 + u) * EXPERTS:(j * 2 + u + 1) * EXPERTS],
                                                fxn_t[:, j % 2, k, u * P:(u + 1) * P], wg[:, k, :],
                                                start=(k == 0), stop=(k == KC - 1))
                last.then_inc(s_gate, 1)

            def gate_turn(turn, first=False):
                g = turn * TURN
                for j in range(TURN):
                    f_transpose(g + j, j, first and j < 2)
                    if j == 1 and not first:
                        pe.wait_ge(s_gate_read, turn)
                    if j:
                        gate(g + (j - 1), j - 1)
                gate(g + (TURN - 1), TURN - 1)

            def count_tokens(half):
                pe.wait_ge(s_route, half * 2 + 1)
                cols = 2 * HALF_PAIRS[half]
                for ps, matrix in ((bank[4], tri), (bank[5], ones_bf)):
                    last = nc.tensor.matmul(ps[:, 0:cols * EXPERTS], matrix[:, :],
                                            both_bf[:, 0:cols, :].rearrange("p b e -> p (b e)"), start=True, stop=True)
                last.then_inc(s_route_psum, 1)
            gate_turn(0, first=True)
            with pe.Fori(1, TURNS_1) as m:
                gate_turn(m)
            count_tokens(0)
            with pe.Fori(TURNS_1, TURNS) as m:
                gate_turn(m)
            count_tokens(1)

            pe.wait_ge(s_w1, 16)
            pe.wait_ge(s_w2, 16)
            pe.wait_ge(s_xtile_row[0], 16)

            w1_flat = w1[:, :, :, :].rearrange("p e k n -> p (e k n)")
            w2_flat = w2[:, :, :, :].rearrange("p e k n -> p (e k n)")

            def x_transpose(t, slot, first=False):
                pe.wait_ge(s_fx[slot], t * 8 + (16 - 8 * slot))
                if not first:
                    pe.wait_ge(s_fxt, t - 1)
                for k in range(KC):
                    last = nc.tensor.transpose(bank[slot][:, k * P:(k + 1) * P], fx[:, slot, k * P:(k + 1) * P], ident[:, :])
                last.then_inc(s_fxt_psum, 1)

            def up(t, slot, expert, first=False):
                pe.wait_ge(s_fxt, t + 1)
                if not first:
                    pe.wait_ge(s_hid, t - 1)
                for k in range(KC):
                    last = nc.tensor.matmul(bank[2 + slot][:, :], fx_t[:, slot, k, :],
                                            w1_flat[:, ds(expert + k * HID, HID)],
                                            start=(k == 0), stop=(k == KC - 1))
                last.then_inc(s_hid_psum, 1)

            def hid_transpose(t, slot, first=False):
                pe.wait_ge(s_hid, t + 1)
                if not first:
                    pe.wait_ge(s_hidt, t - 1)
                for k in range(KH):
                    last = nc.tensor.transpose(bank[4 + slot][:, k * P:(k + 1) * P], hid[:, slot, k * P:(k + 1) * P], ident[:, :])
                last.then_inc(s_hidt_psum, 1)

            def down(t, slot, expert, first=False):
                pe.wait_ge(s_hidt, t + 1)
                if not first:
                    pe.wait_ge(s_fy, t - 1)
                for k in range(KH):
                    last = nc.tensor.matmul(bank[6 + slot][:, 0:C], hid_t[:, slot, k, :],
                                            w2_flat[:, ds(expert + k * C, C)],
                                            start=(k == 0), stop=(k == KH - 1))
                last.then_inc(s_fy_psum, 1)

            def expert_pair(t, experts, first=False, last=False):
                up(t, 0, experts[0], first)
                up(t + 1, 1, experts[1], first)
                hid_transpose(t, 0, first)
                if not last:
                    x_transpose(t + 2, 0)
                    x_transpose(t + 3, 1)
                hid_transpose(t + 1, 1, first)
                down(t, 0, experts[0], first)
                down(t + 1, 1, experts[1], first)

            def experts_of(name, t):
                return load_offsets(pe, name, xtile_row[:, 0, :], t, 4, (EXPERTS - 1) * KC * HID)
            x_transpose(0, 0, first=True)
            x_transpose(1, 1, first=True)
            e = experts_of("expert_first_", 0)
            expert_pair(0, e[0:2], first=True)
            expert_pair(2, e[2:4])
            def group(name, m):
                e = experts_of(name, m * 4)
                expert_pair(m * 4, e[0:2])
                expert_pair(m * 4 + 2, e[2:4])
            with pe.Fori(1, G1) as m:
                group("expert_1_", m)
            pe.wait_ge(s_xtile_row[1], 16)
            with pe.Fori(G1, GROUPS - 1) as m:
                group("expert_2_", m)
            e = experts_of("expert_last_", TXS - 4)
            expert_pair(TXS - 4, e[0:2])
            expert_pair(TXS - 2, e[2:4], last=True)

        @block.vector
        def _(dve):
            steps = Steps(dve, s_dve)
            V = nc.vector
            dve.wait_ge(s_edges, 16 * N_EDGE_LOADS)
            V.tensor_single_scalar(record[:, :, 0], src_i[:, :], 7, ALU.logical_shift_right).then_inc(s_record, 1)
            steps.done(V.tensor_single_scalar(src_i[:, :], src_i[:, :], P - 1, ALU.bitwise_and))
            steps.settle()
            V.tensor_copy(record[:, :, 2].bitcast(F32), src_i[:, :]).then_inc(s_record, 1)
            dve.wait_ge(s_record, 4)
            steps.done(V.tensor_copy(block_bf[:, :], record[:, :, 0]))
            steps.settle()
            dve.wait_ge(s_const, 3)

            def one_hot(chunk, slot):
                V.tensor_tensor(onehot[:, slot, :, :],
                                block_bf[:, ds(chunk * CH, CH)].unsqueeze(1).to_broadcast([P, NB, CH]),
                                iota_b[:, :, :], ALU.is_equal).then_inc(s_hot, 1)
            for slot in range(2):
                one_hot(slot, slot)
            with dve.Fori(1, CHUNKS // 2) as m:
                for slot in range(2):
                    dve.wait_ge(s_hot_read, m * 2 + (slot - 1))
                    one_hot(m * 2 + slot, slot)
            dve.wait_ge(s_hot_read, CHUNKS)
            for half in range(2):
                steps.done(V.tensor_copy(totals[:, half * HB:(half + 1) * HB, :].rearrange("p b t -> p (b t)"),
                                         bank[half][:, 0:HB * CH]))
            steps.settle()
            steps.done(V.tensor_reduce(scan_a[:, :], totals[:, :, :], AX, ALU.add))
            steps.settle()
            steps.done(V.tensor_scalar(scan_i[:, :], scan_a[:, :], float(P - 1), None, ALU.add))
            steps.settle()
            steps.done(V.tensor_single_scalar(scan_i[:, :], scan_i[:, :], 7, ALU.logical_shift_right))
            steps.settle()
            steps.done(V.tensor_copy(scan_a[:, :], scan_i[:, :]))
            steps.settle()
            here, there, step = scan_a, scan_b, 1
            while step < NB:
                steps.done(V.tensor_copy(there[:, 0:step], here[:, 0:step]))
                steps.done(V.tensor_tensor(there[:, step:NB], here[:, step:NB], here[:, 0:NB - step], ALU.add))
                steps.settle()
                here, there, step = there, here, 2 * step
            steps.done(V.tensor_tensor(tile_cmp[:, :, :], iota_t[:, :].unsqueeze(2).to_broadcast([P, TPP, NB]),
                                       here[:, :].unsqueeze(1).to_broadcast([P, TPP, NB]), ALU.is_ge))
            steps.done(V.memset(base[:, 0:1, 0], 0.0))
            steps.done(V.tensor_scalar(base[:, 1:NB, 0], here[:, 0:NB - 1], float(P), None, ALU.mult))
            steps.settle()
            steps.done(V.tensor_reduce(tile_f[:, :], tile_cmp[:, :, :], AX, ALU.add))
            for j in range(1, CH):
                steps.done(V.tensor_tensor(base[:, :, j], base[:, :, j - 1], totals[:, :, j - 1], ALU.add))
                steps.settle()
            V.tensor_scalar(tile_i[:, :], tile_f[:, :], float(NB - 1), float(C), ALU.min, ALU.mult).then_inc(s_tile_out, 1)
            V.engine_nop().then_inc(s_base, 1)

            def position(chunk, slot, first=False):
                if not first:
                    dve.wait_ge(s_rank_next, chunk - 1)
                one_hot(chunk, slot)

            def extract(chunk, slot):
                for half in range(2):
                    dve.wait_ge(s_rank, chunk * 2 + (half + 1))
                    part = slice(half * HB, (half + 1) * HB)
                    V.tensor_tensor(picked[:, part, :].rearrange("p b t -> p (b t)"),
                                    onehot[:, slot, part, :].rearrange("p b t -> p (b t)"),
                                    bank[half][:, 0:HB * CH], ALU.mult).then_inc(s_rank_read, 1)
                dve.wait_ge(s_rank_read, chunk * 2 + 2)
                steps.done(V.tensor_reduce(pos_f[:, :], picked[:, :, :].rearrange("p b t -> p t b"), AX, ALU.add))
                steps.settle()
                steps.done(V.tensor_copy(pos_i[:, 0, :], pos_f[:, :]))
                steps.settle()
                steps.done(V.tensor_single_scalar(pos_i[:, 1, :], pos_i[:, 0, :], 7, ALU.logical_shift_right))
                steps.done(V.tensor_single_scalar(pos_i[:, 2, :], pos_i[:, 0, :], P - 1, ALU.bitwise_and))
                steps.settle()
                V.scalar_tensor_tensor(record[:, ds(chunk * CH, CH), 0], pos_i[:, 2, :], float(TT), pos_i[:, 1, :],
                                       ALU.mult, ALU.add).then_inc(s_pos, 1)
            position(0, 0, first=True)
            position(1, 1, first=True)
            extract(0, 0)
            with dve.Fori(1, CHUNKS // 2) as m:
                steps.enter(m - 1, 8)
                position(m * 2, 0)
                extract(m * 2 - 1, 1)
                position(m * 2 + 1, 1)
                extract(m * 2, 0)
                steps.leave(CHUNKS // 2 - 1)
            extract(CHUNKS - 1, 1)

            def block_stats(first_block, j):
                steps.done(V.bn_stats(stats[:, j, :], acc[:, ds(first_block + j, 1), :].rearrange("p a c -> p (a c)")))

            def gather_stats(first_block):
                steps.settle()
                steps.done(V.memset(turn_mark[:, :], 0.0))
                for j in range(TB):
                    steps.done(V.bn_aggr(turn_stats[:, j, :], stats[:, j, :]))
                steps.settle()
                V.tensor_copy(row_mean[:, ds(first_block, TB), :], turn_stats[:, :, :]).then_inc(s_var, 1)

            def all_row_stats():
                with dve.Fori(0, TURNS) as turn:
                    steps.enter(turn, 2 * TB + 1)
                    first_block = dve.snap(turn * TB)
                    for j in range(TB):
                        block_stats(first_block, j)
                    gather_stats(first_block)
                    dve.wait_ge(s_var, turn + 1)
                    steps.leave(TURNS)

            def invert_std(nth, first_block, count):
                dve.wait_ge(s_std, nth)
                r, n = rstd[:, ds(first_block, count)], newton[:, ds(first_block, count)]
                steps.done(V.reciprocal(r, r))
                steps.settle()
                steps.done(V.tensor_tensor(n, r, r, ALU.mult))
                steps.settle()
                steps.done(V.scalar_tensor_tensor(n, row_mean[:, ds(first_block, count), 1], EPS, n, ALU.add, ALU.mult))
                steps.settle()
                steps.done(V.tensor_scalar(n, n, -0.5, 1.5, ALU.mult, ALU.add))
                steps.settle()
                steps.done(V.tensor_tensor(r, r, n, ALU.mult))
                steps.settle()

            def normalise(g, into, signal):
                for u in range(2):
                    b = g * 2 + u
                    last = V.tensor_scalar(into[:, u, :], acc[:, ds(b, 1), :].rearrange("p a c -> p (a c)"),
                                           row_mean[:, ds(b, 1), 0], rstd[:, ds(b, 1)], ALU.subtract, ALU.mult)
                last.then_inc(signal, 1)
            dve.wait_ge(s_x, 16 * len(XCUT))
            all_row_stats()
            dve.wait_ge(s_wload, 16 * 6)
            steps.done(V.tensor_tensor(bias_row[:, :], bias_in[:, 0, :], bias_in[:, 1, :], ALU.add))
            invert_std(1, 0, NB)

            def activate(g, slot):
                dve.wait_ge(s_proj_read, g * 2 + 2)
                for i, into in ((0, k_act), (1, q_out)):
                    V.scalar_tensor_tensor(into[:, slot, :, :].rearrange("p u c -> p (u c)"),
                                           exp_kq[:, i, :, :].rearrange("p u c -> p (u c)"), 1.0,
                                           relu_kq[:, i, :, :].rearrange("p u c -> p (u c)"),
                                           ALU.min, ALU.add).then_inc(s_kq, 1)
            normalise(0, xn, s_xn)
            dve.wait_ge(s_xt_psum, 1)
            normalise(1, xn, s_xn)
            activate(0, 0)
            dve.wait_ge(s_xt_psum, 2)
            normalise(2, xn, s_xn)
            activate(1, 1)
            with dve.Fori(1, PAIRS // 2) as m:
                for slot in range(2):
                    g = m * 2 + slot
                    dve.wait_ge(s_xt_psum, g + 1)
                    normalise(g + 1, xn, s_xn)
                    dve.wait_ge(s_ctx, g - 1)
                    dve.wait_ge(s_hq_out[slot], (g - slot) * 16)
                    activate(g, slot)
            dve.wait_ge(s_ctx, PAIRS - 2)
            dve.wait_ge(s_hq_out[0], (PAIRS - 1) * 16)
            activate(PAIRS - 1, 0)

            dve.wait_ge(s_ctx, PAIRS)
            for h in range(KC):
                steps.done(V.tensor_tensor(ctx_t[:, h, :], head_mask[:, :], bank[7][:, h * P:(h + 1) * P], ALU.mult))
            steps.done(V.tensor_copy(ksum[:, :], bank[7][:, C:2 * C]))
            steps.settle()
            V.engine_nop().then_inc(s_ctx_sb, 1)
            dve.wait_ge(s_mixw_psum, 1)
            V.tensor_copy(mix_w[:, :, :].rearrange("p k c -> p (k c)"), bank[5][:, :]).then_inc(s_mixw, 1)

            def scale_q(g, slot, first=False):
                if first:
                    dve.wait_ge(s_q_in[slot], 16)
                else:
                    dve.wait_ge(s_q_in[slot], g * 8 + (16 - 8 * slot))
                steps.done(V.tensor_tensor(k_act[:, 0, :, :], q_out[:, slot, :, :],
                                           ksum[:, :].unsqueeze(1).to_broadcast([P, 2, C]), ALU.mult))
                steps.settle()
                steps.done(V.tensor_reduce(den[:, 0, :], k_act[:, 0, :, :].rearrange("p u (h d) -> p (u h) d", d=HD), AX, ALU.add))
                steps.settle()
                steps.done(V.tensor_scalar(den[:, 1, :], den[:, 0, :], 1e-6, None, ALU.max))
                steps.settle()
                steps.done(V.reciprocal(den[:, 2, :], den[:, 1, :]))
                steps.settle()
                if not first or slot:
                    dve.wait_ge(s_qt_psum, g)
                V.tensor_tensor(xn[:, :, :].rearrange("p u (h d) -> p (u h) d", d=HD),
                                q_out[:, slot, :, :].rearrange("p u (h d) -> p (u h) d", d=HD),
                                den[:, 2, :].unsqueeze(2).to_broadcast([P, 2 * HEADS, HD]), ALU.mult).then_inc(s_qn, 1)

            def add_mix(g, slot):
                pair = acc[:, ds(g * 2, 2), :]
                steps.done(V.tensor_tensor(pair, pair, bias_row[:, :].unsqueeze(1).to_broadcast([P, 2, C]), ALU.add))
                steps.settle()
                dve.wait_ge(s_mix, g + 1)
                pair = pair.rearrange("p u c -> p (u c)")
                V.tensor_tensor(pair, pair, bank[3 + slot][:, :], ALU.add).then_inc(s_mix_added, 1)
            scale_q(0, 0, first=True)
            scale_q(1, 1, first=True)
            scale_q(2, 0)
            add_mix(0, 0)
            with dve.Fori(1, PAIRS // 2) as m:
                steps.enter(m - 1, 10)
                scale_q(m * 2 + 1, 1)
                add_mix(m * 2 - 1, 1)
                scale_q(m * 2 + 2, 0)
                add_mix(m * 2, 0)
                steps.leave(PAIRS // 2 - 1)
            add_mix(PAIRS - 2, 1)
            add_mix(PAIRS - 1, 0)

            dve.wait_ge(s_tile_row, 16)
            dve.wait_ge(s_mix_added, PAIRS)

            def select_tile(slot, j):
                return V.tensor_scalar(select[:, slot % 2, j, :], iota_n[:, :], gather_stage[:, slot, j, 1:2].bitcast(F32),
                                       gather_stage[:, slot, j, 2:3].bitcast(F32), ALU.is_equal, ALU.mult)

            acc_flat = acc[:, :, :].rearrange("p b c -> p (b c)")

            def add_set(slot, blocks):
                for j in range(SET):
                    to = acc_flat[:, ds(blocks[j], C)]
                    ps = bank[(slot % 2) * 2 + j // 2][:, (j % 2) * C:(j % 2 + 1) * C]
                    added = V.tensor_tensor(to, to, ps, ALU.add)
                    if j < SET - 1:
                        steps.done(added)
                        steps.settle()
                added.then_inc(s_added, 1)

            def set_turn(k, slot, k_list=None, add_slot=None, first=False):
                dve.wait_ge(s_list[slot], k_list)
                for j in range(SET):
                    made = select_tile(slot, j)
                made.then_inc(s_select, 1)
                if not first:
                    blocks = load_offsets(dve, f"block_{slot}_{int(isinstance(k, int))}_", tile_row, k * SET - SET, SET, (NB - 1) * C)
                    if slot != 1 or not isinstance(k, int):
                        dve.wait_ge(s_added, k - 1)
                    dve.wait_ge(s_agg, k)
                    add_set(add_slot, blocks)
            set_turn(0, 0, 16, first=True)
            for slot in range(1, RING):
                set_turn(slot, slot, 16, slot - 1)
            with dve.Fori(1, TSETS // RING) as m:
                steps.enter(m - 1, (SET - 1) * RING)
                for slot in range(RING):
                    set_turn(m * RING + slot, slot, m * 16 + 16, (slot - 1) % RING)
                steps.leave(TSETS // RING - 1)
            dve.wait_ge(s_added, TSETS - 1)
            dve.wait_ge(s_agg, TSETS)
            add_set(RING - 1, load_offsets(dve, "block_end_", tile_row, TT - SET, SET, (NB - 1) * C))

            dve.wait_ge(s_added, TSETS)

            def finish_stats(turn):
                gather_stats(turn * TB)
                invert_std(turn + 2, turn * TB, TB)
            FINISH = TB + 1 + 5

            def gate_turn(turn, half, ahead=True, first=False):
                for j in range(TURN):
                    g = turn * TURN + j
                    if not first or j > 1:
                        dve.wait_ge(s_xt_psum, g + (PAIRS if j == 0 else PAIRS - 1))
                    normalise(g, fxn[:, j % 2, :, :], s_fxn)
                    if ahead:
                        for u in range(2):
                            block_stats(turn * TB + TB, j * 2 + u)
                if ahead:
                    finish_stats(turn + 1)
                dve.wait_ge(s_gate, turn * TURN + TURN)
                V.tensor_copy(logits[:, ds(turn * TB - 2 * HALF_BEGIN[half], TB), :].rearrange("p b e -> p (b e)"),
                              bank[2][:, 0:TB * EXPERTS]).then_inc(s_gate_read, 1)
            for j in range(TB):
                block_stats(0, j)
            finish_stats(0)
            gate_turn(0, 0, first=True)
            with dve.Fori(1, TURNS_1) as m:
                steps.enter(m - 1, TB + FINISH)
                gate_turn(m, 0)
                steps.leave(TURNS_1 - 1)
            dve.wait_ge(s_fin, 48)
            dve.wait_ge(s_const, 4)

            def route_half(half):
                nb = 2 * HALF_PAIRS[half]
                mine = slice(2 * HALF_BEGIN[half], 2 * HALF_BEGIN[half] + nb)
                dve.wait_ge(s_gate_read, [TURNS_1, TURNS][half])
                lg, wk, rk = logits[:, 0:nb, :], work[:, 0:nb, :], rank[:, 0:nb, :]
                for i in range(2):
                    steps.done(V.tensor_tensor(lg, lg, gate_b[:, i, :].unsqueeze(1).to_broadcast([P, nb, EXPERTS]), ALU.add))
                    steps.settle()

                def over_experts(col):
                    return small[:, col, 0:nb].unsqueeze(2).to_broadcast([P, nb, EXPERTS])

                def over_blocks(row):
                    return row.unsqueeze(1).to_broadcast([P, nb, EXPERTS])

                def best(i):
                    steps.done(V.tensor_reduce(small[:, i, 0:nb], lg, AX, ALU.max))
                    steps.settle()
                    steps.done(V.tensor_tensor(wk, lg, over_experts(i), ALU.is_equal))
                    steps.settle()
                    steps.done(V.tensor_tensor(wk, wk, over_blocks(iota_e[:, 1, :]), ALU.mult))
                    steps.settle()
                    steps.done(V.tensor_reduce(small[:, 2 + i, 0:nb], wk, AX, ALU.min))
                    steps.settle()
                    steps.done(V.tensor_tensor(pick[:, i, 0:nb, :], over_blocks(iota_e[:, 1, :]), over_experts(2 + i), ALU.is_equal))
                    steps.settle()
                best(0)
                steps.done(V.tensor_scalar(wk, pick[:, 0, 0:nb, :], 1.0, -1.0, ALU.subtract, ALU.mult))
                steps.settle()
                steps.done(V.tensor_tensor(lg, lg, wk, ALU.mult))
                steps.settle()
                steps.done(V.scalar_tensor_tensor(lg, pick[:, 0, 0:nb, :], -3.0e38, lg, ALU.mult, ALU.add))
                steps.settle()
                best(1)
                steps.done(V.tensor_tensor(small[:, 4, 0:nb], small[:, 1, 0:nb], small[:, 0, 0:nb], ALU.subtract))
                steps.done(V.tensor_tensor(both_bf[:, 0:nb, :], pick[:, 0, 0:nb, :], pick[:, 1, 0:nb, :], ALU.add))
                steps.settle()
                V.engine_nop().then_inc(s_route, 1)
                dve.wait_ge(s_route, half * 2 + 2)
                steps.done(V.tensor_scalar(small[:, 5, 0:nb], top_w[:, 1, mine], 1.0, None, ALU.add))
                steps.settle()
                steps.done(V.reciprocal(top_w[:, 0, mine], small[:, 5, 0:nb]))
                steps.settle()
                steps.done(V.tensor_tensor(top_w[:, 1, mine], top_w[:, 1, mine], top_w[:, 0, mine], ALU.mult))
                dve.wait_ge(s_route_psum, half + 1)
                steps.done(V.tensor_copy(carry_a[:, 0:nb, :].rearrange("p b e -> p (b e)"), bank[5][:, 0:nb * EXPERTS]))
                steps.settle()
                here, there, step = carry_a, carry_b, 1
                while step < nb:
                    steps.done(V.tensor_copy(there[:, 0:step, :], here[:, 0:step, :]))
                    steps.done(V.tensor_tensor(there[:, step:nb, :], here[:, step:nb, :], here[:, 0:nb - step, :], ALU.add))
                    steps.settle()
                    here, there, step = there, here, 2 * step
                steps.done(V.tensor_scalar(ends_i[:, :], here[:, nb - 1, :], float(P - 1), None, ALU.add))
                steps.settle()
                steps.done(V.tensor_single_scalar(ends_i[:, :], ends_i[:, :], 7, ALU.logical_shift_right))
                steps.settle()
                steps.done(V.tensor_copy(ends[:, 0, :], ends_i[:, :]))
                steps.settle()
                for e in range(1, EXPERTS):
                    steps.done(V.tensor_tensor(ends[:, 0, e:e + 1], ends[:, 0, e:e + 1], ends[:, 0, e - 1:e], ALU.add))
                    steps.settle()
                steps.done(V.tensor_tensor(xcmp[:, :, :], iota_x[:, :].unsqueeze(2).to_broadcast([P, XPP, EXPERTS]),
                                           ends[:, 0, :].unsqueeze(1).to_broadcast([P, XPP, EXPERTS]), ALU.is_ge))
                steps.done(V.memset(ends[:, 1, 0:1], 0.0))
                steps.done(V.tensor_scalar(ends[:, 1, 1:EXPERTS], ends[:, 0, 0:EXPERTS - 1], float(P), None, ALU.mult))
                steps.settle()
                steps.done(V.tensor_reduce(xtile_f[:, :], xcmp[:, :, :], AX, ALU.add))
                steps.settle()
                if half:
                    dve.wait_ge(s_xtile_dram, 16)
                for i, stride in ((0, KC * HID), (1, HID + C)):
                    steps.done(V.tensor_scalar(xtile_i[:, i, :], xtile_f[:, :], float(EXPERTS - 1), float(stride), ALU.min, ALU.mult))
                steps.done(V.tensor_copy(rk.rearrange("p b e -> p (b e)"), bank[4][:, 0:nb * EXPERTS]))
                steps.settle()
                steps.done(V.tensor_tensor(rank[:, 1:nb, :], rank[:, 1:nb, :], here[:, 0:nb - 1, :], ALU.add))
                steps.settle()
                steps.done(V.tensor_tensor(rk, rk, over_blocks(ends[:, 1, :]), ALU.add))
                steps.settle()
                for i in range(2):
                    steps.done(V.tensor_tensor(wk, rk, pick[:, i, 0:nb, :], ALU.mult))
                    steps.settle()
                    steps.done(V.tensor_reduce(small[:, i, 0:nb], wk, AX, ALU.add))
                    steps.settle()
                    steps.done(V.tensor_copy(token_pos[:, mine, i], small[:, i, 0:nb]))
                steps.settle()
                V.engine_nop().then_inc(s_route_done, 1)

            route_half(0)
            with dve.Fori(TURNS_1, TURNS - 1) as m:
                steps.enter(m - TURNS_1, TB + FINISH)
                gate_turn(m, 1)
                steps.leave(TURNS - 1 - TURNS_1)
            gate_turn(TURNS - 1, 1, ahead=False)
            route_half(1)

            dve.wait_ge(s_b12, 32)
            for half in range(2):
                dve.wait_ge(s_xtile_row[half], 16)

            b12_flat = b12[:, :, :].rearrange("p e n -> p (e n)")

            def add_b1(t, slot, expert, first=False):
                dve.wait_ge(s_hid_psum, t + 1)
                if not first:
                    dve.wait_ge(s_hidt_psum, t - 1)
                V.tensor_tensor(hid[:, slot, :], bank[2 + slot][:, :],
                                b12_flat[:, ds(expert, HID)], ALU.add).then_inc(s_hid, 1)

            def add_b2(t, slot, expert, first=False):
                dve.wait_ge(s_fy_psum, t + 1)
                if not first:
                    dve.wait_ge(s_fy_out[slot], (t - slot) * 8)
                V.tensor_tensor(fy[:, slot, :], bank[6 + slot][:, 0:C],
                                b12_flat[:, ds(expert + HID, C)], ALU.add).then_inc(s_fy, 1)

            def expert_pair(t, experts, first=False):
                add_b1(t, 0, experts[0], first)
                add_b1(t + 1, 1, experts[1], first)
                add_b2(t, 0, experts[0], first)
                add_b2(t + 1, 1, experts[1], first)

            def experts_of(name, t):
                return load_offsets(dve, name, xtile_row[:, 1, :], t, 4, (EXPERTS - 1) * (HID + C))
            e = experts_of("expert_first_", 0)
            expert_pair(0, e[0:2], first=True)
            expert_pair(2, e[2:4])

            def group(name, m):
                e = experts_of(name, m * 4)
                expert_pair(m * 4, e[0:2])
                expert_pair(m * 4 + 2, e[2:4])

            def weighted(to, row, b, k, more):
                return V.scalar_tensor_tensor(to, row, top_w[:, k, ds(b, 1)], more, ALU.mult, ALU.add)
            with dve.Fori(1, G1 + 2) as m:
                group("expert_1_", m)
            with dve.Fori(G1 + 2, G1 + 2 + BACK) as m:
                steps.enter(m - (G1 + 2), 2)
                group("expert_2_", m)
                first_block = dve.snap(m * 2 + 2 * (SPARE - G1 - 2))
                dve.wait_ge(s_back_1, m * 64 + 64 * (1 - G1 - 2))
                for u in range(2):
                    b = first_block + u
                    steps.done(weighted(spare[:, u, :], spare[:, u, :], b, 0, acc[:, ds(b, 1), :].rearrange("p a c -> p (a c)")))
                steps.settle()
                for u in range(2):
                    last = weighted(spare[:, u, :], spare[:, 2 + u, :], first_block + u, 1, spare[:, u, :])
                last.then_inc(s_sum_1, 1)
                steps.leave(BACK)
            with dve.Fori(G1 + 2 + BACK, GROUPS) as m:
                group("expert_3_", m)

            def combine(pair, slot, turn, first=False):
                dve.wait_ge(s_back[slot], turn * 64 + 64)
                if not first:
                    dve.wait_ge(s_out[slot], turn * 16)
                for u in range(2):
                    b = pair * 2 + u
                    steps.done(weighted(result[:, slot, u, :], back_1[:, slot, u, :], b, 0,
                                        acc[:, ds(b, 1), :].rearrange("p a c -> p (a c)")))
                steps.settle()
                for u in range(2):
                    last = weighted(result[:, slot, u, :], back_2[:, slot, u, :], pair * 2 + u, 1, result[:, slot, u, :])
                last.then_inc(s_sum, 1)
            for slot in range(2):
                combine(HALF_BEGIN[1] + slot, slot, 0, first=True)
            with dve.Fori(1, HALF_PAIRS[1] // 2) as m:
                steps.enter(m - 1, 4)
                for slot in range(2):
                    combine(m * 2 + (slot + HALF_BEGIN[1]), slot, m)
                steps.leave(HALF_PAIRS[1] // 2 - 1)
            dve.wait_ge(s_reload, 16)
            dve.wait_ge(s_out[1], 16 * (HALF_PAIRS[1] // 2 + 1))
            for pair in range(SPARE):
                combine(pair, pair, HALF_PAIRS[1] // 2)


_INS = ["x", "src", "dst", "edge_weight", "L0_gnn_W", "L0_gnn_b", "L0_mix_Wq", "L0_mix_Wkv", "L0_mix_Wproj",
        "L0_mix_bproj", "L0_ffn_Wg", "L0_ffn_bg", "L0_ffn_bias", "L0_ffn_W1", "L0_ffn_b1", "L0_ffn_W2", "L0_ffn_b2"]


def kernel(**inputs):
    import numpy as np
    import concourse.bacc as bacc
    from concourse import mybir
    from concourse.bass_utils import run_bass_kernel_spmd

    nc = bacc.Bacc("TRN2", target_bir_lowering=False, num_devices=1)
    arrays, args = {}, []
    for name in _INS:
        a = np.ascontiguousarray(inputs[name])
        arrays[f"in_{name}"] = a
        args.append(nc.dram_tensor(f"in_{name}", a.shape, mybir.dt.from_np(a.dtype), kind="ExternalInput").ap())
    out = nc.dram_tensor("out", inputs["x"].shape, mybir.dt.float32, kind="ExternalOutput").ap()
    gps_layer(nc, *args, out)
    return run_bass_kernel_spmd(nc, [arrays], core_ids=[0]).results[0]["out"]
```

```python
from contextlib import ExitStack

from concourse.bass import DynSlice


class Steps:

    def __init__(self, eng, sem):
        self.eng, self.sem, self.base, self.count = eng, sem, 0, 0

    def done(self, instruction):
        instruction.then_inc(self.sem, 1)
        self.count += 1

    def settle(self):
        self.eng.wait_ge(self.sem, self.base + self.count)

    def enter(self, turn, per_turn):
        self.before, self.per_turn = self.count, per_turn
        self.base, self.count = turn * per_turn + self.before, 0

    def leave(self, turns):
        assert self.count == self.per_turn, (self.count, self.per_turn)
        self.base, self.count = 0, self.before + turns * self.per_turn


def load_offsets(eng, name, row, first, count, top):
    registers = [eng.alloc_register(f"{name}{i}") for i in range(count)]
    eng.load(registers, row[0:1, first:first + count] if isinstance(first, int) else row[0:1, DynSlice(first, count)])
    return [eng.snap(r, min_val=0, max_val=top) for r in registers]


def gps_layer(nc, x, src, dst, edge_weight, gnn_W, gnn_b, mix_Wq, mix_Wkv, mix_Wproj, mix_bproj,
              ffn_Wg, ffn_bg, ffn_bias, ffn_W1, ffn_b1, ffn_W2, ffn_b2, out):
    import concourse.bass as bass
    from concourse import mybir

    F32, BF16, I32 = mybir.dt.float32, mybir.dt.bfloat16, mybir.dt.int32
    ALU, ACT, AX = mybir.AluOpType, mybir.ActivationFunctionType, mybir.AxisListType.X
    ds = bass.ds
    Offset = bass.IndirectOffsetOnAxis

    P = 128
    N, C = x.shape
    E = src.shape[0]
    KC = C // P
    NB = -(-N // P)
    LAST = N - (NB - 1) * P
    PAIRS = NB // 2
    HEADS, HD = 8, 32
    EXPERTS, _, HID = ffn_W1.shape
    KH = HID // P
    EPS = 1e-5
    CH = 8
    HB = NB // 2
    EL = -(-E // P)
    ET = -(-EL // (4 * CH)) * 4 * CH
    CHUNKS = ET // CH
    SCATTERS = CHUNKS // 2 - (ET - EL) // (2 * CH)
    LAST_CHUNKS = [min(CH, EL - 2 * (SCATTERS - 1) * CH), EL - (2 * SCATTERS - 1) * CH]
    SET, RING = 4, 4
    TT = -(-((EL * P + NB * (P - 1)) // P) // SET) * SET
    TSETS = TT // SET
    TURNS_G = TSETS // RING
    TPP = -(-TT // P)
    TURN = 7
    TB = 2 * TURN
    TURNS = PAIRS // TURN
    TURNS_1 = TURNS * 3 // 7
    HALF_PAIRS = [TURNS_1 * TURN, (TURNS - TURNS_1) * TURN]
    HALF_BEGIN = [0, HALF_PAIRS[0]]
    NBX = 2 * max(HALF_PAIRS)
    TX = [-(-((4 * n * P + EXPERTS * (P - 1)) // P) // 4) * 4 for n in HALF_PAIRS]
    TXS = sum(TX)
    XPP = 2
    G1, GROUPS = TX[0] // 4, TXS // 4
    SPARE = 2
    BACK = HALF_PAIRS[0] - SPARE
    assert PAIRS % TURN == 0 and max(TX) <= P * XPP and G1 + 1 + BACK < GROUPS and SPARE == 2 and HALF_PAIRS[1] % 4 == 0
    assert CHUNKS % 4 == 0 and LAST_CHUNKS[1] > 0 and KC * HID == KH * C and NB % 4 == 2 and HB * CH <= 512 and KC == 2 and 4 * C == 1024 and HID == 512

    h_table = nc.dram_tensor("h_table", (NB * P, C), F32, kind="Internal").ap()
    q_dram = nc.dram_tensor("q_dram", (PAIRS, P, 2 * C), F32, kind="Internal").ap()
    edge_list = nc.dram_tensor("edge_list", (P * TT, 3), I32, kind="Internal").ap()
    tile_dram = nc.dram_tensor("tile_dram", (P * TPP,), I32, kind="Internal").ap()
    xtile_dram = nc.dram_tensor("xtile_dram", (2, 2, P * XPP), I32, kind="Internal").ap()
    x_sorted = [nc.dram_tensor(f"x_sorted{i}", (TX[i] * P, C), F32, kind="Internal").ap() for i in range(2)]
    y_sorted = [nc.dram_tensor("y_sorted0", (TX[0] * P, C), F32, kind="Internal").ap()]
    NB2 = 2 * HALF_PAIRS[1]
    y_token = nc.dram_tensor("y_token", (2 * NB2 * P + 4 * P, C), F32, kind="Internal").ap()
    number_sorted = nc.dram_tensor("number_sorted", (P * TX[1], 1), I32, kind="Internal").ap()
    acc_dram = nc.dram_tensor("acc_dram", (P, 2 * SPARE * C), F32, kind="Internal").ap()

    with ExitStack() as whole:
        def sem(name):
            return whole.enter_context(nc.semaphore(name))

        def sb(name, shape, dtype, scope=whole):
            return scope.enter_context(nc.sbuf_tensor(name, shape, dtype))

        acc = sb("acc", [P, NB, C], F32)
        ident = sb("ident", [P, P], F32)
        tri = sb("tri", [P, P], BF16)
        ones_bf = sb("ones_bf", [P, P], BF16)
        row_mean = sb("row_mean", [P, NB, 2], F32)
        rstd = sb("rstd", [P, NB], F32)
        stats = sb("stats", [P, TB, 6], F32)
        turn_stats = sb("turn_stats", [P, TB, 2], F32)
        turn_mark = sb("turn_mark", [P, 1], F32)
        eps_col = sb("eps_col", [P, 1], F32)

        early = ExitStack()
        iota_n = sb("iota_n", [P, P], F32, early)
        tri_rest = sb("tri_rest", [P, P], BF16, early)
        record = sb("record", [P, ET, 4], I32, early)
        block_bf = sb("block_bf", [P, ET], BF16, early)
        onehot = sb("onehot", [P, 2, NB, CH], BF16, early)
        totals = sb("totals", [P, NB, CH], F32, early)
        picked = totals
        base = sb("base", [P, NB, CH], F32, early)
        scan_a = sb("scan_a", [P, NB], F32, early)
        scan_b = sb("scan_b", [P, NB], F32, early)
        scan_i = sb("scan_i", [P, NB], I32, early)
        pos_f = sb("pos_f", [P, CH], F32, early)
        pos_i = sb("pos_i", [P, 3, CH], I32, early)
        iota_b = sb("iota_b", [P, NB, CH], BF16, early)
        iota_t = sb("iota_t", [P, TPP], F32, early)
        tile_f = sb("tile_f", [P, TPP], F32, early)
        tile_i = sb("tile_i", [P, TPP], I32, early)
        tile_row = sb("tile_row", [1, P * TPP], I32, early)
        gather_stage = sb("gather_stage", [P, RING, SET, 3], I32, early)
        scatter_stage = sb("scatter_stage", [P, 2, CH, 4], I32, early)
        number_fill = sb("number_fill", [P, TX[1]], I32, early)
        zeros = sb("zeros", [P, 4 * C], F32, early)
        w_cat = sb("w_cat", [P, KC, 4 * C], F32, early)
        wp_t = sb("wp_t", [P, KC, C], F32, early)
        head_mask = sb("head_mask", [P, P], F32, early)
        row_ok = sb("row_ok", [P, 2, P], F32, early)
        bias_row = sb("bias_row", [P, C], F32, early)
        ctx_t = sb("ctx_t", [P, KC, P], F32, early)
        ksum = sb("ksum", [P, C], F32, early)
        mix_w = sb("mix_w", [P, KC, C], F32, early)
        xn = sb("xn", [P, 2, C], F32, early)
        newton = sb("newton", [P, NB], F32, early)
        inputs = ExitStack()
        src_i = sb("src_i", [P, ET], I32, inputs)
        dst_i = sb("dst_i", [P, ET], I32, inputs)
        w_in = sb("w_in", [P, ET], I32, inputs)
        tile_cmp = sb("tile_cmp", [P, TPP, NB], F32, inputs)
        w_nat = sb("w_nat", [P, 8, C], F32, inputs)
        bias_in = sb("bias_in", [P, 2, C], F32, inputs)
        inputs.close()
        attention = ExitStack()
        h_out = sb("h_out", [P, 2, 2, C], F32, attention)
        q_out = sb("q_out", [P, 2, 2, C], F32, attention)
        k_act = sb("k_act", [P, 2, 2, C], F32, attention)
        v_sb = sb("v_sb", [P, 2, 2, C], F32, attention)
        exp_kq = sb("exp_kq", [P, 2, 2, C], F32, attention)
        relu_kq = sb("relu_kq", [P, 2, 2, C], F32, attention)
        xn_t = sb("xn_t", [P, 2, KC, 2 * P], F32, attention)
        den = sb("den", [P, 4, 2 * HEADS], F32, attention)
        attention.close()
        message = sb("message", [P, RING, SET, C], F32, early)
        select = sb("select", [P, 2, SET, P], F32, early)
        early.close()

        w1 = sb("w1", [P, EXPERTS, KC, HID], F32)
        fx = sb("fx", [P, 2, C], F32)
        fx_t = sb("fx_t", [P, 2, KC, P], F32)
        hid = sb("hid", [P, 2, HID], F32)
        hid_t = sb("hid_t", [P, 2, KH, P], F32)
        fy = sb("fy", [P, 2, C], F32)
        wg = sb("wg", [P, KC, EXPERTS], F32)
        gate_b = sb("gate_b", [P, 2, EXPERTS], F32)
        top_w = sb("top_w", [P, 2, NB], F32)
        token_pos = sb("token_pos", [P, NB, 2], I32)
        pos_stage = sb("pos_stage", [P, 2, 2, 2], I32)
        token_pos_2 = sb("token_pos_2", [P, NB2, 2], I32)
        number = sb("number", [P, NB2, 2], I32)
        number_pos = sb("number_pos", [P, 2, 2, 2, 2], I32)
        numbers = sb("numbers", [P, TX[1]], I32)
        number_stage = sb("number_stage", [P, 4], I32)
        xtile_row = sb("xtile_row", [1, 2, TXS], I32)
        w2 = sb("w2", [P, EXPERTS, KH, C], F32)
        route = ExitStack()
        logits = sb("logits", [P, NBX, EXPERTS], F32, route)
        pick = sb("pick", [P, 2, NBX, EXPERTS], F32, route)
        both_bf = sb("both_bf", [P, NBX, EXPERTS], BF16, route)
        work = sb("work", [P, NBX, EXPERTS], F32, route)
        rank = sb("rank", [P, NBX, EXPERTS], F32, route)
        carry_a = sb("carry_a", [P, NBX, EXPERTS], F32, route)
        carry_b = sb("carry_b", [P, NBX, EXPERTS], F32, route)
        small = sb("small", [P, 6, NBX], F32, route)
        iota_e = sb("iota_e", [P, 2, EXPERTS], F32, route)
        ends = sb("ends", [P, 4, EXPERTS], F32, route)
        ends_i = sb("ends_i", [P, EXPERTS], I32, route)
        iota_x = sb("iota_x", [P, XPP], F32, route)
        xcmp = sb("xcmp", [P, XPP, EXPERTS], F32, route)
        xtile_f = sb("xtile_f", [P, XPP], F32, route)
        xtile_i = sb("xtile_i", [P, 2, XPP], I32, route)
        fxn = sb("fxn", [P, 2, 2, C], F32, route)
        fxn_t = sb("fxn_t", [P, 2, KC, 2 * P], F32, route)
        newton_turn = sb("newton_turn", [P, TB], F32, route)
        pos_split = sb("pos_split", [P, 2, NB2, 2], I32, route)
        route.close()
        b12 = sb("b12", [P, EXPERTS, HID + C], F32)

        bank = [whole.enter_context(nc.psum_tensor(f"bank{i}", [P, 512], F32)) for i in range(8)]

        s_const = sem("s_const")
        s_passed = sem("s_passed")
        s_pool = sem("s_pool")
        s_dve = sem("s_dve")
        s_act = sem("s_act")
        s_edges = sem("s_edges")
        s_x = sem("s_x")
        s_wload = sem("s_wload")
        s_zeroed = sem("s_zeroed")
        s_blank = sem("s_blank")
        s_record = sem("s_record")
        s_hots = sem("s_hots")
        s_hots_read = sem("s_hots_read")
        s_hot = sem("s_hot")
        s_base = sem("s_base")
        s_rank = sem("s_rank")
        s_rank_read = sem("s_rank_read")
        s_rank_next = sem("s_rank_next")
        s_pos = sem("s_pos")
        s_staged = [sem(f"s_staged{i}") for i in range(2)]
        s_scattered = [sem(f"s_scattered{i}") for i in range(2)]
        s_tile_out = sem("s_tile_out")
        s_tile_dram = sem("s_tile_dram")
        s_tile_row = sem("s_tile_row")
        s_wt_psum = sem("s_wt_psum")
        s_wt = sem("s_wt")
        s_var = sem("s_var")
        s_std = sem("s_std")
        s_xn = sem("s_xn")
        s_xt_psum = sem("s_xt_psum")
        s_xt = sem("s_xt")
        s_proj = sem("s_proj")
        s_proj_read = sem("s_proj_read")
        s_kq = sem("s_kq")
        s_hq_out = [sem(f"s_hq_out{i}") for i in range(2)]
        s_ctx = sem("s_ctx")
        s_ctx_sb = sem("s_ctx_sb")
        s_mixw_psum = sem("s_mixw_psum")
        s_mixw = sem("s_mixw")
        s_q_in = [sem(f"s_q_in{i}") for i in range(2)]
        s_qn = sem("s_qn")
        s_qt_psum = sem("s_qt_psum")
        s_qt = sem("s_qt")
        s_mix = sem("s_mix")
        s_mix_added = sem("s_mix_added")
        s_list = [sem(f"s_list{i}") for i in range(RING)]
        s_message = [sem(f"s_message{i}") for i in range(RING)]
        s_select = sem("s_select")
        s_agg = sem("s_agg")
        s_added = sem("s_added")
        s_w1 = sem("s_w1")
        s_w2 = sem("s_w2")
        s_b12 = sem("s_b12")
        s_fin = sem("s_fin")
        s_gate = sem("s_gate")
        s_gate_read = sem("s_gate_read")
        s_route = sem("s_route")
        s_route_psum = sem("s_route_psum")
        s_route_done = sem("s_route_done")
        s_xtile_dram = sem("s_xtile_dram")
        s_xtile_row = [sem(f"s_xtile_row{i}") for i in range(2)]
        s_fxn = sem("s_fxn")
        s_row = sem("s_row")
        s_spill = sem("s_spill")
        s_reload = sem("s_reload")
        s_sent = [[sem(f"s_sent{h}_{i}") for i in range(2)] for h in range(2)]
        s_fx = [sem(f"s_fx{i}") for i in range(2)]
        s_fxt_psum = sem("s_fxt_psum")
        s_fxt = sem("s_fxt")
        s_hid_psum = sem("s_hid_psum")
        s_hid = sem("s_hid")
        s_hidt_psum = sem("s_hidt_psum")
        s_hidt = sem("s_hidt")
        s_fy_psum = sem("s_fy_psum")
        s_fy = sem("s_fy")
        s_fy_out = [sem(f"s_fy_out{i}") for i in range(2)]
        s_y_out = [sem(f"s_y_out{i}") for i in range(2)]
        s_back_1 = sem("s_back_1")
        s_sum_1 = sem("s_sum_1")
        s_out_1 = sem("s_out_1")
        s_back = [sem(f"s_back{i}") for i in range(4)]
        s_spare_back = sem("s_spare_back")
        s_numbers = sem("s_numbers")
        s_sum = sem("s_sum")
        s_out = [sem(f"s_out{i}") for i in range(4)]

        hot_places = [onehot[:, :, :, :], base[:, :, :].bitcast(BF16).rearrange("p b t -> p (b t)").rearrange(
            "p (c b t) -> p c b t", c=2, b=NB)]
        spare = acc[:, 0:2 * SPARE, :]
        moving = [hid[:, :, :].rearrange("p s (u c) -> p s u c", c=C), spare.rearrange("p (s u) c -> p s u c", u=2)]
        LAST_SLOTS = 4
        back = w1[:, 0:LAST_SLOTS, :, :].rearrange("p s a n -> p s (a n)").rearrange("p s (u k c) -> p s u k c", u=2, k=2)
        spare_back = w1[:, LAST_SLOTS:LAST_SLOTS + SPARE, :, :].rearrange("p s a n -> p s (a n)").rearrange(
            "p s (u k c) -> p s u k c", u=2, k=2)
        result = w1[:, LAST_SLOTS + SPARE:EXPERTS, :, :].rearrange("p s a n -> p (s a n)").rearrange(
            "p (s u c) -> p s u c", u=2, c=C)

        block = whole.enter_context(nc.Block())
        full = E // EL
        wide = full // 16 * 16
        edge_parts = [(0, wide), (wide, full)] if full > wide else [(0, wide)]
        edge_parts = [(a, b) for a, b in edge_parts if b > a]
        rest = E - full * EL
        x_full = x[0:(NB - 1) * P, :].rearrange("(b p) c -> p b c", p=P)

        XCUT = [0, NB // 4, NB // 2, NB - 1]
        N_EDGE_LOADS = 3 * (len(edge_parts) + (1 if rest else 0))

        @block.sync
        def _(sp):
            sp.wait_ge(s_const, 1)
            for a, b in edge_parts:
                for tile, arr in ((src_i, src), (dst_i, dst), (w_in, edge_weight.bitcast(I32))):
                    sp.dma_start(tile[a:b, 0:EL], arr[a * EL:b * EL].rearrange("(p t) -> p t", t=EL)).then_inc(s_edges, 16)
            if rest:
                for tile, arr in ((src_i, src), (dst_i, dst), (w_in, edge_weight.bitcast(I32))):
                    sp.dma_start(tile[full:full + 1, 0:rest], arr[full * EL:E].rearrange("(a n) -> a n", a=1)).then_inc(s_edges, 16)
            sp.wait_ge(s_const, 2)
            for a, b in zip(XCUT[:-1], XCUT[1:]):
                sp.dma_start(acc[:, a:b, :], x_full[:, a:b, :]).then_inc(s_x, 16)
            sp.dma_start(acc[0:LAST, NB - 1, :], x[(NB - 1) * P:N, :]).then_inc(s_x, 16)
            sp.dma_start(w_nat[:, 0:2, :], mix_Wq.rearrange("(a p) c -> p a c", p=P)).then_inc(s_wload, 16)
            sp.dma_start(w_nat[:, 2:6, :], mix_Wkv.rearrange("(a p) c -> p a c", p=P)).then_inc(s_wload, 16)
            sp.dma_start(w_nat[:, 6:8, :], mix_Wproj.rearrange("(a p) c -> p a c", p=P)).then_inc(s_wload, 16)
            sp.dma_start(w_cat[:, :, 0:C], gnn_W.rearrange("(k p) n -> p k n", p=P)).then_inc(s_wload, 16)
            sp.dma_start(bias_in[:, 0, :], gnn_b.partition_broadcast(P)).then_inc(s_wload, 16)
            sp.dma_start(bias_in[:, 1, :], mix_bproj.partition_broadcast(P)).then_inc(s_wload, 16)
            lrow = edge_list.rearrange("(p t) c -> p (t c)", p=P)
            zcols = 4 * C
            nz = 0
            for a in range(0, 3 * TT, zcols):
                b = min(a + zcols, 3 * TT)
                sp.dma_start(lrow[:, a:b], zeros[:, 0:b - a].bitcast(I32)).then_inc(s_zeroed, 16)
                nz += 1
            for half in range(2):
                sp.dma_start(x_sorted[half].rearrange("(p t) c -> p t c", p=P),
                             zeros[:, 0:C].unsqueeze(1).to_broadcast([P, TX[half], C])).then_inc(s_blank, 16)
            sp.dma_start(number_sorted.rearrange("(p t) a -> p (t a)", p=P), number_fill[:, :]).then_inc(s_blank, 16)
            sp.wait_ge(s_tile_out, 1)
            sp.dma_start(tile_dram.rearrange("(p t) -> p t", p=P), tile_i[:, :]).then_inc(s_tile_dram, 16)
            sp.wait_ge(s_tile_dram, 16)
            sp.dma_start(tile_row[:, :], tile_dram.rearrange("(a n) -> a n", a=1)).then_inc(s_tile_row, 16)
            sp.wait_ge(s_record, 3)

            def stage(first_tile, slot):
                sp.dma_start(scatter_stage[:, slot, :, :], record[:, ds(first_tile, CH), :]).then_inc(s_staged[slot], 16)
            for slot in range(2):
                sp.wait_ge(s_pos, slot + 1)
                stage(slot * CH, slot)
            with sp.Fori(1, SCATTERS) as m:
                for slot in range(2):
                    first_tile = sp.snap(m * (2 * CH) + slot * CH)
                    sp.wait_ge(s_pos, m * 2 + (slot + 1))
                    sp.sem_inc(s_passed, 1)
                    sp.wait_ge(s_scattered[slot], m * (16 * CH))
                    stage(first_tile, slot)

            for slot in range(2):
                sp.wait_ge(s_scattered[slot], 16 * (CH * (SCATTERS - 1) + LAST_CHUNKS[slot]))
            lset = edge_list.rearrange("(p t) c -> p t c", p=P)

            def stage_list(first_tile, slot):
                sp.dma_start(gather_stage[:, slot, :, :], lset[:, ds(first_tile, SET), :]).then_inc(s_list[slot], 16)
            for slot in range(RING):
                stage_list(slot * SET, slot)
            with sp.Fori(1, TURNS_G) as m:
                for slot in range(RING):
                    first_tile = sp.snap((m * RING + slot) * SET)
                    sp.wait_ge(s_agg, m * RING + (slot - RING + 1))
                    stage_list(first_tile, slot)
            for slot in range(TSETS % RING):
                sp.wait_ge(s_agg, (TURNS_G - 1) * RING + slot + 1)
                stage_list((TURNS_G * RING + slot) * SET, slot)

            sp.wait_ge(s_added, TSETS)
            sp.dma_start(wg[:, :, :], ffn_Wg.rearrange("(k p) n -> p k n", p=P)).then_inc(s_fin, 16)
            sp.dma_start(gate_b[:, 0, :], ffn_bg.partition_broadcast(P)).then_inc(s_fin, 16)
            sp.dma_start(gate_b[:, 1, :], ffn_bias.partition_broadcast(P)).then_inc(s_fin, 16)
            sp.dma_start(acc_dram, spare.rearrange("p b c -> p (b c)")).then_inc(s_spill, 16)
            sp.dma_start(w1[:, :, :, :], ffn_W1.rearrange("e (k p) n -> p e k n", p=P)).then_inc(s_w1, 16)
            sp.dma_start(w2[:, :, :, :], ffn_W2.rearrange("e (k p) n -> p e k n", p=P)).then_inc(s_w2, 16)
            def store_experts(half):
                sp.dma_start(xtile_dram[half].rearrange("a (p t) -> p a t", p=P), xtile_i[:, :, :]).then_inc(s_xtile_dram, 16)
                sp.wait_ge(s_xtile_dram, half * 16 + 16)

            def load_experts(half):
                sp.dma_start(xtile_row[:, :, half * TX[0]:half * TX[0] + TX[half]],
                             xtile_dram[half, :, 0:TX[half]].unsqueeze(0)).then_inc(s_xtile_row[half], 16)
            sp.wait_ge(s_route_done, 1)
            store_experts(0)
            load_experts(0)

            x_tiles = [x_sorted[half].rearrange("(t p) c -> t p c", p=P) for half in range(2)]

            def load_x(half, t, slot):
                sp.dma_start(fx[:, slot, :], x_tiles[half][ds(t, 1), :, :].rearrange("a p c -> p (a c)")).then_inc(s_fx[slot], 16)

            def all_sent(half):
                for slot in range(2):
                    sp.wait_ge(s_sent[half][slot], (HALF_PAIRS[half] + 1 - slot) // 2 * (64 + 64 * half))
            all_sent(0)
            for slot in range(2):
                load_x(0, slot, slot)
            sp.wait_ge(s_route_done, 2)
            store_experts(1)
            sp.dma_start(b12[:, :, 0:HID], ffn_b1.partition_broadcast(P)).then_inc(s_b12, 16)
            sp.dma_start(b12[:, :, HID:HID + C], ffn_b2.partition_broadcast(P)).then_inc(s_b12, 16)
            load_experts(1)
            with sp.Fori(1, TX[0] // 2) as m:
                for slot in range(2):
                    tile = sp.snap(m * 2 + slot)
                    sp.wait_ge(s_fxt_psum, m * 2 + (slot - 1))
                    load_x(0, tile, slot)
            all_sent(1)
            sp.dma_start(numbers[:, :], number_sorted.rearrange("(p t) a -> p (t a)", p=P)).then_inc(s_numbers, 16)
            with sp.Fori(TX[0] // 2, TXS // 2) as m:
                for slot in range(2):
                    tile = sp.snap(m * 2 + (slot - TX[0]))
                    sp.wait_ge(s_fxt_psum, m * 2 + (slot - 1))
                    load_x(1, tile, slot)
            sp.wait_ge(s_out_1, 16 * BACK)
            sp.dma_start(spare.rearrange("p b c -> p (b c)"), acc_dram).then_inc(s_reload, 16)

            y_pairs = y_token[0:2 * NB2 * P, :].rearrange("(g u p k) c -> g p u (k c)", u=2, p=P, k=2)
            for slot in range(2):
                sp.wait_ge(s_y_out[slot], TX[1] // 2 * 16)

            def load_back(i, slot):
                sp.dma_start(back[:, slot, :, :, :].rearrange("p u k c -> p u (k c)"),
                             y_pairs[ds(i, 1), :, :, :].rearrange("a p u n -> p (a u) n")).then_inc(s_back[slot], 16)
            for slot in range(LAST_SLOTS):
                load_back(slot, slot)
            with sp.Fori(1, HALF_PAIRS[1] // LAST_SLOTS) as m:
                for slot in range(LAST_SLOTS):
                    i = sp.snap(m * LAST_SLOTS + slot)
                    sp.wait_ge(s_sum, m * LAST_SLOTS + (slot + 1 - LAST_SLOTS))
                    load_back(i, slot)

        @block.gpsimd
        def _(pool):
            steps = Steps(pool, s_pool)
            pool.memset(src_i[:, 0:EL], NB * P - 1)
            if ET > EL:
                pool.memset(src_i[:, EL:ET], NB * P)
            pool.memset(dst_i[:, :], 0)
            pool.memset(w_in[:, :], 0).then_inc(s_const, 1)
            pool.memset(acc[:, NB - 1, :], 0.0)
            pool.iota(number_fill[:, :], [[0, TX[1] // 4], [P, 4]], base=2 * NB2 * P, channel_multiplier=1)
            pool.memset(zeros[:, :], 0.0).then_inc(s_const, 1)
            pool.iota(iota_b[:, :, :], [[1, NB], [0, CH]], base=0, channel_multiplier=0, allow_small_or_imprecise_dtypes=True)
            pool.iota(iota_t[:, :], [[1, TPP]], base=0, channel_multiplier=TPP, allow_small_or_imprecise_dtypes=True)
            pool.iota(iota_n[:, :], [[1, P]], base=0, channel_multiplier=0, allow_small_or_imprecise_dtypes=True)
            pool.memset(eps_col[:, :], EPS)
            steps.done(pool.memset(ones_bf[:, :], 1.0))
            steps.done(pool.memset(ident[:, :], 0.0))
            steps.done(pool.memset(head_mask[:, :], 1.0))
            steps.done(pool.memset(row_ok[:, :, :], 1.0))
            steps.settle()
            pool.affine_select(out=tri[:, :], in_=ones_bf[:, :], pattern=[[1, P]], compare_op=ALU.is_gt,
                               fill=0.0, base=0, channel_multiplier=-1)
            pool.affine_select(out=tri_rest[:, :], in_=ones_bf[:, :], pattern=[[-1, P]], compare_op=ALU.is_ge,
                               fill=0.0, base=0, channel_multiplier=1)
            pool.affine_select(out=row_ok[:, 1, :], in_=row_ok[:, 1, :], pattern=[[0, P]], compare_op=ALU.is_ge,
                               fill=0.0, base=LAST - 1, channel_multiplier=-1)
            heads = head_mask[:, :].rearrange("p (h d) -> p h d", d=HD)
            steps.done(pool.affine_select(out=heads, in_=heads, pattern=[[-HD, P // HD], [0, HD]],
                                          compare_op=ALU.is_ge, fill=0.0, base=0, channel_multiplier=1))
            steps.settle()
            pool.affine_select(out=heads, in_=heads, pattern=[[HD, P // HD], [0, HD]],
                               compare_op=ALU.is_ge, fill=0.0, base=HD - 1, channel_multiplier=-1)
            pool.affine_select(out=ident[:, :], in_=ident[:, :], pattern=[[-1, P]], compare_op=ALU.not_equal,
                               fill=1.0, base=0, channel_multiplier=1).then_inc(s_const, 1)
            pool.wait_ge(s_edges, 16 * N_EDGE_LOADS)
            pool.tensor_copy(record[:, :, 1], dst_i[:, :]).then_inc(s_record, 1)
            pool.tensor_copy(record[:, :, 3], w_in[:, :]).then_inc(s_record, 1)

            n_zero = -(-3 * TT // (4 * C))
            def pass_gate():
                pool.sem_inc(s_passed, 1)
            pool.wait_ge(s_zeroed, 16 * n_zero)

            def scatter_chunk(turn, slot, tiles=CH):
                pool.wait_ge(s_staged[slot], turn * 16 + 16)
                pass_gate()
                for j in range(tiles):
                    pool.indirect_dma_start(
                        out=edge_list, out_offset=Offset(ap=scatter_stage[:, slot, j, 0:1], axis=0),
                        in_=scatter_stage[:, slot, j, 1:4], in_offset=None).then_inc(s_scattered[slot], 16)
            with pool.Fori(0, SCATTERS - 1) as m:
                for slot in range(2):
                    scatter_chunk(m, slot)
            for slot in range(2):
                scatter_chunk(SCATTERS - 1, slot, LAST_CHUNKS[slot])

            pool.wait_ge(s_hq_out[0], 32 * (PAIRS // 2 + 1))
            pool.wait_ge(s_hq_out[1], 32 * (PAIRS // 2))
            pool.wait_ge(s_mix_added, PAIRS)

            def gather_set(slot):
                pass_gate()
                for j in range(SET):
                    pool.indirect_dma_start(
                        out=message[:, slot, j, :], out_offset=None, in_=h_table,
                        in_offset=Offset(ap=gather_stage[:, slot, j, 0:1], axis=0)).then_inc(s_message[slot], 16)
            for slot in range(RING):
                pool.wait_ge(s_list[slot], 16)
                gather_set(slot)
            with pool.Fori(1, TURNS_G) as m:
                for slot in range(RING):
                    pool.wait_ge(s_list[slot], m * 16 + 16)
                    gather_set(slot)
            for slot in range(TSETS % RING):
                pool.wait_ge(s_list[slot], TURNS_G * 16 + 16)
                gather_set(slot)

            pool.wait_ge(s_added, TSETS)
            pool.iota(iota_e[:, 0, :], [[1, EXPERTS]], base=0, channel_multiplier=0, allow_small_or_imprecise_dtypes=True)
            pool.iota(iota_e[:, 1, :], [[1, EXPERTS]], base=-EXPERTS, channel_multiplier=0, allow_small_or_imprecise_dtypes=True)
            pool.iota(iota_x[:, :], [[1, XPP]], base=0, channel_multiplier=XPP,
                      allow_small_or_imprecise_dtypes=True).then_inc(s_const, 1)
            steps.done(pool.iota(number[:, :, :], [[2 * P, NB2], [1, 2]], base=0, channel_multiplier=2))

            def stage_pos(pair, slot):
                steps.done(pool.tensor_copy(pos_stage[:, slot, :, :], token_pos[:, ds(pair * 2, 2), :]))

            def scatter_rows(half, slot):
                for u in range(2):
                    for k in range(2):
                        pool.indirect_dma_start(
                            out=x_sorted[half], out_offset=Offset(ap=pos_stage[:, slot, u, k:k + 1], axis=0),
                            in_=moving[half][:, slot, u, :], in_offset=None).then_inc(s_sent[half][slot], 16)

            def send_1(i, turn, slot, first=False):
                if not first:
                    pool.wait_ge(s_sent[0][slot], turn * 64)
                stage_pos(i, slot)
                steps.settle()
                pool.wait_ge(s_row, i + 1)
                pass_gate()
                scatter_rows(0, slot)

            def send_2(i, turn, slot, first=False):
                if not first:
                    pool.wait_ge(s_sent[1][slot], turn * 128)
                pair = i + HALF_BEGIN[1]
                stage_pos(pair, slot)
                steps.done(pool.tensor_copy(number_pos[:, slot, 0, :, :], token_pos_2[:, ds(i * 2, 2), :]))
                steps.done(pool.tensor_copy(number_pos[:, slot, 1, :, :], number[:, ds(i * 2, 2), :]))
                rows = moving[1][:, slot, :, :]
                steps.done(pool.tensor_tensor(rows, acc[:, ds(pair * 2, 2), :],
                                              row_mean[:, ds(pair * 2, 2), 0:1].to_broadcast([P, 2, C]), ALU.subtract))
                steps.settle()
                steps.done(pool.tensor_tensor(rows, rows, rstd[:, ds(pair * 2, 2)].unsqueeze(2).to_broadcast([P, 2, C]), ALU.mult))
                steps.settle()
                pass_gate()
                scatter_rows(1, slot)
                for u in range(2):
                    for k in range(2):
                        pool.indirect_dma_start(
                            out=number_sorted, out_offset=Offset(ap=number_pos[:, slot, 0, u, k:k + 1], axis=0),
                            in_=number_pos[:, slot, 1, u, k:k + 1], in_offset=None).then_inc(s_sent[1][slot], 16)

            def send_half(half, send, per_pair):
                n = HALF_PAIRS[half]
                pool.wait_ge(s_route_done, half + 1)
                for slot in range(2):
                    send(slot, 0, slot, first=True)
                with pool.Fori(1, n // 2) as m:
                    steps.enter(m - 1, 2 * per_pair)
                    for slot in range(2):
                        send(m * 2 + slot, m, slot)
                    steps.leave(n // 2 - 1)
                if n % 2:
                    send(n - 1, n // 2, 0)
            pool.wait_ge(s_blank, 48)
            send_half(0, send_1, 1)
            for slot in range(2):
                pool.wait_ge(s_sent[0][slot], (HALF_PAIRS[0] + 1 - slot) // 2 * 64)
            pool.wait_ge(s_spill, 16)
            send_half(1, send_2, 5)

            out_full = out[0:(PAIRS - 1) * 2 * P, :].rearrange("(g u p) c -> g p u c", u=2, p=P)
            for slot in range(2):
                pool.wait_ge(s_sent[1][slot], HALF_PAIRS[1] // 2 * 128)
            pool.wait_ge(s_numbers, 16)

            def stage_numbers(group):
                if not isinstance(group, int) or group > G1:
                    for slot in range(2):
                        pool.wait_ge(s_y_out[slot], group * 32 - G1 * 32)
                steps.done(pool.tensor_copy(number_stage[:, :], numbers[:, ds(group * 4 - TX[0], 4)]))
                steps.settle()

            def scatter_y(group, j):
                pool.wait_ge(s_fy, group * 4 + (j + 1))
                pass_gate()
                pool.indirect_dma_start(
                    out=y_token, out_offset=Offset(ap=number_stage[:, j:j + 1], axis=0),
                    in_=fy[:, j % 2, :], in_offset=None).then_inc(s_y_out[j % 2], 16)

            def fetch_1(i):
                stage_pos(i + SPARE, 0)
                steps.settle()
                pass_gate()
                for k in range(2):
                    for u in range(2):
                        pool.indirect_dma_start(
                            out=spare[:, k * 2 + u, :], out_offset=None, in_=y_sorted[0],
                            in_offset=Offset(ap=pos_stage[:, 0, u, k:k + 1], axis=0)).then_inc(s_back_1, 16)

            def store_1(i):
                at = pool.snap(i + SPARE)
                pool.wait_ge(s_sum_1, i + 1)
                pass_gate()
                pool.dma_start(out_full[ds(at, 1), :, :, :].rearrange("a p u c -> p (a u) c"),
                               spare[:, 0:2, :]).then_inc(s_out_1, 16)

            for slot in range(2):
                pool.wait_ge(s_fy_out[slot], TX[0] // 2 * 16)
            stage_numbers(G1)
            for j in range(4):
                scatter_y(G1, j)
            fetch_1(0)
            with pool.Fori(1, BACK) as i:
                steps.enter(i - 1, 2)
                stage_numbers(i + G1)
                for j in range(3):
                    scatter_y(i + G1, j)
                store_1(i - 1)
                scatter_y(i + G1, 3)
                pool.wait_ge(s_out_1, i * 16)
                fetch_1(i)
                steps.leave(BACK - 1)
            stage_numbers(G1 + BACK)
            for j in range(3):
                scatter_y(G1 + BACK, j)
            store_1(BACK - 1)
            scatter_y(G1 + BACK, 3)
            with pool.Fori(G1 + BACK + 1, GROUPS) as group:
                steps.enter(group - (G1 + BACK + 1), 1)
                stage_numbers(group)
                for j in range(4):
                    scatter_y(group, j)
                steps.leave(GROUPS - (G1 + BACK + 1))

            for slot in range(2):
                pool.wait_ge(s_y_out[slot], TX[1] // 2 * 16)
            for pair in range(SPARE):
                stage_pos(pair, pair)
                steps.settle()
                for u in range(2):
                    for k in range(2):
                        pool.indirect_dma_start(
                            out=spare_back[:, pair, u, k, :], out_offset=None, in_=y_sorted[0],
                            in_offset=Offset(ap=pos_stage[:, pair, u, k:k + 1], axis=0)).then_inc(s_spare_back, 16)

        @block.scalar
        def _(act):
            steps = Steps(act, s_act)
            for i in range(4):
                act.wait_ge(s_wt_psum, i + 1)
                ps = bank[2 + i][:, :].rearrange("p (k a n) -> p k a n", k=KC, a=2)
                into = [w_cat[:, :, 3 * C:4 * C], w_cat[:, :, C:2 * C], w_cat[:, :, 2 * C:3 * C], wp_t[:, :, :]][i]
                act.activation(into.rearrange("p k (a n) -> p k a n", a=2), ps, ACT.Copy).then_inc(s_wt, 1)

            act.wait_ge(s_var, TURNS)
            act.activation(rstd[:, :], row_mean[:, :, 1], ACT.Sqrt, bias=eps_col[:, :]).then_inc(s_std, 1)

            def project(g, slot, first=False):
                act.wait_ge(s_xt_psum, g + 1)
                act.activation(xn_t[:, slot, :, :].rearrange("p k n -> p (k n)"), bank[2][:, :], ACT.Copy).then_inc(s_xt, 1)
                if not first:
                    for_slot = (g - slot) * 16
                    act.wait_ge(s_hq_out[slot], for_slot)
                    act.wait_ge(s_ctx, g - 1)
                for u in range(2):
                    act.wait_ge(s_proj, g * 2 + (u + 1))
                    hk, vq = bank[3 + 2 * u], bank[4 + 2 * u]
                    act.activation(h_out[:, slot, u, :], hk[:, 0:C], ACT.Copy)
                    act.activation(v_sb[:, slot, u, :], vq[:, 0:C], ACT.Copy)
                    if u == 0 and not first:
                        act.wait_ge(s_kq, g * 2)
                    elif u == 0 and slot == 1:
                        act.wait_ge(s_kq, 2)
                    act.activation(exp_kq[:, 0, u, :], hk[:, C:2 * C], ACT.Exp)
                    act.activation(exp_kq[:, 1, u, :], vq[:, C:2 * C], ACT.Exp)
                    act.activation(relu_kq[:, 0, u, :], hk[:, C:2 * C], ACT.Relu)
                    act.activation(relu_kq[:, 1, u, :], vq[:, C:2 * C], ACT.Relu).then_inc(s_proj_read, 1)

            h_pairs = h_table.rearrange("(g u p) c -> g p u c", u=2, p=P)

            def store(g, slot):
                act.wait_ge(s_proj_read, g * 2 + 2)
                act.dma_start(h_pairs[ds(g, 1), :, :, :].rearrange("a p u c -> p (a u) c"),
                              h_out[:, slot, :, :]).then_inc(s_hq_out[slot], 16)
                act.wait_ge(s_kq, g * 2 + 2)
                act.dma_start(q_dram[ds(g, 1), :, :].rearrange("a p n -> p (a n)"),
                              q_out[:, slot, :, :].rearrange("p u c -> p (u c)")).then_inc(s_hq_out[slot], 16)
            for g in range(2):
                project(g, g, first=True)
                store(g, g)
            with act.Fori(1, PAIRS // 2) as m:
                for slot in range(2):
                    project(m * 2 + slot, slot)
                    store(m * 2 + slot, slot)
            project(PAIRS - 1, 0)
            store(PAIRS - 1, 0)

            def bring_q(g, slot):
                act.dma_start(q_out[:, slot, :, :].rearrange("p u c -> p (u c)"),
                              q_dram[ds(g, 1), :, :].rearrange("a p n -> p (a n)")).then_inc(s_q_in[slot], 16)

            def copy_qt(g, slot, first=False):
                act.wait_ge(s_qt_psum, g + 1)
                if not first:
                    act.wait_ge(s_mix, g - 1)
                act.activation(xn_t[:, slot, :, :].rearrange("p k n -> p (k n)"), bank[2][:, :], ACT.Copy).then_inc(s_qt, 1)
            for s in range(2):
                act.wait_ge(s_hq_out[s], 32 * (PAIRS // 2 + (PAIRS % 2 if s == 0 else 0)))
            for g in range(2):
                bring_q(g, g)

            def q_turn(g, slot, first=False):
                copy_qt(g - 2, slot, first)
                act.wait_ge(s_qn, g - 1)
                bring_q(g, slot)
            for slot in range(2):
                q_turn(2 + slot, slot, first=True)
            with act.Fori(2, PAIRS // 2) as m:
                for slot in range(2):
                    q_turn(m * 2 + slot, slot)
            copy_qt(PAIRS - 3, 0)
            act.wait_ge(s_qn, PAIRS - 2)
            bring_q(PAIRS - 1, 0)
            copy_qt(PAIRS - 2, 1)
            copy_qt(PAIRS - 1, 0)

            def root(turn):
                act.wait_ge(s_var, turn + (TURNS + 1))
                act.activation(rstd[:, ds(turn * TB, TB)], row_mean[:, ds(turn * TB, TB), 1], ACT.Sqrt,
                               bias=eps_col[:, :]).then_inc(s_std, 1)

            def gate_copies(turn, first=False, last=False):
                for j in range(TURN):
                    g = turn * TURN + j
                    act.wait_ge(s_xt_psum, g + (PAIRS + 1))
                    if not first or j > 1:
                        act.wait_ge(s_gate, g if j == 0 else g - 1)
                    act.activation(fxn_t[:, j % 2, :, :].rearrange("p k n -> p (k n)"), bank[j % 2][:, :], ACT.Identity).then_inc(s_xt, 1)
                    if j == TURN - 3 and not last:
                        root(turn + 1)

            def softmax_exp(half):
                act.wait_ge(s_route, half * 2 + 1)
                blocks = slice(HALF_BEGIN[half] * 2, (HALF_BEGIN[half] + HALF_PAIRS[half]) * 2)
                act.activation(top_w[:, 1, blocks], small[:, 4, 0:2 * HALF_PAIRS[half]], ACT.Exp).then_inc(s_route, 1)
            root(0)
            gate_copies(0, first=True)
            with act.Fori(1, TURNS_1) as m:
                gate_copies(m)
            softmax_exp(0)
            with act.Fori(TURNS_1, TURNS - 1) as m:
                gate_copies(m)
            gate_copies(TURNS - 1, last=True)
            softmax_exp(1)

            y_tiles = y_sorted[0].rearrange("(t p) c -> t p c", p=P)

            def copy_x(t, slot, first=False):
                act.wait_ge(s_fxt_psum, t + 1)
                if not first:
                    act.wait_ge(s_hid_psum, t - 1)
                act.activation(fx_t[:, slot, :, :].rearrange("p k n -> p (k n)"), bank[slot][:, 0:C], ACT.Copy).then_inc(s_fxt, 1)

            def hidden(t, slot, first=False):
                act.wait_ge(s_hidt_psum, t + 1)
                if not first:
                    act.wait_ge(s_fy_psum, t - 1)
                act.activation(hid_t[:, slot, :, :].rearrange("p k n -> p (k n)"), bank[4 + slot][:, :], ACT.Relu).then_inc(s_hidt, 1)

            def store_y(t, slot):
                act.wait_ge(s_fy, t + 1)
                act.dma_start(y_tiles[ds(t, 1), :, :].rearrange("a p c -> p (a c)"),
                              fy[:, slot, :]).then_inc(s_fy_out[slot], 16)

            def expert_pair(half, t, first=False, last=False):
                hidden(t, 0, first)
                if not last:
                    copy_x(t + 2, 0)
                    copy_x(t + 3, 1)
                hidden(t + 1, 1, first)
                if half == 0:
                    store_y(t, 0)
                    store_y(t + 1, 1)
            copy_x(0, 0, first=True)
            copy_x(1, 1, first=True)
            expert_pair(0, 0, first=True)
            with act.Fori(1, TX[0] // 2) as m:
                expert_pair(0, m * 2)
            with act.Fori(TX[0] // 2, TXS // 2 - 1) as m:
                expert_pair(1, m * 2)
            expert_pair(1, TXS - 2, last=True)

            out_full = out[0:(PAIRS - 1) * 2 * P, :].rearrange("(g u p) c -> g p u c", u=2, p=P)

            def store_out(pair, i, slot):
                act.wait_ge(s_sum, i + 1)
                act.dma_start(out_full[ds(pair, 1), :, :, :].rearrange("a p u c -> p (a u) c"),
                              result[:, slot, :, :]).then_inc(s_out[slot], 16)
            n = HALF_PAIRS[1] // LAST_SLOTS
            with act.Fori(0, n - 1) as m:
                for slot in range(LAST_SLOTS):
                    store_out(m * LAST_SLOTS + (slot + HALF_BEGIN[1]), m * LAST_SLOTS + slot, slot)
            for slot in range(LAST_SLOTS - 1):
                store_out(PAIRS - LAST_SLOTS + slot, HALF_PAIRS[1] - LAST_SLOTS + slot, slot)
            act.wait_ge(s_sum, HALF_PAIRS[1])
            end = LAST_SLOTS - 1
            act.dma_start(out[(NB - 2) * P:(NB - 1) * P, :], result[:, end, 0, :]).then_inc(s_out[end], 16)
            act.dma_start(out[(NB - 1) * P:N, :], result[0:LAST, end, 1, :]).then_inc(s_out[end], 16)
            for pair in range(SPARE):
                store_out(pair, HALF_PAIRS[1] + pair, pair)
            for slot in range(LAST_SLOTS):
                act.wait_ge(s_out[slot], 16 * (n + (1 if slot < SPARE or slot == end else 0)))

        @block.tensor
        def _(pe):
            pe.wait_ge(s_const, 3)
            def counts(i):
                return bank[i][:, 0:HB * CH]

            def hot(slot, half):
                return onehot[:, slot, half * HB:(half + 1) * HB, :].rearrange("p b t -> p (b t)")

            def count(duo, place, first=False):
                pe.wait_ge(s_hots, duo + 1)
                for c in range(2):
                    for half in range(2):
                        last = nc.tensor.matmul(counts(half), ones_bf[:, :],
                                                hot_places[place][:, c, half * HB:(half + 1) * HB, :].rearrange("p b t -> p (b t)"),
                                                start=first and c == 0, stop=True, skip_group_check=True)
                last.then_inc(s_hots_read, 1)
            count(0, 0, first=True)
            count(1, 1)
            with pe.Fori(1, CHUNKS // 4) as m:
                for place in range(2):
                    count(m * 2 + place, place)
            pe.wait_ge(s_base, 1)
            for half in range(2):
                nc.tensor.matmul(counts(half), ident[:, :],
                                 base[:, half * HB:(half + 1) * HB, :].rearrange("p b t -> p (b t)"),
                                 start=True, stop=True, skip_group_check=True)

            def ranks(chunk, slot):
                pe.wait_ge(s_hot, chunk + 1)
                for half in range(2):
                    nc.tensor.matmul(counts(half), tri[:, :], hot(slot, half), start=False, stop=True,
                                     skip_group_check=True).then_inc(s_rank, 1)
                for half in range(2):
                    pe.wait_ge(s_rank_read, chunk * 2 + (half + 1))
                    last = nc.tensor.matmul(counts(half), tri_rest[:, :], hot(slot, half), start=False, stop=True,
                                            skip_group_check=True)
                last.then_inc(s_rank_next, 1)
            with pe.Fori(0, CHUNKS // 2) as m:
                for slot in range(2):
                    ranks(m * 2 + slot, slot)

            pe.wait_ge(s_wload, 16 * 6)
            for i in range(4):
                for k in range(KC):
                    for a in range(2):
                        last = nc.tensor.transpose(bank[2 + i][:, (k * 2 + a) * P:(k * 2 + a + 1) * P],
                                                   w_nat[:, 2 * i + a, k * P:(k + 1) * P], ident[:, :])
                last.then_inc(s_wt_psum, 1)
            pe.wait_ge(s_wt, 4)

            def transpose_pair(source, ps, signal):
                for k in range(KC):
                    for u in range(2):
                        last = nc.tensor.transpose(ps[:, (k * 2 + u) * P:(k * 2 + u + 1) * P],
                                                   source[:, u, k * P:(k + 1) * P], ident[:, :])
                last.then_inc(signal, 1)

            def normed(g, first=False):
                pe.wait_ge(s_xn, g + 1)
                if not first:
                    pe.wait_ge(s_xt, g)
                transpose_pair(xn, bank[2], s_xt_psum)

            def project(g, slot, first=False):
                pe.wait_ge(s_xt, g + 1)
                for u in range(2):
                    if not first:
                        pe.wait_ge(s_proj_read, g * 2 + (u - 1))
                    for cols, ps in ((0, bank[3 + 2 * u]), (2 * C, bank[4 + 2 * u])):
                        for k in range(KC):
                            last = nc.tensor.matmul(ps[:, :], xn_t[:, slot, k, u * P:(u + 1) * P],
                                                    w_cat[:, k, cols:cols + 2 * C], start=(k == 0), stop=(k == KC - 1))
                    last.then_inc(s_proj, 1)

            def context(g, slot, first=False, final=False):
                pe.wait_ge(s_kq, g * 2 + 1)
                for u in range(2):
                    ok = row_ok[:, 1 if final and u == 1 else 0, :]
                    for h in range(KC):
                        nc.tensor.matmul(bank[7][:, h * P:(h + 1) * P], v_sb[:, slot, u, h * P:(h + 1) * P],
                                         k_act[:, slot, u, h * P:(h + 1) * P],
                                         start=(first and u == 0 and h == 0), stop=True, skip_group_check=True)
                    last = nc.tensor.matmul(bank[7][:, C:2 * C], ok, k_act[:, slot, u, :], start=False, stop=True,
                                            skip_group_check=True)
                last.then_inc(s_ctx, 1)
            normed(0, first=True)
            normed(1)
            project(0, 0, first=True)
            normed(2)
            project(1, 1)
            context(0, 0, first=True)
            with pe.Fori(1, PAIRS // 2) as m:
                for slot in range(2):
                    g = m * 2 + slot
                    normed(g + 1)
                    project(g, slot)
                    context(g - 1, 1 - slot)
            project(PAIRS - 1, 0)
            context(PAIRS - 2, 1)
            context(PAIRS - 1, 0, final=True)

            pe.wait_ge(s_ctx_sb, 1)
            for h in range(KC):
                last = nc.tensor.matmul(bank[5][:, h * C:(h + 1) * C], ctx_t[:, h, :], wp_t[:, h, :],
                                        start=True, stop=True)
            last.then_inc(s_mixw_psum, 1)

            def q_transpose(g, first=False):
                pe.wait_ge(s_qn, g + 1)
                if not first:
                    pe.wait_ge(s_qt, g)
                transpose_pair(xn, bank[2], s_qt_psum)

            def mix(g, slot, first=False):
                pe.wait_ge(s_qt, g + 1)
                if not first:
                    pe.wait_ge(s_mix_added, g - 1)
                for u in range(2):
                    ps = bank[3 + slot][:, u * C:(u + 1) * C]
                    for k in range(KC):
                        last = nc.tensor.matmul(ps, xn_t[:, slot, k, u * P:(u + 1) * P], mix_w[:, k, :],
                                                start=(k == 0), stop=(k == KC - 1))
                last.then_inc(s_mix, 1)
            pe.wait_ge(s_mixw, 1)
            q_transpose(0, first=True)
            q_transpose(1)
            mix(0, 0, first=True)
            q_transpose(2)
            mix(1, 1, first=True)
            with pe.Fori(1, PAIRS // 2) as m:
                for slot in range(2):
                    g = m * 2 + slot
                    q_transpose(g + 1)
                    mix(g, slot)
            mix(PAIRS - 1, 0)

            def aggregate(k, slot, first=False):
                pe.wait_ge(s_select, k + 1)
                if first:
                    pe.wait_ge(s_message[slot], 64)
                else:
                    pe.wait_ge(s_message[slot], (k - slot) * 16 + 64)
                if not (first and slot < 2):
                    pe.wait_ge(s_added, k - 1)
                for j in range(SET):
                    ps = bank[(slot % 2) * 2 + j // 2][:, (j % 2) * C:(j % 2 + 1) * C]
                    last = nc.tensor.matmul(ps, select[:, slot % 2, j, :], message[:, slot, j, :], start=True, stop=True)
                last.then_inc(s_agg, 1)
            for slot in range(RING):
                aggregate(slot, slot, first=True)
            with pe.Fori(1, TURNS_G) as m:
                for slot in range(RING):
                    aggregate(m * RING + slot, slot)
            for slot in range(TSETS % RING):
                aggregate(TURNS_G * RING + slot, slot)

            pe.wait_ge(s_fin, 48)

            def f_transpose(g, j, first=False):
                pe.wait_ge(s_fxn, g + 1)
                if not first:
                    pe.wait_ge(s_xt, g + (PAIRS if j == 0 else PAIRS - 1))
                transpose_pair(fxn[:, j % 2, :, :], bank[j % 2], s_xt_psum)

            def gate(g, j):
                pe.wait_ge(s_xt, g + (PAIRS + 1))
                for u in range(2):
                    for k in range(KC):
                        last = nc.tensor.matmul(bank[2][:, (j * 2 + u) * EXPERTS:(j * 2 + u + 1) * EXPERTS],
                                                fxn_t[:, j % 2, k, u * P:(u + 1) * P], wg[:, k, :],
                                                start=(k == 0), stop=(k == KC - 1))
                last.then_inc(s_gate, 1)

            def gate_turn(turn, first=False):
                g = turn * TURN
                for j in range(TURN):
                    f_transpose(g + j, j, first and j < 2)
                    if j == 1 and not first:
                        pe.wait_ge(s_gate_read, turn)
                    if j:
                        gate(g + (j - 1), j - 1)
                gate(g + (TURN - 1), TURN - 1)

            def count_tokens(half):
                pe.wait_ge(s_route, half * 2 + 1)
                cols = 2 * HALF_PAIRS[half]
                for ps, matrix in ((bank[4], tri), (bank[5], ones_bf)):
                    last = nc.tensor.matmul(ps[:, 0:cols * EXPERTS], matrix[:, :],
                                            both_bf[:, 0:cols, :].rearrange("p b e -> p (b e)"), start=True, stop=True)
                last.then_inc(s_route_psum, 1)
            gate_turn(0, first=True)
            with pe.Fori(1, TURNS_1) as m:
                gate_turn(m)
            count_tokens(0)
            with pe.Fori(TURNS_1, TURNS) as m:
                gate_turn(m)
            count_tokens(1)

            pe.wait_ge(s_w1, 16)
            pe.wait_ge(s_w2, 16)
            pe.wait_ge(s_xtile_row[0], 16)

            w1_flat = w1[:, :, :, :].rearrange("p e k n -> p (e k n)")
            w2_flat = w2[:, :, :, :].rearrange("p e k n -> p (e k n)")

            def x_transpose(t, slot, first=False):
                pe.wait_ge(s_fx[slot], t * 8 + (16 - 8 * slot))
                if not first:
                    pe.wait_ge(s_fxt, t - 1)
                for k in range(KC):
                    last = nc.tensor.transpose(bank[slot][:, k * P:(k + 1) * P], fx[:, slot, k * P:(k + 1) * P], ident[:, :])
                last.then_inc(s_fxt_psum, 1)

            def up(t, slot, expert, first=False):
                pe.wait_ge(s_fxt, t + 1)
                if not first:
                    pe.wait_ge(s_hid, t - 1)
                for k in range(KC):
                    last = nc.tensor.matmul(bank[2 + slot][:, :], fx_t[:, slot, k, :],
                                            w1_flat[:, ds(expert + k * HID, HID)],
                                            start=(k == 0), stop=(k == KC - 1))
                last.then_inc(s_hid_psum, 1)

            def hid_transpose(t, slot, first=False):
                pe.wait_ge(s_hid, t + 1)
                if not first:
                    pe.wait_ge(s_hidt, t - 1)
                for k in range(KH):
                    last = nc.tensor.transpose(bank[4 + slot][:, k * P:(k + 1) * P], hid[:, slot, k * P:(k + 1) * P], ident[:, :])
                last.then_inc(s_hidt_psum, 1)

            def down(t, slot, expert, first=False):
                pe.wait_ge(s_hidt, t + 1)
                if not first:
                    pe.wait_ge(s_fy, t - 1)
                for k in range(KH):
                    last = nc.tensor.matmul(bank[6 + slot][:, 0:C], hid_t[:, slot, k, :],
                                            w2_flat[:, ds(expert + k * C, C)],
                                            start=(k == 0), stop=(k == KH - 1))
                last.then_inc(s_fy_psum, 1)

            def expert_pair(t, experts, first=False, last=False):
                up(t, 0, experts[0], first)
                up(t + 1, 1, experts[1], first)
                hid_transpose(t, 0, first)
                if not last:
                    x_transpose(t + 2, 0)
                    x_transpose(t + 3, 1)
                hid_transpose(t + 1, 1, first)
                down(t, 0, experts[0], first)
                down(t + 1, 1, experts[1], first)

            def experts_of(name, t):
                return load_offsets(pe, name, xtile_row[:, 0, :], t, 4, (EXPERTS - 1) * KC * HID)
            x_transpose(0, 0, first=True)
            x_transpose(1, 1, first=True)
            e = experts_of("expert_first_", 0)
            expert_pair(0, e[0:2], first=True)
            expert_pair(2, e[2:4])
            def group(name, m):
                e = experts_of(name, m * 4)
                expert_pair(m * 4, e[0:2])
                expert_pair(m * 4 + 2, e[2:4])
            with pe.Fori(1, G1) as m:
                group("expert_1_", m)
            pe.wait_ge(s_xtile_row[1], 16)
            with pe.Fori(G1, GROUPS - 1) as m:
                group("expert_2_", m)
            e = experts_of("expert_last_", TXS - 4)
            expert_pair(TXS - 4, e[0:2])
            expert_pair(TXS - 2, e[2:4], last=True)

        @block.vector
        def _(dve):
            steps = Steps(dve, s_dve)
            V = nc.vector
            dve.wait_ge(s_edges, 16 * N_EDGE_LOADS)
            steps.done(V.tensor_single_scalar(record[:, :, 0], src_i[:, :], 7, ALU.logical_shift_right))
            steps.done(V.tensor_single_scalar(src_i[:, :], src_i[:, :], P - 1, ALU.bitwise_and))
            steps.settle()
            V.tensor_copy(record[:, :, 2].bitcast(F32), src_i[:, :]).then_inc(s_record, 1)
            steps.done(V.tensor_copy(block_bf[:, :], record[:, :, 0]))
            steps.settle()
            dve.wait_ge(s_const, 3)

            def one_hot(chunk, slot):
                V.tensor_tensor(onehot[:, slot, :, :],
                                block_bf[:, ds(chunk * CH, CH)].unsqueeze(1).to_broadcast([P, NB, CH]),
                                iota_b[:, :, :], ALU.is_equal).then_inc(s_hot, 1)

            def one_hots(duo, place):
                V.tensor_tensor(hot_places[place],
                                block_bf[:, ds(duo * 2 * CH, 2 * CH)].rearrange("p (c t) -> p c t", c=2).unsqueeze(2).to_broadcast([P, 2, NB, CH]),
                                iota_b[:, :, :].unsqueeze(1).to_broadcast([P, 2, NB, CH]), ALU.is_equal).then_inc(s_hots, 1)
            for place in range(2):
                one_hots(place, place)
            with dve.Fori(1, CHUNKS // 4) as m:
                for place in range(2):
                    dve.wait_ge(s_hots_read, m * 2 + (place - 1))
                    one_hots(m * 2 + place, place)
            dve.wait_ge(s_hots_read, CHUNKS // 2)
            dve.wait_ge(s_record, 3)
            for half in range(2):
                steps.done(V.tensor_copy(totals[:, half * HB:(half + 1) * HB, :].rearrange("p b t -> p (b t)"),
                                         bank[half][:, 0:HB * CH]))
            steps.settle()
            steps.done(V.tensor_reduce(scan_a[:, :], totals[:, :, :], AX, ALU.add))
            steps.settle()
            steps.done(V.tensor_scalar(scan_i[:, :], scan_a[:, :], float(P - 1), None, ALU.add))
            steps.settle()
            steps.done(V.tensor_single_scalar(scan_i[:, :], scan_i[:, :], 7, ALU.logical_shift_right))
            steps.settle()
            steps.done(V.tensor_copy(scan_a[:, :], scan_i[:, :]))
            steps.settle()
            here, there, step = scan_a, scan_b, 1
            while step < NB:
                steps.done(V.tensor_copy(there[:, 0:step], here[:, 0:step]))
                steps.done(V.tensor_tensor(there[:, step:NB], here[:, step:NB], here[:, 0:NB - step], ALU.add))
                steps.settle()
                here, there, step = there, here, 2 * step
            steps.done(V.tensor_tensor(tile_cmp[:, :, :], iota_t[:, :].unsqueeze(2).to_broadcast([P, TPP, NB]),
                                       here[:, :].unsqueeze(1).to_broadcast([P, TPP, NB]), ALU.is_ge))
            steps.done(V.memset(base[:, 0:1, 0], 0.0))
            steps.done(V.tensor_scalar(base[:, 1:NB, 0], here[:, 0:NB - 1], float(P), None, ALU.mult))
            steps.settle()
            steps.done(V.tensor_reduce(tile_f[:, :], tile_cmp[:, :, :], AX, ALU.add))
            for j in range(1, CH):
                steps.done(V.tensor_tensor(base[:, :, j], base[:, :, j - 1], totals[:, :, j - 1], ALU.add))
                steps.settle()
            V.tensor_scalar(tile_i[:, :], tile_f[:, :], float(NB - 1), float(C), ALU.min, ALU.mult).then_inc(s_tile_out, 1)
            V.engine_nop().then_inc(s_base, 1)

            def position(chunk, slot, first=False):
                if not first:
                    dve.wait_ge(s_rank_next, chunk - 1)
                one_hot(chunk, slot)

            def extract(chunk, slot):
                for half in range(2):
                    dve.wait_ge(s_rank, chunk * 2 + (half + 1))
                    part = slice(half * HB, (half + 1) * HB)
                    V.tensor_tensor(picked[:, part, :].rearrange("p b t -> p (b t)"),
                                    onehot[:, slot, part, :].rearrange("p b t -> p (b t)"),
                                    bank[half][:, 0:HB * CH], ALU.mult).then_inc(s_rank_read, 1)
                dve.wait_ge(s_rank_read, chunk * 2 + 2)
                steps.done(V.tensor_reduce(pos_f[:, :], picked[:, :, :].rearrange("p b t -> p t b"), AX, ALU.add))
                steps.settle()
                steps.done(V.tensor_copy(pos_i[:, 0, :], pos_f[:, :]))
                steps.settle()
                steps.done(V.tensor_single_scalar(pos_i[:, 1, :], pos_i[:, 0, :], 7, ALU.logical_shift_right))
                steps.done(V.tensor_single_scalar(pos_i[:, 2, :], pos_i[:, 0, :], P - 1, ALU.bitwise_and))
                steps.settle()
                V.scalar_tensor_tensor(record[:, ds(chunk * CH, CH), 0], pos_i[:, 2, :], float(TT), pos_i[:, 1, :],
                                       ALU.mult, ALU.add).then_inc(s_pos, 1)
            position(0, 0, first=True)
            position(1, 1, first=True)
            extract(0, 0)
            with dve.Fori(1, CHUNKS // 2) as m:
                steps.enter(m - 1, 8)
                position(m * 2, 0)
                extract(m * 2 - 1, 1)
                position(m * 2 + 1, 1)
                extract(m * 2, 0)
                steps.leave(CHUNKS // 2 - 1)
            extract(CHUNKS - 1, 1)

            def block_stats(first_block, j):
                steps.done(V.bn_stats(stats[:, j, :], acc[:, ds(first_block + j, 1), :].rearrange("p a c -> p (a c)")))

            def gather_stats(first_block):
                steps.settle()
                steps.done(V.memset(turn_mark[:, :], 0.0))
                for j in range(TB):
                    steps.done(V.bn_aggr(turn_stats[:, j, :], stats[:, j, :]))
                steps.settle()
                V.tensor_copy(row_mean[:, ds(first_block, TB), :], turn_stats[:, :, :]).then_inc(s_var, 1)

            def all_row_stats():
                with dve.Fori(0, TURNS) as turn:
                    steps.enter(turn, 2 * TB + 1)
                    first_block = dve.snap(turn * TB)
                    for j in range(TB):
                        block_stats(first_block, j)
                    gather_stats(first_block)
                    dve.wait_ge(s_var, turn + 1)
                    steps.leave(TURNS)

            def invert_std(nth, first_block, count, n):
                dve.wait_ge(s_std, nth)
                r = rstd[:, ds(first_block, count)]
                steps.done(V.reciprocal(r, r))
                steps.settle()
                steps.done(V.tensor_tensor(n, r, r, ALU.mult))
                steps.settle()
                steps.done(V.scalar_tensor_tensor(n, row_mean[:, ds(first_block, count), 1], EPS, n, ALU.add, ALU.mult))
                steps.settle()
                steps.done(V.tensor_scalar(n, n, -0.5, 1.5, ALU.mult, ALU.add))
                steps.settle()
                steps.done(V.tensor_tensor(r, r, n, ALU.mult))
                steps.settle()

            def normalise(g, into, signal):
                for u in range(2):
                    b = g * 2 + u
                    last = V.tensor_scalar(into[:, u, :], acc[:, ds(b, 1), :].rearrange("p a c -> p (a c)"),
                                           row_mean[:, ds(b, 1), 0], rstd[:, ds(b, 1)], ALU.subtract, ALU.mult)
                last.then_inc(signal, 1)
            dve.wait_ge(s_x, 16 * len(XCUT))
            all_row_stats()
            dve.wait_ge(s_wload, 16 * 6)
            steps.done(V.tensor_tensor(bias_row[:, :], bias_in[:, 0, :], bias_in[:, 1, :], ALU.add))
            invert_std(1, 0, NB, newton[:, :])

            def activate(g, slot):
                dve.wait_ge(s_proj_read, g * 2 + 2)
                for i, into in ((0, k_act), (1, q_out)):
                    V.scalar_tensor_tensor(into[:, slot, :, :].rearrange("p u c -> p (u c)"),
                                           exp_kq[:, i, :, :].rearrange("p u c -> p (u c)"), 1.0,
                                           relu_kq[:, i, :, :].rearrange("p u c -> p (u c)"),
                                           ALU.min, ALU.add).then_inc(s_kq, 1)

            def add_bias(g):
                pair = acc[:, ds(g * 2, 2), :]
                steps.done(V.tensor_tensor(pair, pair, bias_row[:, :].unsqueeze(1).to_broadcast([P, 2, C]), ALU.add))
            normalise(0, xn, s_xn)
            dve.wait_ge(s_xt_psum, 1)
            normalise(1, xn, s_xn)
            activate(0, 0)
            add_bias(0)
            dve.wait_ge(s_xt_psum, 2)
            normalise(2, xn, s_xn)
            activate(1, 1)
            add_bias(1)
            with dve.Fori(1, PAIRS // 2) as m:
                steps.enter(m - 1, 2)
                for slot in range(2):
                    g = m * 2 + slot
                    dve.wait_ge(s_xt_psum, g + 1)
                    normalise(g + 1, xn, s_xn)
                    dve.wait_ge(s_ctx, g - 1)
                    dve.wait_ge(s_hq_out[slot], (g - slot) * 16)
                    activate(g, slot)
                    add_bias(g)
                steps.leave(PAIRS // 2 - 1)
            dve.wait_ge(s_ctx, PAIRS - 2)
            dve.wait_ge(s_hq_out[0], (PAIRS - 1) * 16)
            activate(PAIRS - 1, 0)
            add_bias(PAIRS - 1)

            dve.wait_ge(s_ctx, PAIRS)
            for h in range(KC):
                steps.done(V.tensor_tensor(ctx_t[:, h, :], head_mask[:, :], bank[7][:, h * P:(h + 1) * P], ALU.mult))
            steps.done(V.tensor_copy(ksum[:, :], bank[7][:, C:2 * C]))
            steps.settle()
            V.engine_nop().then_inc(s_ctx_sb, 1)
            dve.wait_ge(s_mixw_psum, 1)
            V.tensor_copy(mix_w[:, :, :].rearrange("p k c -> p (k c)"), bank[5][:, :]).then_inc(s_mixw, 1)

            def scale_q(g, slot, first=False):
                if first:
                    dve.wait_ge(s_q_in[slot], 16)
                else:
                    dve.wait_ge(s_q_in[slot], g * 8 + (16 - 8 * slot))
                steps.done(V.tensor_tensor(k_act[:, 0, :, :], q_out[:, slot, :, :],
                                           ksum[:, :].unsqueeze(1).to_broadcast([P, 2, C]), ALU.mult))
                steps.settle()
                steps.done(V.tensor_reduce(den[:, 0, :], k_act[:, 0, :, :].rearrange("p u (h d) -> p (u h) d", d=HD), AX, ALU.add))
                steps.settle()
                steps.done(V.tensor_scalar(den[:, 1, :], den[:, 0, :], 1e-6, None, ALU.max))
                steps.settle()
                steps.done(V.reciprocal(den[:, 2, :], den[:, 1, :]))
                steps.settle()
                if not first or slot:
                    dve.wait_ge(s_qt_psum, g)
                V.tensor_tensor(xn[:, :, :].rearrange("p u (h d) -> p (u h) d", d=HD),
                                q_out[:, slot, :, :].rearrange("p u (h d) -> p (u h) d", d=HD),
                                den[:, 2, :].unsqueeze(2).to_broadcast([P, 2 * HEADS, HD]), ALU.mult).then_inc(s_qn, 1)

            def add_mix(g, slot):
                pair = acc[:, ds(g * 2, 2), :]
                dve.wait_ge(s_mix, g + 1)
                pair = pair.rearrange("p u c -> p (u c)")
                V.tensor_tensor(pair, pair, bank[3 + slot][:, :], ALU.add).then_inc(s_mix_added, 1)
            scale_q(0, 0, first=True)
            scale_q(1, 1, first=True)
            scale_q(2, 0)
            add_mix(0, 0)
            with dve.Fori(1, PAIRS // 2) as m:
                steps.enter(m - 1, 8)
                scale_q(m * 2 + 1, 1)
                add_mix(m * 2 - 1, 1)
                scale_q(m * 2 + 2, 0)
                add_mix(m * 2, 0)
                steps.leave(PAIRS // 2 - 1)
            add_mix(PAIRS - 2, 1)
            add_mix(PAIRS - 1, 0)

            dve.wait_ge(s_tile_row, 16)
            dve.wait_ge(s_mix_added, PAIRS)

            def select_tile(slot, j):
                return V.tensor_scalar(select[:, slot % 2, j, :], iota_n[:, :], gather_stage[:, slot, j, 1:2].bitcast(F32),
                                       gather_stage[:, slot, j, 2:3].bitcast(F32), ALU.is_equal, ALU.mult)

            acc_flat = acc[:, :, :].rearrange("p b c -> p (b c)")

            def add_set(slot, blocks):
                for j in range(SET):
                    to = acc_flat[:, ds(blocks[j], C)]
                    ps = bank[(slot % 2) * 2 + j // 2][:, (j % 2) * C:(j % 2 + 1) * C]
                    added = V.tensor_tensor(to, to, ps, ALU.add)
                    if j < SET - 1:
                        steps.done(added)
                        steps.settle()
                added.then_inc(s_added, 1)

            def set_turn(k, slot, k_list=None, add_slot=None, first=False):
                dve.wait_ge(s_list[slot], k_list)
                for j in range(SET):
                    made = select_tile(slot, j)
                made.then_inc(s_select, 1)
                if not first:
                    blocks = load_offsets(dve, f"block_{slot}_{k if isinstance(k, int) else 'turn'}_", tile_row, k * SET - SET, SET, (NB - 1) * C)
                    if not (isinstance(k, int) and k == 1):
                        dve.wait_ge(s_added, k - 1)
                    dve.wait_ge(s_agg, k)
                    add_set(add_slot, blocks)
            set_turn(0, 0, 16, first=True)
            for slot in range(1, RING):
                set_turn(slot, slot, 16, slot - 1)
            with dve.Fori(1, TURNS_G) as m:
                steps.enter(m - 1, (SET - 1) * RING)
                for slot in range(RING):
                    set_turn(m * RING + slot, slot, m * 16 + 16, (slot - 1) % RING)
                steps.leave(TURNS_G - 1)
            for slot in range(TSETS % RING):
                set_turn(TURNS_G * RING + slot, slot, TURNS_G * 16 + 16, (slot - 1) % RING)
            dve.wait_ge(s_added, TSETS - 1)
            dve.wait_ge(s_agg, TSETS)
            add_set((TSETS - 1) % RING, load_offsets(dve, "block_end_", tile_row, TT - SET, SET, (NB - 1) * C))

            dve.wait_ge(s_added, TSETS)

            def invert_turn(turn):
                invert_std(turn + 2, turn * TB, TB, newton_turn[:, :])
            FINISH = TB + 1 + 5

            def send_row(i, trip, slot):
                if not isinstance(trip, int) or trip:
                    dve.wait_ge(s_sent[0][slot], trip * 64)
                normalise(i, moving[0][:, slot, :, :], s_row)

            def read_logits(turn, half):
                dve.wait_ge(s_gate, turn * TURN + TURN)
                V.tensor_copy(logits[:, ds(turn * TB - 2 * HALF_BEGIN[half], TB), :].rearrange("p b e -> p (b e)"),
                              bank[2][:, 0:TB * EXPERTS]).then_inc(s_gate_read, 1)

            def gate_turn(turn, half, ahead=True, first=False, read=True, rows=None):
                for j in range(TURN):
                    g = turn * TURN + j
                    if not first or j > 1:
                        dve.wait_ge(s_xt_psum, g + (PAIRS if j == 0 else PAIRS - 1))
                    normalise(g, fxn[:, j % 2, :, :], s_fxn)
                    if read and j == 1:
                        read_logits(turn - 1, half)
                    if ahead and j < TURN - 2:
                        for b in range(j * 3, min(j * 3 + 3, TB)):
                            block_stats(turn * TB + TB, b)
                    if ahead and j == TURN - 3:
                        gather_stats(turn * TB + TB)
                    if rows is not None and j % 2 == 0:
                        send_row(rows[0] + j // 2, rows[1] + j // 4, j // 2 % 2)
                if ahead:
                    invert_turn(turn + 1)
            for j in range(TB):
                block_stats(0, j)
            gather_stats(0)
            invert_turn(0)
            gate_turn(0, 0, first=True, read=False)
            with dve.Fori(1, TURNS_1) as m:
                steps.enter(m - 1, TB + FINISH)
                gate_turn(m, 0)
                steps.leave(TURNS_1 - 1)
            read_logits(TURNS_1 - 1, 0)
            dve.wait_ge(s_fin, 48)
            dve.wait_ge(s_const, 4)

            def route_half(half, rows_from=None):
                rows_left = [] if rows_from is None else list(range(rows_from, HALF_PAIRS[0]))

                def next_row():
                    if rows_left:
                        i = rows_left.pop(0)
                        send_row(i, i // 2, i % 2)
                nb = 2 * HALF_PAIRS[half]
                mine = slice(2 * HALF_BEGIN[half], 2 * HALF_BEGIN[half] + nb)
                dve.wait_ge(s_gate_read, [TURNS_1, TURNS][half])
                lg, wk, rk = logits[:, 0:nb, :], work[:, 0:nb, :], rank[:, 0:nb, :]
                for i in range(2):
                    steps.done(V.tensor_tensor(lg, lg, gate_b[:, i, :].unsqueeze(1).to_broadcast([P, nb, EXPERTS]), ALU.add))
                    steps.settle()

                def over_experts(col):
                    return small[:, col, 0:nb].unsqueeze(2).to_broadcast([P, nb, EXPERTS])

                def over_blocks(row):
                    return row.unsqueeze(1).to_broadcast([P, nb, EXPERTS])

                def best(i):
                    steps.done(V.tensor_reduce(small[:, i, 0:nb], lg, AX, ALU.max))
                    steps.settle()
                    steps.done(V.tensor_tensor(wk, lg, over_experts(i), ALU.is_equal))
                    steps.settle()
                    steps.done(V.tensor_tensor(wk, wk, over_blocks(iota_e[:, 1, :]), ALU.mult))
                    steps.settle()
                    steps.done(V.tensor_reduce(small[:, 2 + i, 0:nb], wk, AX, ALU.min))
                    steps.settle()
                    steps.done(V.tensor_tensor(pick[:, i, 0:nb, :], over_blocks(iota_e[:, 1, :]), over_experts(2 + i), ALU.is_equal))
                    steps.settle()
                best(0)
                next_row()
                steps.done(V.tensor_scalar(wk, pick[:, 0, 0:nb, :], 1.0, -1.0, ALU.subtract, ALU.mult))
                steps.settle()
                steps.done(V.tensor_tensor(lg, lg, wk, ALU.mult))
                steps.settle()
                steps.done(V.scalar_tensor_tensor(lg, pick[:, 0, 0:nb, :], -3.0e38, lg, ALU.mult, ALU.add))
                steps.settle()
                best(1)
                next_row()
                steps.done(V.tensor_tensor(small[:, 4, 0:nb], small[:, 1, 0:nb], small[:, 0, 0:nb], ALU.subtract))
                steps.done(V.tensor_tensor(both_bf[:, 0:nb, :], pick[:, 0, 0:nb, :], pick[:, 1, 0:nb, :], ALU.add))
                steps.settle()
                V.engine_nop().then_inc(s_route, 1)
                dve.wait_ge(s_route, half * 2 + 2)
                steps.done(V.tensor_scalar(small[:, 5, 0:nb], top_w[:, 1, mine], 1.0, None, ALU.add))
                steps.settle()
                steps.done(V.reciprocal(top_w[:, 0, mine], small[:, 5, 0:nb]))
                steps.settle()
                steps.done(V.tensor_tensor(top_w[:, 1, mine], top_w[:, 1, mine], top_w[:, 0, mine], ALU.mult))
                dve.wait_ge(s_route_psum, half + 1)
                steps.done(V.tensor_copy(carry_a[:, 0:nb, :].rearrange("p b e -> p (b e)"), bank[5][:, 0:nb * EXPERTS]))
                steps.settle()
                here, there, step = carry_a, carry_b, 1
                while step < nb:
                    steps.done(V.tensor_copy(there[:, 0:step, :], here[:, 0:step, :]))
                    steps.done(V.tensor_tensor(there[:, step:nb, :], here[:, step:nb, :], here[:, 0:nb - step, :], ALU.add))
                    steps.settle()
                    here, there, step = there, here, 2 * step
                next_row()
                steps.done(V.tensor_scalar(ends_i[:, :], here[:, nb - 1, :], float(P - 1), None, ALU.add))
                steps.settle()
                steps.done(V.tensor_single_scalar(ends_i[:, :], ends_i[:, :], 7, ALU.logical_shift_right))
                steps.settle()
                steps.done(V.tensor_copy(ends[:, 0, :], ends_i[:, :]))
                steps.settle()
                for e in range(1, EXPERTS):
                    steps.done(V.tensor_tensor(ends[:, 0, e:e + 1], ends[:, 0, e:e + 1], ends[:, 0, e - 1:e], ALU.add))
                    steps.settle()
                steps.done(V.tensor_tensor(xcmp[:, :, :], iota_x[:, :].unsqueeze(2).to_broadcast([P, XPP, EXPERTS]),
                                           ends[:, 0, :].unsqueeze(1).to_broadcast([P, XPP, EXPERTS]), ALU.is_ge))
                steps.done(V.memset(ends[:, 1, 0:1], 0.0))
                steps.done(V.tensor_scalar(ends[:, 1, 1:EXPERTS], ends[:, 0, 0:EXPERTS - 1], float(P), None, ALU.mult))
                steps.settle()
                steps.done(V.tensor_reduce(xtile_f[:, :], xcmp[:, :, :], AX, ALU.add))
                steps.settle()
                if half:
                    dve.wait_ge(s_xtile_dram, 16)
                for i, stride in ((0, KC * HID), (1, HID + C)):
                    steps.done(V.tensor_scalar(xtile_i[:, i, :], xtile_f[:, :], float(EXPERTS - 1), float(stride), ALU.min, ALU.mult))
                steps.done(V.tensor_copy(rk.rearrange("p b e -> p (b e)"), bank[4][:, 0:nb * EXPERTS]))
                steps.settle()
                steps.done(V.tensor_tensor(rank[:, 1:nb, :], rank[:, 1:nb, :], here[:, 0:nb - 1, :], ALU.add))
                steps.settle()
                steps.done(V.tensor_tensor(rk, rk, over_blocks(ends[:, 1, :]), ALU.add))
                steps.settle()
                for i in range(2):
                    steps.done(V.tensor_tensor(wk, rk, pick[:, i, 0:nb, :], ALU.mult))
                    steps.settle()
                    steps.done(V.tensor_reduce(small[:, i, 0:nb], wk, AX, ALU.add))
                    steps.settle()
                    steps.done(V.tensor_copy(token_pos[:, mine, i], small[:, i, 0:nb]))
                steps.settle()
                if half:
                    steps.done(V.tensor_single_scalar(pos_split[:, 0, :, :], token_pos[:, mine, :], 7, ALU.logical_shift_right))
                    steps.done(V.tensor_single_scalar(pos_split[:, 1, :, :], token_pos[:, mine, :], P - 1, ALU.bitwise_and))
                    steps.settle()
                    steps.done(V.scalar_tensor_tensor(token_pos_2[:, :, :], pos_split[:, 1, :, :], float(TX[1]), pos_split[:, 0, :, :],
                                                      ALU.mult, ALU.add))
                    steps.settle()
                while rows_left:
                    next_row()
                V.engine_nop().then_inc(s_route_done, 1)

            route_half(0)
            send_row(0, 0, 0)
            send_row(1, 0, 1)
            gate_turn(TURNS_1, 1, read=False, rows=(2, 1))
            with dve.Fori(TURNS_1 + 1, TURNS - 1) as m:
                steps.enter(m - (TURNS_1 + 1), TB + FINISH)
                gate_turn(m, 1, rows=(m * 4 + (2 - 4 * TURNS_1), m * 2 + (1 - 2 * TURNS_1)))
                steps.leave(TURNS - 1 - (TURNS_1 + 1))
            rows_sent = 2 + 4 * (TURNS - 1 - TURNS_1)
            gate_turn(TURNS - 1, 1, ahead=False, rows=(rows_sent, rows_sent // 2))
            read_logits(TURNS - 1, 1)
            rows_sent += 4
            route_half(1, rows_sent)

            dve.wait_ge(s_b12, 32)
            dve.wait_ge(s_xtile_row[0], 16)

            b12_flat = b12[:, :, :].rearrange("p e n -> p (e n)")

            def add_b1(t, slot, expert, first=False):
                dve.wait_ge(s_hid_psum, t + 1)
                if not first:
                    dve.wait_ge(s_hidt_psum, t - 1)
                V.tensor_tensor(hid[:, slot, :], bank[2 + slot][:, :],
                                b12_flat[:, ds(expert, HID)], ALU.add).then_inc(s_hid, 1)

            def add_b2(t, slot, expert, first=False, second_half=False):
                dve.wait_ge(s_fy_psum, t + 1)
                if second_half:
                    dve.wait_ge(s_y_out[slot], (t - slot) * 8 - TX[0] * 8)
                elif not first:
                    dve.wait_ge(s_fy_out[slot], (t - slot) * 8)
                V.tensor_tensor(fy[:, slot, :], bank[6 + slot][:, 0:C],
                                b12_flat[:, ds(expert + HID, C)], ALU.add).then_inc(s_fy, 1)

            def expert_pair(t, experts, first=False, second_half=False):
                add_b1(t, 0, experts[0], first)
                add_b1(t + 1, 1, experts[1], first)
                add_b2(t, 0, experts[0], first, second_half)
                add_b2(t + 1, 1, experts[1], first, second_half)

            def experts_of(name, t):
                return load_offsets(dve, name, xtile_row[:, 1, :], t, 4, (EXPERTS - 1) * (HID + C))
            e = experts_of("expert_first_", 0)
            expert_pair(0, e[0:2], first=True)
            expert_pair(2, e[2:4])

            def group(name, m, second_half=False):
                e = experts_of(name, m * 4)
                expert_pair(m * 4, e[0:2], second_half=second_half)
                expert_pair(m * 4 + 2, e[2:4], second_half=second_half)

            def weighted(to, row, b, k, more):
                return V.scalar_tensor_tensor(to, row, top_w[:, k, ds(b, 1)], more, ALU.mult, ALU.add)
            with dve.Fori(1, G1) as m:
                group("expert_1_", m)
            dve.wait_ge(s_xtile_row[1], 16)
            e = experts_of("expert_turn_", TX[0])
            expert_pair(TX[0], e[0:2])
            expert_pair(TX[0] + 2, e[2:4], second_half=True)
            with dve.Fori(G1 + 1, G1 + 1 + BACK) as m:
                steps.enter(m - (G1 + 1), 2)
                e = experts_of("expert_2_", m * 4)
                expert_pair(m * 4, e[0:2], second_half=True)
                add_b1(m * 4 + 2, 0, e[2])
                add_b1(m * 4 + 3, 1, e[3])
                first_block = dve.snap(m * 2 + 2 * (SPARE - G1 - 1))
                dve.wait_ge(s_back_1, m * 64 - 64 * G1)
                for u in range(2):
                    b = first_block + u
                    steps.done(weighted(spare[:, u, :], spare[:, u, :], b, 0, acc[:, ds(b, 1), :].rearrange("p a c -> p (a c)")))
                steps.settle()
                for u in range(2):
                    last = weighted(spare[:, u, :], spare[:, 2 + u, :], first_block + u, 1, spare[:, u, :])
                last.then_inc(s_sum_1, 1)
                add_b2(m * 4 + 2, 0, e[2], second_half=True)
                add_b2(m * 4 + 3, 1, e[3], second_half=True)
                steps.leave(BACK)
            with dve.Fori(G1 + 1 + BACK, GROUPS) as m:
                group("expert_3_", m, second_half=True)

            def combine(pair, rows, slot):
                for u in range(2):
                    b = pair * 2 + u
                    steps.done(weighted(result[:, slot, u, :], rows[:, u, 0, :], b, 0, acc[:, ds(b, 1), :].rearrange("p a c -> p (a c)")))
                steps.settle()
                for u in range(2):
                    last = weighted(result[:, slot, u, :], rows[:, u, 1, :], pair * 2 + u, 1, result[:, slot, u, :])
                last.then_inc(s_sum, 1)
            for slot in range(LAST_SLOTS):
                dve.wait_ge(s_back[slot], 16)
                combine(HALF_BEGIN[1] + slot, back[:, slot, :, :, :], slot)
            n = HALF_PAIRS[1] // LAST_SLOTS
            with dve.Fori(1, n) as m:
                steps.enter(m - 1, 2 * LAST_SLOTS)
                for slot in range(LAST_SLOTS):
                    dve.wait_ge(s_back[slot], m * 16 + 16)
                    dve.wait_ge(s_out[slot], m * 16)
                    combine(m * LAST_SLOTS + (slot + HALF_BEGIN[1]), back[:, slot, :, :, :], slot)
                steps.leave(n - 1)
            dve.wait_ge(s_reload, 16)
            dve.wait_ge(s_spare_back, SPARE * 64)
            for pair in range(SPARE):
                dve.wait_ge(s_out[pair], n * 16)
                combine(pair, spare_back[:, pair, :, :, :], pair)


_INS = ["x", "src", "dst", "edge_weight", "L0_gnn_W", "L0_gnn_b", "L0_mix_Wq", "L0_mix_Wkv", "L0_mix_Wproj",
        "L0_mix_bproj", "L0_ffn_Wg", "L0_ffn_bg", "L0_ffn_bias", "L0_ffn_W1", "L0_ffn_b1", "L0_ffn_W2", "L0_ffn_b2"]


def kernel(**inputs):
    import numpy as np
    import concourse.bacc as bacc
    from concourse import mybir
    from concourse.bass_utils import run_bass_kernel_spmd

    nc = bacc.Bacc("TRN2", target_bir_lowering=False, num_devices=1)
    arrays, args = {}, []
    for name in _INS:
        a = np.ascontiguousarray(inputs[name])
        arrays[f"in_{name}"] = a
        args.append(nc.dram_tensor(f"in_{name}", a.shape, mybir.dt.from_np(a.dtype), kind="ExternalInput").ap())
    out = nc.dram_tensor("out", inputs["x"].shape, mybir.dt.float32, kind="ExternalOutput").ap()
    gps_layer(nc, *args, out)
    return run_bass_kernel_spmd(nc, [arrays], core_ids=[0]).results[0]["out"]
```
